# Optimizing a Trainium2 kernel written in Bass

```python
import numpy as np
import jax
import jax.numpy as jnp

def _softmax(x, axis=-1):
    return jax.nn.softmax(x, axis=axis)

def _gelu(x):
    return jax.nn.gelu(x, approximate=True)

def _silu(x):
    return jax.nn.silu(x)

def _sigmoid(x):
    return jax.nn.sigmoid(x)

def _layernorm(x, axis=-1, eps=1e-05):
    m = jnp.mean(x, axis=axis, keepdims=True)
    v = jnp.var(x, axis=axis, keepdims=True)
    return (x - m) / jnp.sqrt(v + eps)

def _scatter_add(tgt, idx, src, axis=0):
    return tgt.at[idx].add(src)

def _segment_sum(src, seg, n):
    return jax.ops.segment_sum(src, seg, n)
kernel_name = 'mk_xattn_ffn_d2_seqx_r8_c7904e'

def setup_inputs(seed: int=0):
    np.random.seed(seed)
    _w = jnp.asarray

    def _rec_inputs():
        import jax
        import jax.numpy as jnp
        _rk = jax.random.key(seed)
        x = 7.22e-05 + 1 * jax.random.normal(jax.random.fold_in(_rk, 1), (16, 128, 128), jnp.float32)
        _lenS = 128 - jax.random.randint(jax.random.fold_in(_rk, 7), (16,), 0, max(1, 128 // 4) + 1, jnp.int32)
        _lenS2 = 128 - jax.random.randint(jax.random.fold_in(_rk, 8), (16,), 0, max(1, 128 // 4) + 1, jnp.int32)
        _ctx_1024P = jax.random.normal(jax.random.fold_in(_rk, 11), (16, 16, 128), jnp.float32)
        _ctx_1024c = jax.random.dirichlet(jax.random.fold_in(_rk, 511), 0.3 * jnp.ones((16,), jnp.float32), (16, 128))
        _ctx_1024t = jnp.einsum('bsk,bkd->bsd', _ctx_1024c, _ctx_1024P)
        _ctx_1024t = _ctx_1024t * jax.lax.rsqrt(jnp.mean(jnp.square(_ctx_1024t)) + 1e-12) * 0.953939
        ctx_1024 = 4.13588e-05 + 0.999923 * (_ctx_1024t + 0.3 * jax.random.normal(jax.random.fold_in(_rk, 611), (16, 128, 128), jnp.float32))
        return (x, ctx_1024)
    x, ctx_1024 = _rec_inputs()

    def _L0_xattn_setup():
        import jax, jax.numpy as jnp
        import numpy as np
        HIDDEN = 128
        HEADS = 16
        HEAD_DIM = HIDDEN // HEADS
        key = jax.random.key(seed)
        ks = jax.random.split(key, 12)
        B, S, D = (4, 256, HIDDEN)
        scale = 1.0 / np.sqrt(D)
        inp = {'q': jax.random.normal(ks[0], (B, S, D), jnp.float32), 'k': jax.random.normal(ks[1], (B, S, D), jnp.float32), 'v': jax.random.normal(ks[2], (B, S, D), jnp.float32), 'Wq': jax.random.normal(ks[3], (D, D), jnp.float32) * scale, 'bq': jnp.zeros((D,), jnp.float32), 'Wk': jax.random.normal(ks[4], (D, D), jnp.float32) * scale, 'bk': jnp.zeros((D,), jnp.float32), 'Wv': jax.random.normal(ks[5], (D, D), jnp.float32) * scale, 'bv': jnp.zeros((D,), jnp.float32), 'Wo': jax.random.normal(ks[6], (D, D), jnp.float32) * scale, 'bo': jnp.zeros((D,), jnp.float32)}
        return inp
    _L0_xattn_all = _L0_xattn_setup()
    _L0_xattn_in = {k: v for k, v in _L0_xattn_all.items() if k in ('Wq', 'bq', 'Wk', 'bk', 'Wv', 'bv', 'Wo', 'bo')}
    del _L0_xattn_all

    def _L0_ffn_setup():
        import jax, jax.numpy as jnp
        import numpy as np
        DIM = 128
        DEPTH = 6
        HEADS = 16
        DIM_HEAD = 64
        WINDOW = 32
        INNER = HEADS * DIM_HEAD
        DIM_INNER = int(DIM * 4 * 2 / 3)
        QK_SCALE = 8.0

        def shift_tokens(t):
            a, s = jnp.split(t, 2, -1)
            s = jnp.pad(s, ((0, 0), (1, 0), (0, 0)))[:, :-1]
            return jnp.concatenate([a, s], -1)

        def l2norm(t):
            return t / jnp.maximum(jnp.linalg.norm(t, axis=-1, keepdims=True), 1e-12)

        def rotate_half(x):
            x1, x2 = jnp.split(x, 2, -1)
            return jnp.concatenate([-x2, x1], -1)

        def rotary_tables(n):
            half = jnp.arange(0, DIM_HEAD, 2, dtype=jnp.float32)
            inv_freq = 1.0 / 10000.0 ** (half / DIM_HEAD)
            t = jnp.arange(n, dtype=jnp.float32)
            freqs = t[:, None] * inv_freq[None, :]
            freqs = jnp.concatenate([freqs, freqs], -1)
            base_scale = (half + 0.4 * DIM_HEAD) / (1.4 * DIM_HEAD)
            power = (t - n // 2) / (WINDOW // 2)
            scale = base_scale[None, :] ** power[:, None]
            scale = jnp.concatenate([scale, scale], -1)
            return (freqs, scale)

        def local_attention(q, k, v):
            b, h, n, d = q.shape
            w = WINDOW
            nw = n // w
            bq = q.reshape(b, h, nw, w, d)
            bk = k.reshape(b, h, nw, w, d)
            bv = v.reshape(b, h, nw, w, d)

            def look(t):
                p = jnp.pad(t, ((0, 0), (0, 0), (1, 0), (0, 0), (0, 0)))
                return jnp.concatenate([p[:, :, :nw], p[:, :, 1:]], axis=3)
            bk2, bv2 = (look(bk), look(bv))
            seq = jnp.arange(n).reshape(nw, w)
            seq_p = jnp.pad(seq, ((1, 0), (0, 0)), constant_values=-1)
            jt = jnp.concatenate([seq_p[:nw], seq_p[1:]], axis=1)
            it = seq[:, :, None]
            jb = jt[:, None, :]
            mask = (it < jb) | (it > jb + w) | (jb == -1)
            sim = jnp.einsum('bhwie,bhwje->bhwij', bq, bk2) * QK_SCALE
            sim = jnp.where(mask, -jnp.finfo(sim.dtype).max, sim)
            attn = jax.nn.softmax(sim, -1)
            out = jnp.einsum('bhwij,bhwje->bhwie', attn, bv2)
            return out.reshape(b, h, n, d)

        def attn_layer(x, Wqkv, qs, ksc, Wo):
            b, n, _ = x.shape
            qkv = x @ Wqkv
            q, k, v = jnp.split(qkv, 3, -1)
            sh = lambda t: t.reshape(b, n, HEADS, DIM_HEAD).transpose(0, 2, 1, 3)
            q, k, v = (sh(q), sh(k), sh(v))
            q = l2norm(q) * qs
            k = l2norm(k) * ksc
            freqs, scale = rotary_tables(n)
            cos, sin = (jnp.cos(freqs), jnp.sin(freqs))
            q = q * cos * scale + rotate_half(q) * sin * scale
            inv = 1.0 / scale
            k = k * cos * inv + rotate_half(k) * sin * inv
            out = local_attention(q, k, v)
            out = out.transpose(0, 2, 1, 3).reshape(b, n, INNER)
            return out @ Wo

        def ffn_layer(x, g, bln, W1, b1, W2, b2):
            mu = x.mean(-1, keepdims=True)
            var = ((x - mu) ** 2).mean(-1, keepdims=True)
            xn = (x - mu) / jnp.sqrt(var + 1e-05) * g + bln
            hg = xn @ W1 + b1
            a, gate = jnp.split(hg, 2, -1)
            return a * jax.nn.gelu(gate, approximate=False) @ W2 + b2
        key = jax.random.key(seed)
        ks = jax.random.split(key, 8)
        B, N = (2, 256)
        init = lambda k, shape: jax.random.normal(k, shape, jnp.float32) * 0.02
        return {'x': jax.random.normal(ks[0], (B, N, DIM), jnp.float32), 'Wqkv': init(ks[1], (DEPTH, DIM, 3 * INNER)), 'q_scale': jnp.ones((DEPTH, DIM_HEAD), jnp.float32), 'k_scale': jnp.ones((DEPTH, DIM_HEAD), jnp.float32), 'Wo': init(ks[2], (DEPTH, INNER, DIM)), 'ln_g': jnp.ones((DEPTH, DIM), jnp.float32), 'ln_b': jnp.zeros((DEPTH, DIM), jnp.float32), 'W1': init(ks[3], (DEPTH, DIM, 2 * DIM_INNER)), 'b1': jnp.zeros((DEPTH, 2 * DIM_INNER), jnp.float32), 'W2': init(ks[4], (DEPTH, DIM_INNER, DIM)), 'b2': jnp.zeros((DEPTH, DIM), jnp.float32)}
    _L0_ffn_all = _L0_ffn_setup()
    _L0_ffn_in = {k: v for k, v in _L0_ffn_all.items() if k in ('Wqkv', 'q_scale', 'k_scale', 'Wo', 'ln_g', 'ln_b', 'W1', 'b1', 'W2', 'b2')}
    del _L0_ffn_all

    def _L1_xattn_setup():
        import jax, jax.numpy as jnp
        import numpy as np
        H = 128
        B = 8
        L_CHAR = 256
        L_SUB = 128

        def _linear(x, W, b):
            return jnp.einsum('blh,oh->blo', x, W) + b

        def _interp_linear(x, out_len):
            L_in = x.shape[1]
            pos = (jnp.arange(out_len, dtype=x.dtype) + 0.5) * (L_in / out_len) - 0.5
            pos = jnp.clip(pos, 0.0, L_in - 1)
            lo = jnp.floor(pos).astype(jnp.int32)
            hi = jnp.minimum(lo + 1, L_in - 1)
            w = (pos - lo.astype(x.dtype))[None, :, None]
            return x[:, lo] * (1 - w) + x[:, hi] * w
        key = jax.random.key(seed)
        ks = jax.random.split(key, 18)
        s = 0.02
        inp = {'char_emb': jax.random.normal(ks[0], (B, L_CHAR, H), jnp.float32), 'subword_emb': jax.random.normal(ks[1], (B, L_SUB, H), jnp.float32)}
        names = ['Wq_c', 'Wk_s', 'Wv_s', 'Wq_s', 'Wk_c', 'Wv_c']
        for i, n in enumerate(names):
            inp[n] = jax.random.normal(ks[2 + 2 * i], (H, H), jnp.float32) * s
            inp['b' + n[1:]] = jax.random.normal(ks[3 + 2 * i], (H,), jnp.float32) * s
        inp['Wg'] = jax.random.normal(ks[14], (H, 2 * H), jnp.float32) * s
        inp['bg'] = jax.random.normal(ks[15], (H,), jnp.float32) * s
        return inp
    _L1_xattn_all = _L1_xattn_setup()
    _L1_xattn_in = {k: v for k, v in _L1_xattn_all.items() if k in ('Wq_c', 'bq_c', 'Wk_s', 'bk_s', 'Wv_s', 'bv_s', 'Wq_s', 'bq_s', 'Wk_c', 'bk_c', 'Wv_c', 'bv_c', 'Wg', 'bg')}
    del _L1_xattn_all

    def _L1_ffn_setup():
        import jax, jax.numpy as jnp
        import numpy as np
        DIM = 128
        DEPTH = 2
        HEADS = 8
        DIM_HEAD = 64
        WINDOW = 64
        INNER = HEADS * DIM_HEAD
        HID = int(DIM * 4 * 2 / 3)
        B, N = (2, 1024)
        QK_SCALE = 8.0

        def shift_token(t):
            t1, t2 = jnp.split(t, 2, axis=-1)
            t2 = jnp.pad(t2, ((0, 0), (1, 0), (0, 0)))[:, :-1]
            return jnp.concatenate([t1, t2], axis=-1)

        def l2norm(t):
            return t / jnp.clip(jnp.linalg.norm(t, axis=-1, keepdims=True), 1e-12)

        def rotate_half(x):
            x1, x2 = jnp.split(x, 2, axis=-1)
            return jnp.concatenate([-x2, x1], axis=-1)

        def rotary_xpos(q, k):
            n = q.shape[-2]
            half_idx = jnp.arange(0, DIM_HEAD, 2, dtype=jnp.float32)
            inv_freq = 1.0 / 10000.0 ** (half_idx / DIM_HEAD)
            t = jnp.arange(n, dtype=jnp.float32)
            freqs = t[:, None] * inv_freq[None, :]
            freqs = jnp.concatenate([freqs, freqs], axis=-1)
            base = (half_idx + 0.4 * DIM_HEAD) / (1.4 * DIM_HEAD)
            power = (t - n // 2) / float(WINDOW // 2)
            scale = base[None, :] ** power[:, None]
            scale = jnp.concatenate([scale, scale], axis=-1)
            cos, sin = (jnp.cos(freqs), jnp.sin(freqs))
            q = q * cos * scale + rotate_half(q) * sin * scale
            k = k * cos / scale + rotate_half(k) * sin / scale
            return (q, k)

        def local_attention(q, k, v):
            b, h, n, d = q.shape
            w = n // WINDOW
            bq = q.reshape(b, h, w, WINDOW, d) * QK_SCALE
            bk = k.reshape(b, h, w, WINDOW, d)
            bv = v.reshape(b, h, w, WINDOW, d)

            def look_around(t):
                p = jnp.pad(t, ((0, 0), (0, 0), (1, 0), (0, 0), (0, 0)))
                return jnp.concatenate([p[:, :, :w], p[:, :, 1:]], axis=3)
            bk, bv = (look_around(bk), look_around(bv))
            bt = jnp.arange(n).reshape(w, WINDOW)
            btp = jnp.pad(bt, ((1, 0), (0, 0)), constant_values=-1)
            btk = jnp.concatenate([btp[:w], btp[1:]], axis=1)
            sim = jnp.einsum('bhwid,bhwjd->bhwij', bq, bk)
            i = bt[:, :, None]
            j = btk[:, None, :]
            mask = (i < j) | (i > j + WINDOW) | (j == -1)
            sim = jnp.where(mask, -jnp.finfo(sim.dtype).max, sim)
            attn = jax.nn.softmax(sim, axis=-1)
            out = jnp.einsum('bhwij,bhwjd->bhwid', attn, bv)
            return out.reshape(b, h, n, d)

        def _layer(x, wqkv, qs, ksc, wo, lg, lb, w1, b1, w2, b2):
            b, n, _ = x.shape
            h = shift_token(x)
            qkv = h @ wqkv
            q, k, v = jnp.split(qkv, 3, axis=-1)
            to_heads = lambda t: t.reshape(b, n, HEADS, DIM_HEAD).transpose(0, 2, 1, 3)
            q, k, v = (to_heads(q), to_heads(k), to_heads(v))
            q = l2norm(q) * qs
            k = l2norm(k) * ksc
            q, k = rotary_xpos(q, k)
            o = local_attention(q, k, v)
            o = o.transpose(0, 2, 1, 3).reshape(b, n, INNER)
            x = x + o @ wo
            h = shift_token(x)
            mu = h.mean(-1, keepdims=True)
            var = h.var(-1, keepdims=True)
            h = (h - mu) / jnp.sqrt(var + 1e-05) * lg + lb
            h = h @ w1 + b1
            a, g = jnp.split(h, 2, axis=-1)
            h = a * jax.nn.gelu(g, approximate=False)
            x = x + h @ w2 + b2
            return x
        key = jax.random.key(seed)
        ks = jax.random.split(key, 6)
        return {'x': jax.random.normal(ks[0], (B, N, DIM), jnp.float32), 'wqkv': jax.random.normal(ks[1], (DEPTH, DIM, 3 * INNER), jnp.float32) * 0.02, 'q_scale': jnp.ones((DEPTH, DIM_HEAD), jnp.float32), 'k_scale': jnp.ones((DEPTH, DIM_HEAD), jnp.float32), 'wo': jax.random.normal(ks[2], (DEPTH, INNER, DIM), jnp.float32) * 0.02, 'ln_g': jnp.ones((DEPTH, DIM), jnp.float32), 'ln_b': jnp.zeros((DEPTH, DIM), jnp.float32), 'w1': jax.random.normal(ks[3], (DEPTH, DIM, 2 * HID), jnp.float32) * 0.02, 'b1': jnp.zeros((DEPTH, 2 * HID), jnp.float32), 'w2': jax.random.normal(ks[4], (DEPTH, HID, DIM), jnp.float32) * 0.02, 'b2': jnp.zeros((DEPTH, DIM), jnp.float32)}
    _L1_ffn_all = _L1_ffn_setup()
    _L1_ffn_in = {k: v for k, v in _L1_ffn_all.items() if k in ('wqkv', 'q_scale', 'k_scale', 'wo', 'ln_g', 'ln_b', 'w1', 'b1', 'w2', 'b2')}
    del _L1_ffn_all
    return {'x': x, 'ctx_1024': ctx_1024, 'L0_xattn_Wq': _L0_xattn_in['Wq'], 'L0_xattn_bq': _L0_xattn_in['bq'], 'L0_xattn_Wk': _L0_xattn_in['Wk'], 'L0_xattn_bk': _L0_xattn_in['bk'], 'L0_xattn_Wv': _L0_xattn_in['Wv'], 'L0_xattn_bv': _L0_xattn_in['bv'], 'L0_xattn_Wo': _L0_xattn_in['Wo'], 'L0_xattn_bo': _L0_xattn_in['bo'], 'L0_ffn_Wqkv': _L0_ffn_in['Wqkv'], 'L0_ffn_q_scale': _L0_ffn_in['q_scale'], 'L0_ffn_k_scale': _L0_ffn_in['k_scale'], 'L0_ffn_Wo': _L0_ffn_in['Wo'], 'L0_ffn_ln_g': _L0_ffn_in['ln_g'], 'L0_ffn_ln_b': _L0_ffn_in['ln_b'], 'L0_ffn_W1': _L0_ffn_in['W1'], 'L0_ffn_b1': _L0_ffn_in['b1'], 'L0_ffn_W2': _L0_ffn_in['W2'], 'L0_ffn_b2': _L0_ffn_in['b2'], 'L1_xattn_Wq_c': _L1_xattn_in['Wq_c'], 'L1_xattn_bq_c': _L1_xattn_in['bq_c'], 'L1_xattn_Wk_s': _L1_xattn_in['Wk_s'], 'L1_xattn_bk_s': _L1_xattn_in['bk_s'], 'L1_xattn_Wv_s': _L1_xattn_in['Wv_s'], 'L1_xattn_bv_s': _L1_xattn_in['bv_s'], 'L1_xattn_Wq_s': _L1_xattn_in['Wq_s'], 'L1_xattn_bq_s': _L1_xattn_in['bq_s'], 'L1_xattn_Wk_c': _L1_xattn_in['Wk_c'], 'L1_xattn_bk_c': _L1_xattn_in['bk_c'], 'L1_xattn_Wv_c': _L1_xattn_in['Wv_c'], 'L1_xattn_bv_c': _L1_xattn_in['bv_c'], 'L1_xattn_Wg': _L1_xattn_in['Wg'], 'L1_xattn_bg': _L1_xattn_in['bg'], 'L1_ffn_wqkv': _L1_ffn_in['wqkv'], 'L1_ffn_q_scale': _L1_ffn_in['q_scale'], 'L1_ffn_k_scale': _L1_ffn_in['k_scale'], 'L1_ffn_wo': _L1_ffn_in['wo'], 'L1_ffn_ln_g': _L1_ffn_in['ln_g'], 'L1_ffn_ln_b': _L1_ffn_in['ln_b'], 'L1_ffn_w1': _L1_ffn_in['w1'], 'L1_ffn_b1': _L1_ffn_in['b1'], 'L1_ffn_w2': _L1_ffn_in['w2'], 'L1_ffn_b2': _L1_ffn_in['b2']}

def reference(x, ctx_1024, L0_xattn_Wq, L0_xattn_bq, L0_xattn_Wk, L0_xattn_bk, L0_xattn_Wv, L0_xattn_bv, L0_xattn_Wo, L0_xattn_bo, L0_ffn_Wqkv, L0_ffn_q_scale, L0_ffn_k_scale, L0_ffn_Wo, L0_ffn_ln_g, L0_ffn_ln_b, L0_ffn_W1, L0_ffn_b1, L0_ffn_W2, L0_ffn_b2, L1_xattn_Wq_c, L1_xattn_bq_c, L1_xattn_Wk_s, L1_xattn_bk_s, L1_xattn_Wv_s, L1_xattn_bv_s, L1_xattn_Wq_s, L1_xattn_bq_s, L1_xattn_Wk_c, L1_xattn_bk_c, L1_xattn_Wv_c, L1_xattn_bv_c, L1_xattn_Wg, L1_xattn_bg, L1_ffn_wqkv, L1_ffn_q_scale, L1_ffn_k_scale, L1_ffn_wo, L1_ffn_ln_g, L1_ffn_ln_b, L1_ffn_w1, L1_ffn_b1, L1_ffn_w2, L1_ffn_b2):
    import jax
    import jax.numpy as jnp

    def _L0_xattn_ref(q, k, v, Wq, bq, Wk, bk, Wv, bv, Wo, bo):
        import jax, jax.numpy as jnp
        import numpy as np
        HIDDEN = 128
        HEADS = 16
        HEAD_DIM = HIDDEN // HEADS
        B, S, D = q.shape
        H, Dh = (HEADS, HEAD_DIM)
        Q = q @ Wq + bq
        K = k @ Wk + bk
        V = v @ Wv + bv
        Qh = Q.reshape(B, S, H, Dh).transpose(0, 2, 1, 3)
        Kh = K.reshape(B, S, H, Dh).transpose(0, 2, 1, 3)
        Vh = V.reshape(B, S, H, Dh).transpose(0, 2, 1, 3)
        scores = jnp.einsum('bhqd,bhkd->bhqk', Qh, Kh) / jnp.sqrt(jnp.float32(Dh))
        attn = jax.nn.softmax(scores, axis=-1)
        ctx = jnp.einsum('bhqk,bhkd->bhqd', attn, Vh)
        out = ctx.transpose(0, 2, 1, 3).reshape(B, S, D)
        return out @ Wo + bo

    def _L0_ffn_ref(x, Wqkv, q_scale, k_scale, Wo, ln_g, ln_b, W1, b1, W2, b2):
        import jax, jax.numpy as jnp
        import numpy as np
        DIM = 128
        DEPTH = 6
        HEADS = 16
        DIM_HEAD = 64
        WINDOW = 32
        INNER = HEADS * DIM_HEAD
        DIM_INNER = int(DIM * 4 * 2 / 3)
        QK_SCALE = 8.0

        def shift_tokens(t):
            a, s = jnp.split(t, 2, -1)
            s = jnp.pad(s, ((0, 0), (1, 0), (0, 0)))[:, :-1]
            return jnp.concatenate([a, s], -1)

        def l2norm(t):
            return t / jnp.maximum(jnp.linalg.norm(t, axis=-1, keepdims=True), 1e-12)

        def rotate_half(x):
            x1, x2 = jnp.split(x, 2, -1)
            return jnp.concatenate([-x2, x1], -1)

        def rotary_tables(n):
            half = jnp.arange(0, DIM_HEAD, 2, dtype=jnp.float32)
            inv_freq = 1.0 / 10000.0 ** (half / DIM_HEAD)
            t = jnp.arange(n, dtype=jnp.float32)
            freqs = t[:, None] * inv_freq[None, :]
            freqs = jnp.concatenate([freqs, freqs], -1)
            base_scale = (half + 0.4 * DIM_HEAD) / (1.4 * DIM_HEAD)
            power = (t - n // 2) / (WINDOW // 2)
            scale = base_scale[None, :] ** power[:, None]
            scale = jnp.concatenate([scale, scale], -1)
            return (freqs, scale)

        def local_attention(q, k, v):
            b, h, n, d = q.shape
            w = WINDOW
            nw = n // w
            bq = q.reshape(b, h, nw, w, d)
            bk = k.reshape(b, h, nw, w, d)
            bv = v.reshape(b, h, nw, w, d)

            def look(t):
                p = jnp.pad(t, ((0, 0), (0, 0), (1, 0), (0, 0), (0, 0)))
                return jnp.concatenate([p[:, :, :nw], p[:, :, 1:]], axis=3)
            bk2, bv2 = (look(bk), look(bv))
            seq = jnp.arange(n).reshape(nw, w)
            seq_p = jnp.pad(seq, ((1, 0), (0, 0)), constant_values=-1)
            jt = jnp.concatenate([seq_p[:nw], seq_p[1:]], axis=1)
            it = seq[:, :, None]
            jb = jt[:, None, :]
            mask = (it < jb) | (it > jb + w) | (jb == -1)
            sim = jnp.einsum('bhwie,bhwje->bhwij', bq, bk2) * QK_SCALE
            sim = jnp.where(mask, -jnp.finfo(sim.dtype).max, sim)
            attn = jax.nn.softmax(sim, -1)
            out = jnp.einsum('bhwij,bhwje->bhwie', attn, bv2)
            return out.reshape(b, h, n, d)

        def attn_layer(x, Wqkv, qs, ksc, Wo):
            b, n, _ = x.shape
            qkv = x @ Wqkv
            q, k, v = jnp.split(qkv, 3, -1)
            sh = lambda t: t.reshape(b, n, HEADS, DIM_HEAD).transpose(0, 2, 1, 3)
            q, k, v = (sh(q), sh(k), sh(v))
            q = l2norm(q) * qs
            k = l2norm(k) * ksc
            freqs, scale = rotary_tables(n)
            cos, sin = (jnp.cos(freqs), jnp.sin(freqs))
            q = q * cos * scale + rotate_half(q) * sin * scale
            inv = 1.0 / scale
            k = k * cos * inv + rotate_half(k) * sin * inv
            out = local_attention(q, k, v)
            out = out.transpose(0, 2, 1, 3).reshape(b, n, INNER)
            return out @ Wo

        def ffn_layer(x, g, bln, W1, b1, W2, b2):
            mu = x.mean(-1, keepdims=True)
            var = ((x - mu) ** 2).mean(-1, keepdims=True)
            xn = (x - mu) / jnp.sqrt(var + 1e-05) * g + bln
            hg = xn @ W1 + b1
            a, gate = jnp.split(hg, 2, -1)
            return a * jax.nn.gelu(gate, approximate=False) @ W2 + b2
        for i in range(DEPTH):
            x = attn_layer(shift_tokens(x), Wqkv[i], q_scale[i], k_scale[i], Wo[i]) + x
            x = ffn_layer(shift_tokens(x), ln_g[i], ln_b[i], W1[i], b1[i], W2[i], b2[i]) + x
        return x

    def _L1_xattn_ref(char_emb, subword_emb, Wq_c, bq_c, Wk_s, bk_s, Wv_s, bv_s, Wq_s, bq_s, Wk_c, bk_c, Wv_c, bv_c, Wg, bg):
        import jax, jax.numpy as jnp
        import numpy as np
        H = 128
        B = 8
        L_CHAR = 256
        L_SUB = 128

        def _linear(x, W, b):
            return jnp.einsum('blh,oh->blo', x, W) + b

        def _interp_linear(x, out_len):
            L_in = x.shape[1]
            pos = (jnp.arange(out_len, dtype=x.dtype) + 0.5) * (L_in / out_len) - 0.5
            pos = jnp.clip(pos, 0.0, L_in - 1)
            lo = jnp.floor(pos).astype(jnp.int32)
            hi = jnp.minimum(lo + 1, L_in - 1)
            w = (pos - lo.astype(x.dtype))[None, :, None]
            return x[:, lo] * (1 - w) + x[:, hi] * w
        h = char_emb.shape[-1]
        scale = 1.0 / jnp.sqrt(jnp.asarray(h, char_emb.dtype))
        Q_char = _linear(char_emb, Wq_c, bq_c)
        K_sub = _linear(subword_emb, Wk_s, bk_s)
        V_sub = _linear(subword_emb, Wv_s, bv_s)
        scores = jnp.einsum('bqh,bkh->bqk', Q_char, K_sub) * scale
        char2sub = jnp.einsum('bqk,bkh->bqh', jax.nn.softmax(scores, axis=-1), V_sub)
        Q_sub = _linear(subword_emb, Wq_s, bq_s)
        K_char = _linear(char_emb, Wk_c, bk_c)
        V_char = _linear(char_emb, Wv_c, bv_c)
        scores2 = jnp.einsum('bqh,bkh->bqk', Q_sub, K_char) * scale
        sub2char = jnp.einsum('bqk,bkh->bqh', jax.nn.softmax(scores2, axis=-1), V_char)
        L_char = char_emb.shape[1]
        if sub2char.shape[1] != L_char:
            sub2char = _interp_linear(sub2char, L_char)
        gate_in = jnp.concatenate([char2sub, sub2char], axis=-1)
        gate = jax.nn.sigmoid(jnp.einsum('blh,oh->blo', gate_in, Wg) + bg)
        return gate * char2sub + (1 - gate) * sub2char

    def _L1_ffn_ref(x, wqkv, q_scale, k_scale, wo, ln_g, ln_b, w1, b1, w2, b2):
        import jax, jax.numpy as jnp
        import numpy as np
        DIM = 128
        DEPTH = 2
        HEADS = 8
        DIM_HEAD = 64
        WINDOW = 64
        INNER = HEADS * DIM_HEAD
        HID = int(DIM * 4 * 2 / 3)
        B, N = (2, 1024)
        QK_SCALE = 8.0

        def shift_token(t):
            t1, t2 = jnp.split(t, 2, axis=-1)
            t2 = jnp.pad(t2, ((0, 0), (1, 0), (0, 0)))[:, :-1]
            return jnp.concatenate([t1, t2], axis=-1)

        def l2norm(t):
            return t / jnp.clip(jnp.linalg.norm(t, axis=-1, keepdims=True), 1e-12)

        def rotate_half(x):
            x1, x2 = jnp.split(x, 2, axis=-1)
            return jnp.concatenate([-x2, x1], axis=-1)

        def rotary_xpos(q, k):
            n = q.shape[-2]
            half_idx = jnp.arange(0, DIM_HEAD, 2, dtype=jnp.float32)
            inv_freq = 1.0 / 10000.0 ** (half_idx / DIM_HEAD)
            t = jnp.arange(n, dtype=jnp.float32)
            freqs = t[:, None] * inv_freq[None, :]
            freqs = jnp.concatenate([freqs, freqs], axis=-1)
            base = (half_idx + 0.4 * DIM_HEAD) / (1.4 * DIM_HEAD)
            power = (t - n // 2) / float(WINDOW // 2)
            scale = base[None, :] ** power[:, None]
            scale = jnp.concatenate([scale, scale], axis=-1)
            cos, sin = (jnp.cos(freqs), jnp.sin(freqs))
            q = q * cos * scale + rotate_half(q) * sin * scale
            k = k * cos / scale + rotate_half(k) * sin / scale
            return (q, k)

        def local_attention(q, k, v):
            b, h, n, d = q.shape
            w = n // WINDOW
            bq = q.reshape(b, h, w, WINDOW, d) * QK_SCALE
            bk = k.reshape(b, h, w, WINDOW, d)
            bv = v.reshape(b, h, w, WINDOW, d)

            def look_around(t):
                p = jnp.pad(t, ((0, 0), (0, 0), (1, 0), (0, 0), (0, 0)))
                return jnp.concatenate([p[:, :, :w], p[:, :, 1:]], axis=3)
            bk, bv = (look_around(bk), look_around(bv))
            bt = jnp.arange(n).reshape(w, WINDOW)
            btp = jnp.pad(bt, ((1, 0), (0, 0)), constant_values=-1)
            btk = jnp.concatenate([btp[:w], btp[1:]], axis=1)
            sim = jnp.einsum('bhwid,bhwjd->bhwij', bq, bk)
            i = bt[:, :, None]
            j = btk[:, None, :]
            mask = (i < j) | (i > j + WINDOW) | (j == -1)
            sim = jnp.where(mask, -jnp.finfo(sim.dtype).max, sim)
            attn = jax.nn.softmax(sim, axis=-1)
            out = jnp.einsum('bhwij,bhwjd->bhwid', attn, bv)
            return out.reshape(b, h, n, d)

        def _layer(x, wqkv, qs, ksc, wo, lg, lb, w1, b1, w2, b2):
            b, n, _ = x.shape
            h = shift_token(x)
            qkv = h @ wqkv
            q, k, v = jnp.split(qkv, 3, axis=-1)
            to_heads = lambda t: t.reshape(b, n, HEADS, DIM_HEAD).transpose(0, 2, 1, 3)
            q, k, v = (to_heads(q), to_heads(k), to_heads(v))
            q = l2norm(q) * qs
            k = l2norm(k) * ksc
            q, k = rotary_xpos(q, k)
            o = local_attention(q, k, v)
            o = o.transpose(0, 2, 1, 3).reshape(b, n, INNER)
            x = x + o @ wo
            h = shift_token(x)
            mu = h.mean(-1, keepdims=True)
            var = h.var(-1, keepdims=True)
            h = (h - mu) / jnp.sqrt(var + 1e-05) * lg + lb
            h = h @ w1 + b1
            a, g = jnp.split(h, 2, axis=-1)
            h = a * jax.nn.gelu(g, approximate=False)
            x = x + h @ w2 + b2
            return x
        for l in range(DEPTH):
            x = _layer(x, wqkv[l], q_scale[l], k_scale[l], wo[l], ln_g[l], ln_b[l], w1[l], b1[l], w2[l], b2[l])
        return x
    x = x + _L0_xattn_ref(_layernorm(x, axis=-1), ctx_1024, ctx_1024, L0_xattn_Wq, L0_xattn_bq, L0_xattn_Wk, L0_xattn_bk, L0_xattn_Wv, L0_xattn_bv, L0_xattn_Wo, L0_xattn_bo)
    x = x + _L0_ffn_ref(_layernorm(x, axis=-1), L0_ffn_Wqkv, L0_ffn_q_scale, L0_ffn_k_scale, L0_ffn_Wo, L0_ffn_ln_g, L0_ffn_ln_b, L0_ffn_W1, L0_ffn_b1, L0_ffn_W2, L0_ffn_b2)
    x = x + _L1_xattn_ref(_layernorm(x, axis=-1), ctx_1024, L1_xattn_Wq_c, L1_xattn_bq_c, L1_xattn_Wk_s, L1_xattn_bk_s, L1_xattn_Wv_s, L1_xattn_bv_s, L1_xattn_Wq_s, L1_xattn_bq_s, L1_xattn_Wk_c, L1_xattn_bk_c, L1_xattn_Wv_c, L1_xattn_bv_c, L1_xattn_Wg, L1_xattn_bg)
    x = x + _L1_ffn_ref(_layernorm(x, axis=-1), L1_ffn_wqkv, L1_ffn_q_scale, L1_ffn_k_scale, L1_ffn_wo, L1_ffn_ln_g, L1_ffn_ln_b, L1_ffn_w1, L1_ffn_b1, L1_ffn_w2, L1_ffn_b2)
    return x

_drawn_inputs = setup_inputs


def setup_inputs(seed=0):
    import zlib

    import numpy as np

    out = dict(_drawn_inputs(seed))
    spreads = {'L0_xattn_bq': (0.0, 0.35),
     'L0_xattn_bk': (0.0, 2.0),
     'L0_xattn_bv': (0.0, 0.1),
     'L0_xattn_bo': (0.0, 0.1),
     'L0_ffn_q_scale': (1.0, 0.6),
     'L0_ffn_k_scale': (1.0, 0.6),
     'L0_ffn_ln_g': (1.0, 0.6),
     'L0_ffn_ln_b': (0.0, 0.8),
     'L0_ffn_b1': (0.0, 0.8),
     'L0_ffn_b2': (0.0, 0.1),
     'L1_ffn_q_scale': (1.0, 0.6),
     'L1_ffn_k_scale': (1.0, 0.6),
     'L1_ffn_ln_g': (1.0, 0.6),
     'L1_ffn_ln_b': (0.0, 0.8),
     'L1_ffn_b1': (0.0, 0.8),
     'L1_ffn_b2': (0.0, 0.8)}
    factors = {'L0_ffn_W1': 3.919,
     'L0_ffn_W2': 3.842,
     'L1_xattn_Wq_c': 30.724,
     'L1_xattn_bq_c': 64.0,
     'L1_xattn_Wk_s': 34.485,
     'L1_xattn_bk_s': 200.0,
     'L1_xattn_bv_s': 28.135,
     'L1_xattn_Wq_s': 50.251,
     'L1_xattn_bq_s': 64.0,
     'L1_xattn_Wk_c': 48.854,
     'L1_xattn_bk_c': 200.0,
     'L1_xattn_bv_c': 34.419,
     'L1_xattn_Wg': 44.688,
     'L1_xattn_bg': 192.726,
     'L1_ffn_w1': 8.0,
     'L1_ffn_w2': 8.0,
     'L1_xattn_Wv_s': 3.389,
     'L1_xattn_Wv_c': 3.736}
    for name, (base, spread) in spreads.items():
        noise = np.random.default_rng([zlib.crc32(name.encode()), seed]).standard_normal(out[name].shape)
        drawn = base * np.exp(spread * noise) if base else spread * noise
        out[name] = jnp.asarray(drawn.astype(out[name].dtype))
    for name, factor in factors.items():
        out[name] = (out[name] * factor).astype(out[name].dtype)
    return out
```

```python
from contextlib import ExitStack

import numpy as np

import concourse.bass as bass
from concourse import mybir

ALU = mybir.AluOpType
ACT = mybir.ActivationFunctionType
F32 = mybir.dt.float32
I32 = mybir.dt.int32
BF16 = mybir.dt.bfloat16
AX = mybir.AxisListType

P = 128
NB = 16
TOK = NB * P
BLK = 512
NBLK = TOK // BLK
HU = 8
DH = 64
VW = DH + 2
XH, XD = 16, 8
XVW = XD + 2
HID = int(P * 4 * 2 / 3)
CH = [(0, 128), (128, 128), (256, HID - 256)]
EPS = 1e-5
QK_SCALE = 8.0
MAGIC = float(0x5F3759DF)
MASKED = -1e30
PEEL = 6


def rotary_constants(window):
    half = np.arange(0, DH, 2, dtype=np.float32)
    inv_freq = (1.0 / 10000.0 ** (half / DH)).astype(np.float32)
    t = np.arange(P, dtype=np.float32)
    freqs = t[:, None] * inv_freq[None, :]
    base = (half + np.float32(0.4 * DH)) / np.float32(1.4 * DH)
    power = (t - P // 2) / np.float32(window // 2)
    scale = base[None, :] ** power[:, None]
    two = lambda a: np.concatenate([a, a], -1)
    cos, sin, scale = two(np.cos(freqs)), np.sin(freqs), two(scale)
    sin = np.concatenate([-sin, sin], -1)
    return [a.astype(np.float32) for a in (cos * scale, sin * scale, cos / scale, sin / scale)]


def mask_constant(window):
    i, j = np.arange(P)[:, None], np.arange(P)[None, :]
    return np.where((i < j) | (i > j + window) | (j < (i // window - 1) * window), np.float32(MASKED), np.float32(0))


class Step:

    def __init__(self, units, base, c, r=None):
        self.units, self.base, self.c, self.r = units, base, c, r

    @property
    def parity(self):
        return self.c % 2

    def has(self, lag):
        return self.r is not None or 0 <= self.c - lag < self.units

    def count(self, lag):
        n = self.c + 1 - lag
        if self.r is not None:
            n = self.r * 2 + n
        return self.base + n

    def unit(self, lag):
        return self.c - lag if self.r is None else self.r * 2 + (self.c - lag)

    def half(self, lag):
        n = self.c - lag
        return (n // 2 if self.r is None else self.r + n // 2), n % 2

    def wait(self, eng, sem, lag):
        if self.has(lag):
            eng.wait_ge(sem, self.count(lag))


def run_steps(eng, units, base, last_lag, step):
    for c in range(PEEL):
        step(Step(units, base, c))
    with eng.Fori(0, (units - PEEL) // 2 - 1) as r:
        for c in (PEEL, PEEL + 1):
            step(Step(units, base, c, r))
    for c in range(units - 2, units + last_lag):
        step(Step(units, base, c))


def build(nc, A, out):
    const = lambda name, a: nc.inline_tensor(np.ascontiguousarray(a), name=name).ap()
    c_ident = const("c_ident", np.eye(P, dtype=np.float32))
    c_rot = [const(f"c_rot{n}", np.concatenate(rotary_constants(w), 1)) for n, w in enumerate((32, 64))]
    c_mask = const("c_mask", np.concatenate([mask_constant(32), mask_constant(64)], 1))
    c_head = const("c_head", (np.arange(P)[:, None] // XD == np.arange(XH)[None, :]).astype(np.float32))

    with ExitStack() as ctx:
        sb = lambda name, shape, dt=F32: ctx.enter_context(nc.sbuf_tensor(name, shape, dt))
        sem = lambda name: ctx.enter_context(nc.semaphore(name))
        bank = [ctx.enter_context(nc.psum_tensor(f"bank{i}", [P, BLK], F32)) for i in range(8)]
        bank4 = [b[:].rearrange("p (a n) -> p a n", a=4) for b in bank]

        ident = sb("ident", [P, P])
        ident_b = sb("ident_b", [P, P], BF16)
        mean_w = sb("mean_w", [P, P])
        eps_t = sb("eps_t", [P, 1])
        tick = sb("tick", [P, 1])
        rot_c = [sb(f"rot_c{n}", [P, 4, DH]) for n in range(2)]
        mask_f = sb("mask_f", [P, 2, P])
        mask_b = sb("mask_b", [P, 2, 4, P], BF16)
        head_m = sb("head_m", [P, XH])
        wqkv = sb("wqkv", [P, 3 * 1024])
        wo = sb("wo", [P, 8, P])
        w1 = sb("w1", [P, 2 * HID])
        w2 = sb("w2", [P, 3, P])
        b1 = sb("b1", [P, 6])
        lnp = sb("lnp", [P, 3])
        qks = sb("qks", [P, 2, DH])
        rot = sb("rot", [P, 4, DH])
        xw = sb("xw", [P, 3, P])
        xwo = sb("xwo", [DH, 2, P])
        xb = sb("xb", [P, 3])
        xbv = sb("xbv", [DH, 2])
        yw_in = sb("yw_in", [P, 8, P])
        yw = sb("yw", [P, 8, P])
        yb = sb("yb", [P, 7])

        base_x = sb("base_x", [P, TOK])
        z = sb("z", [P, TOK])
        ctx_t = sb("ctx_t", [P, TOK])
        shifted = sb("shifted", [P, NB, P])
        cen = sb("cen", [P, TOK])
        dev = sb("dev", [P, TOK])
        big = sb("big", [P, 32 * HU * VW])
        v_all = big[:].rearrange("p (u h d) -> p u h d", u=32, h=HU)
        xv = big[:, 0:NB * XH * XVW].rearrange("p (b h d) -> p b h d", b=NB, h=XH)
        o_ = NB * XH * XVW
        x_q = big[:, o_:o_ + TOK]
        x_k = big[:, o_ + TOK:o_ + 2 * TOK]
        y_qk = big[:, 0:4 * TOK].rearrange("p (a n) -> p a n", a=4)
        y_v = big[:, 4 * TOK:6 * TOK].rearrange("p (b a n) -> p b a n", b=NB, a=2)

        y_ctx = big[:, 6 * TOK:8 * TOK].rearrange("p (a n) -> p a n", a=2)

        hs = [sb(f"hs{i}", [P, P]) for i in range(2)]
        sq = [sb(f"sq{i}", [P, HU, DH]) for i in range(2)]
        rc = [[sb(f"rc{i}{j}", [P, HU, DH]) for j in range(2)] for i in range(2)]
        rs = [[sb(f"rs{i}{j}", [P, HU, DH]) for j in range(2)] for i in range(2)]
        ss = sb("ss", [P, 2 * HU])
        ssc = sb("ssc", [P, 2 * HU])
        nt_y = [sb(f"nt_y{i}", [P, 2 * HU]) for i in range(3)]
        nt_a = sb("nt_a", [P, 2 * HU])
        nt_b = sb("nt_b", [P, 2 * HU])
        rnorm = [sb(f"rnorm{i}", [P, 2 * HU]) for i in range(2)]
        q_t = sb("q_t", [P, 4, P])
        k_blk = sb("k_blk", [P, 4, 2, P])
        xq_s = [sb(f"xq_s{i}", [P, P]) for i in range(2)]
        o_ += 2 * TOK
        xk_s = [big[:, o_ + i * HU * P:o_ + (i + 1) * HU * P].rearrange("p (h t) -> p h t", h=HU) for i in range(2)]
        mx = sb("mx", [P, HU])
        prob = [sb(f"prob{g}", [P, 4, P]) for g in range(2)]
        prob_t = [sb(f"prob_t{g}", [P, 4, P]) for g in range(2)]
        rsum = sb("rsum", [P, 2, 4])
        o_tok = sb("o_tok", [P, HU * DH])
        o_t = sb("o_t", [P, 4, P])
        gl = [sb(f"gl{i}", [P, BLK]) for i in range(2)]
        hid = [sb(f"hid{i}", [P, BLK]) for i in range(3)]
        yq_s = sb("yq_s", [P, 2, 2, P])

        ld_c, ld_x, ld_xw, ld_yw = sem("ld_c"), sem("ld_x"), sem("ld_xw"), sem("ld_yw")
        ld_qkv, ld_rot, ld_wo, ld_ff = sem("ld_qkv"), sem("ld_rot"), sem("ld_wo"), sem("ld_ff")
        c_dve, c_act, c_pool = sem("c_dve"), sem("c_act"), sem("c_pool")
        in_ps, in_dve, in_act = sem("in_ps"), sem("in_dve"), sem("in_act")
        out_ps, out_dve, out_st = sem("out_ps"), sem("out_dve"), sem("out_st")
        LN = {n: sem("ln_" + n) for n in "mean cen sq var dev rec xn aff".split()}
        FF = {n: sem("ff_" + n) for n in "lo hi ag gelu hid y z outer".split()}
        XP = {n: sem("xp_" + n) for n in "q k v qe ke ve".split()}
        YP = {n: sem("yp_" + n) for n in "w we qk qke v ve g gd gm sg s mx sh ex rs pt pte o rr on ot ote qs".split()}
        COMMON = "s0 s1 mx0 mx1 sh0 sh1 ex0 ex1 pt0 pt1 pe0 pe1 o0 o1 rr0 rr1 on0 on1 ot ote y res prep".split()
        X0 = {n: sem("x0_" + n) for n in COMMON}
        AT = {n: sem("at_" + n) for n in COMMON + "hs q k v sqq sqk ve rq rk ssq ssk aq ak mq mk qt kt qte kte rot".split()}
        NT = [sem(f"nt{i}") for i in range(11)]

        NETS = [dict(idx=0, H=16, depth=6, units=32, base0=0, ff0=0, ln0=2, pre="L0_ffn_",
                     Wqkv="Wqkv", Wo="Wo", W1="W1", W2="W2"),
                dict(idx=1, H=8, depth=2, units=16, base0=192, ff0=6, ln0=10, pre="L1_ffn_",
                     Wqkv="wqkv", Wo="wo", W1="w1", W2="w2")]

        def batch_of(net_idx, st, lag):
            return st.half(lag)[0] if net_idx == 0 else st.unit(lag)

        def ln_pe(pe, m, src, ready):
            for k in range(NBLK):
                ready(pe, k)
                nc.tensor.matmul(bank[k][:], mean_w[:], src[:, k * BLK:(k + 1) * BLK],
                                 start=True, stop=True).then_inc(LN["mean"], 1)
            for k in range(NBLK):
                pe.wait_ge(LN["sq"], m * 4 + (k + 1))
                nc.tensor.matmul(bank[4 + k][:], mean_w[:], dev[:, k * BLK:(k + 1) * BLK],
                                 start=True, stop=True).then_inc(LN["var"], 1)

        def ln_act(act, m):
            for k in range(NBLK):
                b = slice(k * BLK, (k + 1) * BLK)
                act.wait_ge(LN["cen"], m * 4 + (k + 1))
                nc.scalar.activation(dev[:, b], cen[:, b], ACT.Square).then_inc(LN["sq"], 1)
            for k in range(NBLK):
                b = slice(k * BLK, (k + 1) * BLK)
                act.wait_ge(LN["var"], m * 4 + (k + 1))
                nc.scalar.activation(dev[:, b], bank[4 + k][:], ACT.Sqrt, bias=eps_t[:, 0:1]).then_inc(LN["dev"], 1)

        def ln_dve(dve, m, src, dst, affine):
            for k in range(NBLK):
                b = slice(k * BLK, (k + 1) * BLK)
                dve.wait_ge(LN["mean"], m * 4 + (k + 1))
                nc.vector.tensor_tensor(cen[:, b], src[:, b], bank[k][:], ALU.subtract).then_inc(LN["cen"], 1)
            for k in range(NBLK):
                b = slice(k * BLK, (k + 1) * BLK)
                dve.wait_ge(LN["dev"], m * 4 + (k + 1))
                nc.vector.reciprocal(dev[:, b], dev[:, b]).then_inc(LN["rec"], 1)
            for k in range(NBLK):
                b = slice(k * BLK, (k + 1) * BLK)
                dve.wait_ge(LN["rec"], m * 4 + (k + 1))
                nc.vector.tensor_tensor(dst[:, b], cen[:, b], dev[:, b], ALU.mult).then_inc(LN["xn"], 1)
            if affine:
                for k in range(NBLK):
                    b = slice(k * BLK, (k + 1) * BLK)
                    dve.wait_ge(LN["xn"], m * 4 + (k + 1))
                    nc.vector.tensor_scalar(dst[:, b], dst[:, b], lnp[:, 0:1], lnp[:, 1:2],
                                            ALU.mult, ALU.add).then_inc(LN["aff"], 1)

        def pe_probs_t(pe, st, S, lc):
            if st.has(lc + 1):
                st.wait(pe, S["ex0"], lc + 1)
                st.wait(pe, S["res"], lc + 3)
                for h in range(4):
                    mm = nc.tensor.transpose(bank4[7][:, h, :], prob[0][:, h, :], ident[:])
                mm.then_inc(S["pt0"], 1)
                st.wait(pe, S["ex1"], lc + 1)
                if S is AT and st.has(lc):
                    st.wait(pe, S["qte"], lc)
                else:
                    st.wait(pe, S["on0"], lc + 2)
                for h in range(4):
                    mm = nc.tensor.transpose(bank4[5][:, h, :], prob[1][:, h, :], ident[:])
                mm.then_inc(S["pt1"], 1)
            if st.has(lc + 2):
                st.wait(pe, S["on1"], lc + 2)
                if S is AT:
                    st.wait(pe, S["kte"], lc)
                    for j in range(4):
                        mm = nc.tensor.transpose(bank4[6][:, j, :], o_tok[:, j * P:(j + 1) * P], ident[:])
                else:
                    mm = nc.tensor.transpose(bank4[6][:, 0, :], o_tok[:, 0:P], ident[:])
                mm.then_inc(S["ot"], 1)

        def pe_values(pe, st, S, lc):
            if st.has(lc + 1):
                width = VW if S is AT else XVW
                half = st.half(lc + 1)
                for g in range(2):
                    st.wait(pe, S["pe%d" % g], lc + 1)
                    if g == 0:
                        st.wait(pe, S["pe1"], lc + 1)
                        if S is AT:
                            st.wait(pe, S["ve"], lc + 1)
                    else:
                        st.wait(pe, S["ote"], lc + 2)
                    dst = bank[5 + g][:, 0:4 * width].rearrange("p (h d) -> p h d", h=4)
                    for h in range(4):
                        if S is AT:
                            v = v_all[:, st.unit(lc + 1), 4 * g + h, :]
                        else:
                            v = xv[:, half[0], HU * half[1] + 4 * g + h, :]
                        mm = nc.tensor.matmul(dst[:, h, :], prob_t[g][:, h, :], v, start=True, stop=True)
                    mm.then_inc(S["o%d" % g], 1)

        def pe_project(pe, st, S, lc, net=0):
            if st.has(lc + 2):
                st.wait(pe, S["ote"], lc + 2)
                if st.has(lc + 1):
                    st.wait(pe, S["pe0"], lc + 1)
                else:
                    st.wait(pe, S["res"], lc + 3)
                p = st.half(lc + 2)[1]
                if S is AT:
                    for j in range(4):
                        mm = nc.tensor.matmul(bank4[7][:, 0, :], wo[:, (4 * p if net == 0 else 0) + j, :],
                                              o_t[:, j, :], start=(j == 0), stop=(j == 3))
                else:
                    mm = nc.tensor.matmul(bank4[7][:, 0, :], xwo[:, p, :], o_t[0:DH, 0, :], start=True, stop=True)
                mm.then_inc(S["y"], 1)

        def act_probs_t(act, st, S, lc):
            if st.has(lc + 1):
                for g in range(2):
                    st.wait(act, S["pt%d" % g], lc + 1)
                    st.wait(act, S["o%d" % g], lc + 2)
                    nc.scalar.activation(prob_t[g][:], bank4[7 if g == 0 else 5], ACT.Copy).then_inc(S["pe%d" % g], 1)
            if st.has(lc + 2):
                st.wait(act, S["ot"], lc + 2)
                st.wait(act, S["y"], lc + 3)
                if S is AT:
                    nc.scalar.activation(o_t[:], bank4[6], ACT.Copy).then_inc(S["ote"], 1)
                else:
                    p = st.half(lc + 2)[1]
                    nc.scalar.activation(o_t[0:DH, 0, :], bank4[6][0:DH, 0, :], ACT.Identity,
                                         bias=xbv[:, p:p + 1]).then_inc(S["ote"], 1)

        def act_exp(act, st, S, lc, scale):
            if st.has(lc):
                for g in range(2):
                    st.wait(act, S["sh%d" % g], lc)
                    nc.scalar.activation(prob[g][:], prob[g][:], ACT.Exp, scale=scale).then_inc(S["ex%d" % g], 1)

        def dve_max(dve, st, S, lc, g):
            if st.has(lc):
                st.wait(dve, S["s%d" % g], lc)
                nc.vector.tensor_reduce(mx[:, 4 * g:4 * g + 4], bank4[3 + g], AX.X, ALU.max).then_inc(S["mx%d" % g], 1)

        def dve_shift(dve, st, S, lc, g):
            if st.has(lc):
                st.wait(dve, S["mx%d" % g], lc)
                st.wait(dve, S["pt%d" % g], lc + 1)
                nc.vector.tensor_tensor(prob[g][:], bank4[3 + g],
                                        mx[:, 4 * g:4 * g + 4].unsqueeze(2).to_broadcast([P, 4, P]),
                                        ALU.subtract).then_inc(S["sh%d" % g], 1)

        def dve_rsum(dve, st, S, lc, g):
            if st.has(lc + 1):
                w, d = (VW, DH) if S is AT else (XVW, XD)
                o = bank[5 + g][:, 0:4 * w].rearrange("p (h d) -> p h d", h=4)
                st.wait(dve, S["o%d" % g], lc + 1)
                st.wait(dve, S["on%d" % g], lc + 2)
                nc.vector.reciprocal(rsum[:, g, :], o[:, :, d]).then_inc(S["rr%d" % g], 1)

        def dve_divide(dve, st, S, lc, g):
            if st.has(lc + 1):
                w, d = (VW, DH) if S is AT else (XVW, XD)
                o = bank[5 + g][:, 0:4 * w].rearrange("p (h d) -> p h d", h=4)
                st.wait(dve, S["rr%d" % g], lc + 1)
                st.wait(dve, S["ot"], lc + 2)
                nc.vector.tensor_tensor(
                    o_tok[:, 4 * g * d:4 * (g + 1) * d].rearrange("p (h d) -> p h d", h=4), o[:, :, 0:d],
                    rsum[:, g, :].unsqueeze(2).to_broadcast([P, 4, d]), ALU.mult).then_inc(S["on%d" % g], 1)

        def dve_residual(dve, st, S, lc, net=0):
            if st.has(lc + 2):
                st.wait(dve, S["y"], lc + 2)
                st.wait(dve, S["res"], lc + 3)
                half = st.half(lc + 2)
                b = batch_of(net, st, lc + 2)
                if S is AT:
                    x = z[:].rearrange("p (b t) -> p b t", b=NB)[:, b, :]
                    nc.vector.tensor_tensor(x, bank4[7][:, 0, :], x, ALU.add).then_inc(S["res"], 1)
                else:
                    x = base_x[:].rearrange("p (b t) -> p b t", b=NB)[:, half[0], :]
                    if half[1] == 0:
                        nc.vector.scalar_tensor_tensor(out=x, in0=bank4[7][:, 0, :], scalar=xb[:, 2:3], in1=x,
                                                       op0=ALU.add, op1=ALU.add).then_inc(S["res"], 1)
                    else:
                        nc.vector.tensor_tensor(x, bank4[7][:, 0, :], x, ALU.add).then_inc(S["res"], 1)

        block = ctx.enter_context(nc.Block())

        @block.sync
        def _(sp):
            sp.dma_start(cen[:].rearrange("p (b d) -> p b d", b=NB), A["x"].rearrange("b t d -> t b d")).then_inc(ld_x, 16)
            sp.dma_start(dev[:].rearrange("p (b d) -> p b d", b=NB), A["ctx_1024"].rearrange("b t d -> t b d")).then_inc(ld_x, 16)
            sp.dma_start(ident[:], c_ident).then_inc(ld_c, 16)
            for n in range(2):
                sp.dma_start(rot_c[n][:], c_rot[n].rearrange("p (a d) -> p a d", a=4)).then_inc(ld_c, 16)
            sp.dma_start(mask_f[:], c_mask.rearrange("p (a d) -> p a d", a=2)).then_inc(ld_c, 16)
            sp.dma_start(head_m[:], c_head).then_inc(ld_c, 16)
            col = lambda a: a.rearrange("(p o) -> p o", o=1)
            for i, n in enumerate(("Wq", "Wk", "Wv")):
                sp.dma_start(xw[:, i, :], A["L0_xattn_" + n]).then_inc(ld_xw, 16)
            sp.dma_start(xwo[:], A["L0_xattn_Wo"].rearrange("(a p) n -> p a n", a=2)).then_inc(ld_xw, 16)
            for i, n in enumerate(("bq", "bk", "bo")):
                sp.dma_start(xb[:, i:i + 1], col(A["L0_xattn_" + n])).then_inc(ld_xw, 16)
            for i in range(2):
                sp.dma_start(xbv[:, i:i + 1], col(A["L0_xattn_bv"][i * DH:(i + 1) * DH])).then_inc(ld_xw, 16)

            def load_layer(net, layer, first):
                pre, units = net["pre"], net["units"]
                inner = net["H"] * DH
                done = lambda per: None if first and net["idx"] == 0 else (
                    net[per[0]] + (0 if first else layer) * per[1]) * per[2]
                n_units = None if first and net["idx"] == 0 else net["base0"] + (0 if first else layer * units)
                n_ff = None if n_units is None else (net["ff0"] + (0 if first else layer)) * 4
                n_rot = None if n_units is None else net["ff0"] + (0 if first else layer)
                if n_units is not None:
                    sp.wait_ge(AT["v"], n_units)
                sp.dma_start(wqkv[:, 0:3 * inner], A[pre + net["Wqkv"]][layer]).then_inc(ld_qkv, 16)
                if n_rot is not None:
                    sp.wait_ge(AT["rot"], n_rot)
                for i, n in enumerate(("q_scale", "k_scale")):
                    sp.dma_start(qks[:, i, :], A[pre + n][layer].rearrange("(o d) -> o d", o=1).to_broadcast([P, DH])
                                 ).then_inc(ld_rot, 16)
                if n_units is not None:
                    sp.wait_ge(AT["y"], n_units)
                sp.dma_start(wo[:, 0:inner // P, :], A[pre + net["Wo"]][layer].rearrange("(j p) n -> p j n", p=P)
                             ).then_inc(ld_wo, 16)
                if n_ff is not None:
                    sp.wait_ge(FF["z"], n_ff)
                ff = [(w1[:], A[pre + net["W1"]][layer])]
                w2_, b1_ = A[pre + net["W2"]][layer], A[pre + "b1"][layer]
                ff.append((w2[:, 0:2, :], w2_[0:256, :].rearrange("(j p) n -> p j n", p=P)))
                ff.append((w2[0:CH[2][1], 2, :], w2_[256:HID, :]))
                for part in range(2):
                    for c, (o, w) in enumerate(CH):
                        ff.append((b1[0:w, 3 * part + c:3 * part + c + 1], col(b1_[part * HID + o:part * HID + o + w])))
                for i, n in enumerate(("ln_g", "ln_b", "b2")):
                    ff.append((lnp[:, i:i + 1], col(A[pre + n][layer])))
                assert len(ff) == 12
                for dst, src in ff:
                    sp.dma_start(dst, src).then_inc(ld_ff, 16)

            net = NETS[0]
            load_layer(net, 0, True)
            names = ["Wq_c", "Wk_s", "Wq_s", "Wk_c", "Wv_s", "Wv_c"]
            for i, n in enumerate(names):
                sp.dma_start(yw_in[:, i, :], A["L1_xattn_" + n]).then_inc(ld_yw, 16)
                sp.dma_start(yb[:, i:i + 1], col(A["L1_xattn_b" + n[1:]])).then_inc(ld_yw, 16)
            sp.dma_start(yw_in[:, 6:8, :], A["L1_xattn_Wg"].rearrange("o (a i) -> o a i", a=2)).then_inc(ld_yw, 16)
            sp.dma_start(yb[:, 6:7], col(A["L1_xattn_bg"])).then_inc(ld_yw, 16)
            with sp.Fori(1, net["depth"]) as layer:
                load_layer(net, layer, False)
            net = NETS[1]
            load_layer(net, 0, True)
            with sp.Fori(1, net["depth"]) as layer:
                load_layer(net, layer, False)
            sp.wait_ge(out_dve, NBLK)
            sp.dma_start(out.rearrange("b t d -> t b d"), cen[:].rearrange("p (b d) -> p b d", b=NB)).then_inc(out_st, 16)
            sp.wait_ge(out_st, 16)

        @block.tensor
        def _(pe):
            pe.wait_ge(ld_x, 32)
            pe.wait_ge(ld_c, 80)
            for src, o in ((cen, 0), (dev, 4)):
                for k in range(NBLK):
                    for j in range(4):
                        b = 4 * k + j
                        mm = nc.tensor.transpose(bank4[o + k][:, j, :], src[:, b * P:(b + 1) * P], ident[:])
                    mm.then_inc(in_ps, 1)

            pe.wait_ge(c_pool, 1)
            pe.wait_ge(in_act, NBLK)
            ln_pe(pe, 0, base_x, lambda e, k: e.wait_ge(in_dve, NBLK))
            pe.wait_ge(ld_xw, 9 * 16)
            for k in range(NBLK):
                pe.wait_ge(LN["xn"], k + 1)
                nc.tensor.matmul(bank[k][:], xw[:, 0, :], z[:, k * BLK:(k + 1) * BLK], start=True, stop=True
                                 ).then_inc(XP["q"], 1)
            for k in range(NBLK):
                nc.tensor.matmul(bank[4 + k][:], xw[:, 1, :], ctx_t[:, k * BLK:(k + 1) * BLK], start=True, stop=True
                                 ).then_inc(XP["k"], 1)
            for k in range(NBLK):
                pe.wait_ge(XP["qe"], k + 1)
                for j in range(4):
                    b = 4 * k + j
                    mm = nc.tensor.matmul(bank4[k][:, j, :], ctx_t[:, b * P:(b + 1) * P], xw[:, 2, :],
                                          start=True, stop=True)
                mm.then_inc(XP["v"], 1)

            def x0_step(st):
                pe_probs_t(pe, st, X0, 1)
                pe_values(pe, st, X0, 1)
                pe_project(pe, st, X0, 1)
                if st.has(1):
                    p = st.half(1)[1]
                    if st.c == 1 and st.r is None:
                        pe.wait_ge(XP["ve"], NBLK)
                        pe.wait_ge(XP["ke"], NBLK)
                    st.wait(pe, X0["prep"], 1)
                    for g in range(2):
                        st.wait(pe, X0["sh%d" % g], 2)
                        nc.tensor.matmul(bank[3 + g][:], xq_s[p][:], xk_s[p][:, 4 * g:4 * g + 4, :],
                                         start=True, stop=True).then_inc(X0["s%d" % g], 1)

            run_steps(pe, 32, 0, 3, x0_step)

            def transformer(net):
                ni, units, inner = net["idx"], net["units"], net["H"] * DH

                def steps(base, layer):
                    def step(st):
                        if st.has(2):
                            p = st.half(2)[1]
                            st.wait(pe, AT["mq"], 2)
                            st.wait(pe, AT["on0"], 4)
                            for j in range(4):
                                mm = nc.tensor.transpose(
                                    bank4[5][:, j, :], rc[0][p][:].rearrange("p h d -> p (h d)")[:, j * P:(j + 1) * P], ident[:])
                            mm.then_inc(AT["qt"], 1)
                            st.wait(pe, AT["mk"], 2)
                            st.wait(pe, AT["on1"], 4)
                            for j in range(4):
                                mm = nc.tensor.transpose(
                                    bank4[6][:, j, :], rc[1][p][:].rearrange("p h d -> p (h d)")[:, j * P:(j + 1) * P], ident[:])
                            mm.then_inc(AT["kt"], 1)
                        pe_probs_t(pe, st, AT, 2)
                        if st.has(0):
                            p = st.parity
                            if st.c == 0 and st.r is None:
                                pe.wait_ge(ld_qkv, (layer + (net["ff0"] + 1)) * 16)
                            st.wait(pe, AT["hs"], 0)
                            o = 512 * p if ni == 0 else 0
                            st.wait(pe, AT["rq"], 1)
                            nc.tensor.matmul(bank[0][:], hs[p][:], wqkv[:, o:o + 512], start=True, stop=True).then_inc(AT["q"], 1)
                            st.wait(pe, AT["rk"], 1)
                            nc.tensor.matmul(bank[1][:], hs[p][:], wqkv[:, inner + o:inner + o + 512], start=True, stop=True).then_inc(AT["k"], 1)
                            st.wait(pe, AT["ve"], 1)
                            nc.tensor.matmul(bank[2][:], hs[p][:], wqkv[:, 2 * inner + o:2 * inner + o + 512], start=True, stop=True).then_inc(AT["v"], 1)
                        pe_values(pe, st, AT, 2)
                        if st.c == 4 and st.r is None:
                            pe.wait_ge(ld_wo, (layer + (net["ff0"] + 1)) * 16)
                        pe_project(pe, st, AT, 2, ni)
                        if st.has(2):
                            st.wait(pe, AT["qte"], 2)
                            st.wait(pe, AT["kte"], 2)
                            for g in range(2):
                                st.wait(pe, AT["sh%d" % g], 3)
                                for j in range(2):
                                    pair = bank[3 + g][:, 256 * j:256 * j + 256]
                                    nc.tensor.matmul(pair, ident_b[:], mask_b[:, ni, 2 * j:2 * j + 2], start=True, stop=False)
                                    mm = nc.tensor.matmul(pair, q_t[:, 2 * g + j, :], k_blk[:, 2 * g + j], start=False, stop=True)
                                mm.then_inc(AT["s%d" % g], 1)
                    run_steps(pe, units, base, 4, step)

                def feed_forward(layer):
                    f = layer + net["ff0"]
                    ln_pe(pe, layer + net["ln0"], shifted[:].rearrange("p b t -> p (b t)"),
                          lambda e, k: (e.wait_ge(FF["lo"], f * 4 + (k + 1)), e.wait_ge(FF["hi"], f * 4 + (k + 1))))
                    pe.wait_ge(ld_ff, (f + 1) * 192)

                    def down(i):
                        k, c = divmod(i, 3)
                        w = CH[c][1]
                        pe.wait_ge(FF["hid"], f * 12 + (i + 1))
                        mm = nc.tensor.matmul(bank[4 + k][:], w2[0:w, c, :], hid[i % 3][0:w, :], start=(c == 0), stop=(c == 2))
                        if c == 2:
                            mm.then_inc(FF["y"], 1)

                    for i in range(3 * NBLK):
                        k, c = divmod(i, 3)
                        o, w = CH[c]
                        if c == 0:
                            pe.wait_ge(LN["aff"], f * 4 + (k + 1))
                        if i >= 2:
                            pe.wait_ge(FF["hid"], f * 12 + (i - 1))
                        x = cen[:, k * BLK:(k + 1) * BLK]
                        nc.tensor.matmul(bank[2 + i % 2][0:w, :], w1[:, HID + o:HID + o + w], x, start=True, stop=True)
                        nc.tensor.matmul(bank[i % 2][0:w, :], w1[:, o:o + w], x, start=True, stop=True).then_inc(FF["ag"], 1)
                        if i >= 2:
                            down(i - 2)
                    down(3 * NBLK - 2)
                    down(3 * NBLK - 1)

                ln_pe(pe, net["ln0"] - 1, base_x, src_ready[ni])
                with pe.Fori(0, net["depth"]) as layer:
                    steps(layer * units + net["base0"], layer)
                    feed_forward(layer)

            src_ready = [lambda e, k: e.wait_ge(X0["res"], 32), lambda e, k: e.wait_ge(YP["gm"], 3 * NBLK)]
            transformer(NETS[0])

            ln_pe(pe, 8, base_x, lambda e, k: e.wait_ge(FF["outer"], NBLK))
            pe.wait_ge(ld_yw, 14 * 16)
            for g in range(2):
                if g == 0:
                    pe.wait_ge(LN["xn"], 4 * 9)
                for i in range(4 * g, 4 * g + 4):
                    mm = nc.tensor.transpose(bank4[g][:, i % 4, :], yw_in[:, i, :], ident[:])
                mm.then_inc(YP["w"], 1)
            n = 0
            for a in range(4):
                src = z if a in (0, 3) else ctx_t
                for k in range(NBLK):
                    if n == 0:
                        pe.wait_ge(YP["we"], 2)
                    if n >= 6:
                        pe.wait_ge(YP["qke"], n - 5)
                    nc.tensor.matmul(bank[2 + n % 6][:], yw[:, a, :], src[:, k * BLK:(k + 1) * BLK], start=True, stop=True
                                     ).then_inc(YP["qk"], 1)
                    n += 1
            for b2 in range(NB // 2):
                if b2 >= 2:
                    pe.wait_ge(YP["ve"], b2 - 1)
                for j in range(2):
                    b = 2 * b2 + j
                    for a, src in enumerate((ctx_t, z)):
                        mm = nc.tensor.matmul(bank4[b2 % 2][:, 2 * j + a, :], src[:, b * P:(b + 1) * P], yw[:, 4 + a, :],
                                              start=True, stop=True)
                mm.then_inc(YP["v"], 1)
            pe.wait_ge(YP["qke"], 16)
            pe.wait_ge(YP["ve"], 8)
            with pe.Fori(0, NB // 2) as it:
                cnt = it + 1
                pe.wait_ge(YP["qs"], cnt)
                for j in range(2):
                    for a in range(2):
                        ks = y_qk[:, 2 * a + 1, :].rearrange("p (b t) -> p b t", b=NB)[:, it * 2 + j, :]
                        mm = nc.tensor.matmul(bank4[3][:, 2 * j + a, :], yq_s[:, j, a, :], ks, start=True, stop=True)
                mm.then_inc(YP["s"], 1)
                pe.wait_ge(YP["ex"], cnt)
                for i in range(4):
                    mm = nc.tensor.transpose(bank4[4][:, i, :], prob[0][:, i, :], ident[:])
                mm.then_inc(YP["pt"], 1)
                pe.wait_ge(YP["pte"], cnt)
                for j in range(2):
                    for a in range(2):
                        mm = nc.tensor.matmul(bank4[5][:, 2 * j + a, :], prob_t[0][:, 2 * j + a, :],
                                              y_v[:, it * 2 + j, a, :], start=True, stop=True)
                mm.then_inc(YP["o"], 1)
                pe.wait_ge(YP["on"], cnt)
                for i in range(4):
                    mm = nc.tensor.transpose(bank4[6][:, i, :], o_tok[:, i * P:(i + 1) * P], ident[:])
                mm.then_inc(YP["ot"], 1)
            pe.wait_ge(YP["ote"], 16)
            for k in range(NBLK):
                for a in range(2):
                    mm = nc.tensor.matmul(bank[k][:], yw[:, 6 + a, :], y_ctx[:, a, k * BLK:(k + 1) * BLK],
                                          start=(a == 0), stop=(a == 1))
                mm.then_inc(YP["g"], 1)

            transformer(NETS[1])

            pe.wait_ge(FF["outer"], 2 * NBLK)
            for k in range(NBLK):
                for j in range(4):
                    b = 4 * k + j
                    mm = nc.tensor.transpose(bank4[k][:, j, :], base_x[:, b * P:(b + 1) * P], ident[:])
                mm.then_inc(out_ps, 1)

        @block.scalar
        def _(act):
            act.wait_ge(ld_c, 80)
            nc.scalar.activation(ident_b[:], ident[:], ACT.Copy).then_inc(c_act, 1)
            for n in range(2):
                nc.scalar.activation(mask_b[:, n], mask_f[:, n, :].unsqueeze(1).to_broadcast([P, 4, P]), ACT.Copy
                                     ).then_inc(c_act, 1)
            for k in range(NBLK):
                act.wait_ge(in_ps, NBLK + k + 1)
                nc.scalar.activation(ctx_t[:, k * BLK:(k + 1) * BLK], bank[4 + k][:], ACT.Copy).then_inc(in_act, 1)
            act.wait_ge(c_pool, 1)
            ln_act(act, 0)
            act.wait_ge(ld_xw, 9 * 16)
            for k in range(NBLK):
                act.wait_ge(XP["q"], k + 1)
                nc.scalar.activation(x_q[:, k * BLK:(k + 1) * BLK], bank[k][:], ACT.Identity, bias=xb[:, 0:1]
                                     ).then_inc(XP["qe"], 1)
            act.wait_ge(c_pool, 2)
            for k in range(NBLK):
                act.wait_ge(XP["v"], k + 1)
                nc.scalar.activation(xv[:, 4 * k:4 * k + 4, :, 0:XD].rearrange("p b h d -> p (b h) d"),
                                     bank[k][:].rearrange("p (h d) -> p h d", d=XD), ACT.Copy
                                     ).then_inc(XP["ve"], 1)

            def x0_step(st):
                act_probs_t(act, st, X0, 1)
                act_exp(act, st, X0, 1, float(1 / np.sqrt(XD)))

            run_steps(act, 32, 0, 3, x0_step)

            def transformer(net):
                ni, units = net["idx"], net["units"]

                def step(st):
                    if st.has(2):
                        st.wait(act, AT["qt"], 2)
                        st.wait(act, AT["s1"], 3)
                        nc.scalar.activation(q_t[:], bank4[5], ACT.Copy).then_inc(AT["qte"], 1)
                        st.wait(act, AT["kt"], 2)
                        nc.scalar.activation(k_blk[0:DH, :, 0, :], bank4[6][0:DH], ACT.Copy)
                        nc.scalar.activation(k_blk[DH:P, :, 1, :], bank4[6][DH:P], ACT.Copy).then_inc(AT["kte"], 1)
                    act_probs_t(act, st, AT, 2)
                    if st.has(0):
                        st.wait(act, AT["q"], 0)
                        st.wait(act, AT["ssq"], 1)
                        nc.scalar.activation(sq[0][:].rearrange("p h d -> p (h d)"), bank[0][:], ACT.Square).then_inc(AT["sqq"], 1)
                        st.wait(act, AT["k"], 0)
                        st.wait(act, AT["ssk"], 1)
                        nc.scalar.activation(sq[1][:].rearrange("p h d -> p (h d)"), bank[1][:], ACT.Square).then_inc(AT["sqk"], 1)
                        st.wait(act, AT["v"], 0)
                        nc.scalar.activation(v_all[:, st.unit(0), :, 0:DH], bank[2][:].rearrange("p (h d) -> p h d", h=HU),
                                             ACT.Copy).then_inc(AT["ve"], 1)
                    act_exp(act, st, AT, 2, QK_SCALE)

                ln_act(act, net["ln0"] - 1)
                act.wait_ge(c_pool, 3 if ni == 0 else 4)
                with act.Fori(0, net["depth"]) as layer:
                    run_steps(act, units, layer * units + net["base0"], 4, step)
                    f = layer + net["ff0"]
                    act.wait_ge(AT["res"], (layer + 1) * units + net["base0"])
                    zb = z[:].rearrange("p (b t) -> p b t", b=NB)
                    for k in range(NBLK):
                        nc.scalar.activation(shifted[DH:P, 4 * k:4 * k + 4, 1:P], zb[DH:P, 4 * k:4 * k + 4, 0:P - 1],
                                             ACT.Copy).then_inc(FF["hi"], 1)
                    ln_act(act, layer + net["ln0"])
                    act.wait_ge(ld_ff, (f + 1) * 192)
                    for i in range(3 * NBLK):
                        w = CH[i % 3][1]
                        act.wait_ge(FF["ag"], f * 12 + (i + 1))
                        if i >= 2:
                            act.wait_ge(FF["hid"], f * 12 + (i - 1))
                        nc.scalar.activation(gl[i % 2][0:w, :], bank[2 + i % 2][0:w, :], ACT.Gelu,
                                             bias=b1[0:w, 3 + i % 3:4 + i % 3]).then_inc(FF["gelu"], 1)

            transformer(NETS[0])

            ln_act(act, 8)
            act.wait_ge(ld_yw, 14 * 16)
            for g in range(2):
                act.wait_ge(YP["w"], g + 1)
                nc.scalar.activation(yw[:, 4 * g:4 * g + 4, :], bank4[g], ACT.Copy).then_inc(YP["we"], 1)
            for n in range(16):
                act.wait_ge(YP["qk"], n + 1)
                nc.scalar.activation(y_qk[:, n // 4, (n % 4) * BLK:(n % 4 + 1) * BLK], bank[2 + n % 6][:], ACT.Identity,
                                     bias=yb[:, n // 4:n // 4 + 1]).then_inc(YP["qke"], 1)
            for b2 in range(NB // 2):
                act.wait_ge(YP["v"], b2 + 1)
                nc.scalar.activation(y_v[:, 2 * b2:2 * b2 + 2].rearrange("p b a n -> p (b a) n"), bank4[b2 % 2], ACT.Copy
                                     ).then_inc(YP["ve"], 1)
            with act.Fori(0, NB // 2) as it:
                cnt = it + 1
                act.wait_ge(YP["sh"], cnt)
                nc.scalar.activation(prob[0][:], prob[0][:], ACT.Exp, scale=float(1 / np.sqrt(P))).then_inc(YP["ex"], 1)
                act.wait_ge(YP["pt"], cnt)
                nc.scalar.activation(prob_t[0][:], bank4[4], ACT.Copy).then_inc(YP["pte"], 1)
                act.wait_ge(YP["ot"], cnt)
                src = bank4[6].rearrange("p (j a) n -> p j a n", j=2)
                for a in range(2):
                    dst = y_ctx[:, a, :].rearrange("p (i n) -> p i n", i=NB // 2)[:, it, :].rearrange("p (j n) -> p j n", j=2)
                    nc.scalar.activation(dst, src[:, :, a, :], ACT.Identity, bias=yb[:, 4 + a:5 + a]).then_inc(YP["ote"], 1)
            for k in range(NBLK):
                act.wait_ge(YP["g"], k + 1)
                nc.scalar.activation(dev[:, k * BLK:(k + 1) * BLK], bank[k][:], ACT.Sigmoid, bias=yb[:, 6:7]
                                     ).then_inc(YP["sg"], 1)
            transformer(NETS[1])

        @block.gpsimd
        def _(pool):
            nc.gpsimd.memset(eps_t[:], EPS)
            nc.gpsimd.memset(mean_w[:], 1.0 / P).then_inc(c_pool, 1)
            pool.wait_ge(c_pool, 1)
            nc.gpsimd.memset(big[:, 0:NB * XH * XVW], 1.0).then_inc(c_pool, 1)
            nc.gpsimd.memset(o_tok[:], 0.0)
            for i in range(2):
                nc.gpsimd.memset(hs[i][:], 0.0)
            nc.gpsimd.memset(k_blk[:], 0.0)
            nc.gpsimd.memset(shifted[:], 0.0)
            pool.wait_ge(ld_c, 80)
            pool.wait_ge(XP["qe"], NBLK)
            pool.wait_ge(XP["ke"], NBLK)

            def x0_step(st):
                if st.has(0):
                    b, p = st.half(0)
                    st.wait(pool, X0["prep"], 1)
                    st.wait(pool, X0["s1"], 2)
                    nc.gpsimd.tensor_tensor(tick[:], eps_t[:], eps_t[:], ALU.add)
                    nc.gpsimd.tensor_tensor(
                        xk_s[p], x_k.rearrange("p (b t) -> p b t", b=NB)[:, b, :].unsqueeze(1).to_broadcast([P, HU, P]),
                        head_m[:, HU * p:HU * p + HU].unsqueeze(2).to_broadcast([P, HU, P]), ALU.mult)
                    nc.gpsimd.tensor_copy(xq_s[p][:], x_q.rearrange("p (b t) -> p b t", b=NB)[:, b, :]
                                          ).then_inc(X0["prep"], 1)

            run_steps(pool, 32, 0, 3, x0_step)

            def transformer(net):
                ni, units = net["idx"], net["units"]
                def step(st):
                    if st.has(1):
                        p = st.half(1)[1]
                        st.wait(pool, NT[10], 1)
                        for i, (a, m) in enumerate((("aq", "mq"), ("ak", "mk"))):
                            st.wait(pool, AT[a], 1)
                            nc.gpsimd.tensor_tensor(rc[i][p][:], rc[i][p][:],
                                                    rnorm[p][:, HU * i:HU * i + HU].unsqueeze(2).to_broadcast([P, HU, DH]),
                                                    ALU.mult).then_inc(AT[m], 1)
                    if st.has(0):
                        p = st.parity
                        for i, (r_, a) in enumerate((("rq", "aq"), ("rk", "ak"))):
                            st.wait(pool, AT[r_], 0)
                            nc.gpsimd.tensor_tensor(rc[i][p][:], rc[i][p][:], rs[i][p][:], ALU.add).then_inc(AT[a], 1)

                if ni == 0:
                    pool.wait_ge(X0["res"], 32)
                else:
                    pool.wait_ge(YP["gm"], 3 * NBLK)
                nc.gpsimd.memset(v_all[:, 0:units, :, DH:VW].rearrange("p u h d -> p (u h) d"), 1.0).then_inc(c_pool, 1)
                with pool.Fori(0, net["depth"]) as layer:
                    run_steps(pool, units, layer * units + net["base0"], 4, step)

            transformer(NETS[0])
            pool.wait_ge(YP["qke"], 16)
            with pool.Fori(0, NB // 2) as it:
                for a in range(2):
                    q = y_qk[:, 2 * a, :].rearrange("p (i n) -> p i n", i=NB // 2)[:, it, :].rearrange("p (j n) -> p j n", j=2)
                    cp = nc.gpsimd.tensor_copy(yq_s[:, :, a, :], q)
                cp.then_inc(YP["qs"], 1)
                pool.wait_ge(YP["s"], it + 1)
            transformer(NETS[1])

        @block.vector
        def _(dve):
            for k in range(NBLK):
                dve.wait_ge(in_ps, k + 1)
                nc.vector.tensor_copy(base_x[:, k * BLK:(k + 1) * BLK], bank[k][:]).then_inc(in_dve, 1)
            dve.wait_ge(in_dve, NBLK)
            dve.wait_ge(in_ps, 2 * NBLK)
            ln_dve(dve, 0, base_x, z, False)
            dve.wait_ge(ld_xw, 9 * 16)
            for k in range(NBLK):
                dve.wait_ge(XP["k"], k + 1)
                nc.vector.tensor_scalar(x_k[:, k * BLK:(k + 1) * BLK], bank[4 + k][:], xb[:, 1:2], None, ALU.add
                                        ).then_inc(XP["ke"], 1)

            def x0_step(st):
                for g in range(2):
                    dve_rsum(dve, st, X0, 1, g)
                for g in range(2):
                    dve_divide(dve, st, X0, 1, g)
                dve_residual(dve, st, X0, 1)
                for g in range(2):
                    dve_max(dve, st, X0, 1, g)
                for g in range(2):
                    dve_shift(dve, st, X0, 1, g)

            run_steps(dve, 32, 0, 3, x0_step)

            def newton(st, i):
                if not st.has(0):
                    return
                if i > 0:
                    st.wait(dve, NT[i - 1], 0)
                if i == 0:
                    st.wait(dve, AT["ssq"], 0)
                    st.wait(dve, AT["ssk"], 0)
                    ins = nc.vector.tensor_scalar(ssc[:], ss[:], 1e-24, None, ALU.max)
                elif i == 1:
                    ins = nc.vector.tensor_scalar(nt_y[0][:].bitcast(I32), ssc[:].bitcast(I32), -0.5, MAGIC, ALU.mult, ALU.add)
                else:
                    n, part = divmod(i - 2, 3)
                    y = nt_y[n]
                    dst = nt_y[n + 1] if n < 2 else rnorm[st.parity]
                    if part == 0:
                        ins = nc.vector.scalar_tensor_tensor(out=nt_a[:], in0=y[:], scalar=-0.5, in1=y[:],
                                                             op0=ALU.mult, op1=ALU.mult)
                    elif part == 1:
                        ins = nc.vector.tensor_tensor(nt_b[:], nt_a[:], ssc[:], ALU.mult)
                    else:
                        if n == 2:
                            st.wait(dve, AT["mk"], 2)
                        ins = nc.vector.scalar_tensor_tensor(out=dst[:], in0=nt_b[:], scalar=1.5, in1=y[:],
                                                             op0=ALU.add, op1=ALU.mult)
                ins.then_inc(NT[i], 1)

            def rotate(st, i):
                if not st.has(0):
                    return
                p = st.parity
                st.wait(dve, AT["sqq" if i == 0 else "sqk"], 0)
                st.wait(dve, AT["qt" if i == 0 else "kt"], 2)
                src = bank[i][:].rearrange("p (h d) -> p h d", h=HU)
                nc.vector.tensor_tensor(rc[i][p][:], src, rot[:, 2 * i, :].unsqueeze(1).to_broadcast([P, HU, DH]), ALU.mult)
                hd = DH // 2
                for a in range(2):
                    dst = rs[i][p][:, :, a * hd:(a + 1) * hd]
                    ins = nc.vector.tensor_tensor(dst, src[:, :, (1 - a) * hd:(2 - a) * hd],
                                                  rot[:, 2 * i + 1, a * hd:(a + 1) * hd].unsqueeze(1).to_broadcast([P, HU, hd]),
                                                  ALU.mult)
                ins.then_inc(AT["rq" if i == 0 else "rk"], 1)

            def sum_squares(st, i):
                if st.has(0):
                    st.wait(dve, AT["sqq" if i == 0 else "sqk"], 0)
                    nc.vector.tensor_reduce(ss[:, HU * i:HU * i + HU], sq[i][:], AX.X, ALU.add
                                            ).then_inc(AT["ssq" if i == 0 else "ssk"], 1)

            def transformer(net):
                ni, units = net["idx"], net["units"]

                zb = z[:].rearrange("p (b t) -> p b t", b=NB)

                def shift(st, lag):
                    if not st.has(lag):
                        return
                    b = batch_of(ni, st, lag)
                    p = (st.c - lag) % 2
                    st.wait(dve, AT["v"], lag + 2)
                    nc.vector.tensor_scalar(hs[p][0:DH, :], zb[0:DH, b, :], 1.0, None, ALU.mult)
                    nc.vector.tensor_scalar(hs[p][DH:P, 1:P], zb[DH:P, b, 0:P - 1], 1.0, None, ALU.mult
                                            ).then_inc(AT["hs"], 1)

                def step(st):
                    if st.c == 0 and st.r is None:
                        shift(st, 0)
                    rotate(st, 0)
                    shift(st, -1)
                    sum_squares(st, 0)
                    sum_squares(st, 1)
                    newton(st, 0)
                    rotate(st, 1)
                    newton(st, 1)
                    dve_rsum(dve, st, AT, 2, 0)
                    newton(st, 2)
                    dve_rsum(dve, st, AT, 2, 1)
                    newton(st, 3)
                    dve_divide(dve, st, AT, 2, 0)
                    newton(st, 4)
                    dve_divide(dve, st, AT, 2, 1)
                    newton(st, 5)
                    dve_max(dve, st, AT, 2, 0)
                    newton(st, 6)
                    dve_max(dve, st, AT, 2, 1)
                    newton(st, 7)
                    dve_shift(dve, st, AT, 2, 0)
                    newton(st, 8)
                    dve_shift(dve, st, AT, 2, 1)
                    newton(st, 9)
                    dve_residual(dve, st, AT, 2, ni)
                    newton(st, 10)

                m0 = net["ln0"] - 1
                ln_dve(dve, m0, base_x, z, False)
                dve.wait_ge(LN["xn"], net["ln0"] * 4)
                with dve.Fori(0, net["depth"]) as layer:
                    f = layer + net["ff0"]
                    base = layer * units + net["base0"]
                    dve.wait_ge(ld_rot, (f + 1) * 32)
                    for i in range(2):
                        nc.vector.tensor_tensor(rot[:, 2 * i, :], rot_c[ni][:, 2 * i, :], qks[:, i, :], ALU.mult)
                        hd = DH // 2
                        for a in range(2):
                            ins = nc.vector.tensor_tensor(rot[:, 2 * i + 1, a * hd:(a + 1) * hd],
                                                          rot_c[ni][:, 2 * i + 1, a * hd:(a + 1) * hd],
                                                          qks[:, i, (1 - a) * hd:(2 - a) * hd], ALU.mult)
                    ins.then_inc(AT["rot"], 1)
                    dve.wait_ge(AT["rot"], f + 1)
                    run_steps(dve, units, base, 4, step)
                    dve.wait_ge(AT["res"], base + units)
                    zb = z[:].rearrange("p (b t) -> p b t", b=NB)
                    for k in range(NBLK):
                        nc.vector.tensor_copy(shifted[0:DH, 4 * k:4 * k + 4, :], zb[0:DH, 4 * k:4 * k + 4, :]
                                              ).then_inc(FF["lo"], 1)
                    dve.wait_ge(FF["lo"], f * 4 + 4)
                    dve.wait_ge(FF["hi"], f * 4 + 4)
                    dve.wait_ge(ld_ff, (f + 1) * 192)
                    ln_dve(dve, layer + net["ln0"], shifted[:].rearrange("p b t -> p (b t)"), cen, True)

                    def close(k):
                        b = slice(k * BLK, (k + 1) * BLK)
                        dve.wait_ge(FF["y"], f * 4 + (k + 1))
                        nc.vector.scalar_tensor_tensor(out=z[:, b], in0=bank[4 + k][:], scalar=lnp[:, 2:3], in1=z[:, b],
                                                       op0=ALU.add, op1=ALU.add).then_inc(FF["z"], 1)

                    for i in range(3 * NBLK):
                        w = CH[i % 3][1]
                        dve.wait_ge(FF["gelu"], f * 12 + (i + 1))
                        nc.vector.scalar_tensor_tensor(out=hid[i % 3][0:w, :], in0=bank[i % 2][0:w, :],
                                                       scalar=b1[0:w, i % 3:i % 3 + 1], in1=gl[i % 2][0:w, :],
                                                       op0=ALU.add, op1=ALU.mult).then_inc(FF["hid"], 1)
                        if i % 3 == 1 and i > 3:
                            close(i // 3 - 1)
                    close(NBLK - 1)
                    dve.wait_ge(FF["z"], f * 4 + 4)
                for k in range(NBLK):
                    b = slice(k * BLK, (k + 1) * BLK)
                    nc.vector.tensor_tensor(base_x[:, b], base_x[:, b], z[:, b], ALU.add).then_inc(FF["outer"], 1)

            dve.wait_ge(X0["res"], 32)
            transformer(NETS[0])
            dve.wait_ge(FF["outer"], NBLK)
            ln_dve(dve, 8, base_x, z, False)
            with dve.Fori(0, NB // 2) as it:
                cnt = it + 1
                dve.wait_ge(YP["s"], cnt)
                nc.vector.tensor_reduce(mx[:, 0:4], bank4[3], AX.X, ALU.max).then_inc(YP["mx"], 1)
                dve.wait_ge(YP["mx"], cnt)
                nc.vector.tensor_tensor(prob[0][:], bank4[3], mx[:, 0:4].unsqueeze(2).to_broadcast([P, 4, P]),
                                        ALU.subtract).then_inc(YP["sh"], 1)
                dve.wait_ge(YP["ex"], cnt)
                nc.vector.tensor_reduce(mx[:, 4:8], prob[0][:], AX.X, ALU.add).then_inc(YP["rs"], 1)
                dve.wait_ge(YP["rs"], cnt)
                nc.vector.reciprocal(rsum[:, 0, :], mx[:, 4:8]).then_inc(YP["rr"], 1)
                dve.wait_ge(YP["rr"], cnt)
                dve.wait_ge(YP["o"], cnt)
                nc.vector.tensor_tensor(o_tok[:].rearrange("p (i n) -> p i n", i=4), bank4[5],
                                        rsum[:, 0, :].unsqueeze(2).to_broadcast([P, 4, P]), ALU.mult).then_inc(YP["on"], 1)
            dve.wait_ge(YP["ote"], 16)
            for k in range(NBLK):
                b = slice(k * BLK, (k + 1) * BLK)
                nc.vector.tensor_tensor(cen[:, b], y_ctx[:, 0, b], y_ctx[:, 1, b], ALU.subtract).then_inc(YP["gd"], 1)
            for k in range(NBLK):
                b = slice(k * BLK, (k + 1) * BLK)
                dve.wait_ge(YP["gd"], k + 1)
                nc.vector.tensor_tensor(base_x[:, b], base_x[:, b], y_ctx[:, 1, b], ALU.add).then_inc(YP["gm"], 1)
            for k in range(NBLK):
                b = slice(k * BLK, (k + 1) * BLK)
                dve.wait_ge(YP["sg"], k + 1)
                nc.vector.tensor_tensor(cen[:, b], cen[:, b], dev[:, b], ALU.mult).then_inc(YP["gm"], 1)
            for k in range(NBLK):
                b = slice(k * BLK, (k + 1) * BLK)
                dve.wait_ge(YP["gm"], NBLK + k + 1)
                nc.vector.tensor_tensor(base_x[:, b], base_x[:, b], cen[:, b], ALU.add).then_inc(YP["gm"], 1)
            dve.wait_ge(YP["gm"], 3 * NBLK)
            transformer(NETS[1])
            for k in range(NBLK):
                dve.wait_ge(out_ps, k + 1)
                nc.vector.tensor_copy(cen[:, k * BLK:(k + 1) * BLK], bank[k][:]).then_inc(out_dve, 1)


_INS = ["x", "ctx_1024"] + ["L0_xattn_" + n for n in "Wq bq Wk bk Wv bv Wo bo".split()] \
    + ["L0_ffn_" + n for n in "Wqkv q_scale k_scale Wo ln_g ln_b W1 b1 W2 b2".split()] \
    + ["L1_xattn_" + n for n in "Wq_c bq_c Wk_s bk_s Wv_s bv_s Wq_s bq_s Wk_c bk_c Wv_c bv_c Wg bg".split()] \
    + ["L1_ffn_" + n for n in "wqkv q_scale k_scale wo ln_g ln_b w1 b1 w2 b2".split()]


def kernel(**inputs):
    import concourse.bacc as _bacc
    from concourse.bass_utils import run_bass_kernel_spmd as _run

    nc = _bacc.Bacc("TRN2", target_bir_lowering=False, num_devices=1)
    arrays, aps = {}, {}
    for name in _INS:
        a = np.ascontiguousarray(inputs[name])
        arrays[f"in_{name}_dram"] = a
        aps[name] = nc.dram_tensor(f"in_{name}_dram", a.shape, mybir.dt.from_np(a.dtype), kind="ExternalInput").ap()
    out = nc.dram_tensor("out_0_dram", (NB, P, P), F32, kind="ExternalOutput").ap()
    build(nc, aps, out)
    r = _run(nc, [arrays], core_ids=[0])
    return r.results[0]["out_0_dram"]
```

```python
from contextlib import ExitStack

import numpy as np

import concourse.bass as bass
from concourse import mybir

ALU = mybir.AluOpType
ACT = mybir.ActivationFunctionType
F32 = mybir.dt.float32
I32 = mybir.dt.int32
BF16 = mybir.dt.bfloat16
AX = mybir.AxisListType

P = 128
NB = 16
TOK = NB * P
BLK = 512
NBLK = TOK // BLK
HU = 8
DH = 64
XH, XD = 16, 8
HID = int(P * 4 * 2 / 3)
CH = [(0, 128), (128, 128), (256, HID - 256)]
EPS = 1e-5
QK_SCALE = 8.0
MAGIC = float(0x5F3759DF)
MASKED = -1e30
PEEL = 6


def rotary_constants(window):
    half = np.arange(0, DH, 2, dtype=np.float32)
    inv_freq = (1.0 / 10000.0 ** (half / DH)).astype(np.float32)
    t = np.arange(P, dtype=np.float32)
    freqs = t[:, None] * inv_freq[None, :]
    base = (half + np.float32(0.4 * DH)) / np.float32(1.4 * DH)
    power = (t - P // 2) / np.float32(window // 2)
    scale = base[None, :] ** power[:, None]
    two = lambda a: np.concatenate([a, a], -1)
    cos, sin, scale = two(np.cos(freqs)), np.sin(freqs), two(scale)
    sin = np.concatenate([-sin, sin], -1)
    return [a.astype(np.float32) for a in (QK_SCALE * cos * scale, QK_SCALE * sin * scale, cos / scale, sin / scale)]


def mask_constant(window):
    i, j = np.arange(P)[:, None], np.arange(P)[None, :]
    return np.where((i < j) | (i > j + window) | (j < (i // window - 1) * window), np.float32(MASKED), np.float32(0))


class Step:

    def __init__(self, units, base, c, r=None):
        self.units, self.base, self.c, self.r = units, base, c, r

    @property
    def parity(self):
        return self.c % 2

    def has(self, lag):
        return self.r is not None or 0 <= self.c - lag < self.units

    def count(self, lag):
        n = self.c + 1 - lag
        if self.r is not None:
            n = self.r * 2 + n
        return self.base + n

    def unit(self, lag):
        return self.c - lag if self.r is None else self.r * 2 + (self.c - lag)

    def half(self, lag):
        n = self.c - lag
        return (n // 2 if self.r is None else self.r + n // 2), n % 2

    def wait(self, eng, sem, lag):
        if self.has(lag):
            eng.wait_ge(sem, self.count(lag))


def run_steps(eng, units, base, last_lag, step):
    for c in range(PEEL):
        step(Step(units, base, c))
    with eng.Fori(0, (units - PEEL) // 2 - 1) as r:
        for c in (PEEL, PEEL + 1):
            step(Step(units, base, c, r))
    for c in range(units - 2, units + last_lag):
        step(Step(units, base, c))


def build(nc, A, out):
    const = lambda name, a: nc.inline_tensor(np.ascontiguousarray(a), name=name).ap()
    c_ident = const("c_ident", np.eye(P, dtype=np.float32))
    c_rot = [const(f"c_rot{n}", np.concatenate(rotary_constants(w), 1)) for n, w in enumerate((32, 64))]
    c_mask = const("c_mask", np.concatenate([mask_constant(32), mask_constant(64)], 1))
    c_vmask = const("c_vmask", np.tile(np.repeat(np.eye(HU), XD, 1).reshape(1, -1), (P, 1)).astype(np.float32))
    c_head = const("c_head", (np.arange(P)[:, None] // XD == np.arange(XH)[None, :]).astype(np.float32))

    with ExitStack() as ctx:
        sb = lambda name, shape, dt=F32: ctx.enter_context(nc.sbuf_tensor(name, shape, dt))
        sem = lambda name: ctx.enter_context(nc.semaphore(name))
        bank = [ctx.enter_context(nc.psum_tensor(f"bank{i}", [P, BLK], F32)) for i in range(8)]
        bank4 = [b[:].rearrange("p (a n) -> p a n", a=4) for b in bank]

        ident = sb("ident", [P, P])
        ident_b = sb("ident_b", [P, P], BF16)
        mean_w = sb("mean_w", [P, P])
        rot_c = [sb(f"rot_c{n}", [P, 4, DH]) for n in range(2)]
        mask_f = sb("mask_f", [P, 2, P])
        mask_b = sb("mask_b", [P, 2, 4, P], BF16)
        head_m = sb("head_m", [P, XH])
        v_mask = sb("v_mask", [P, HU, HU * XD])
        wqkv = sb("wqkv", [P, 3 * 1024])
        wo = sb("wo", [P, 8, P])
        w1 = sb("w1", [P, 2 * HID])
        w2 = sb("w2", [P, 3, P])
        b1 = sb("b1", [P, 6])
        lnp = sb("lnp", [P, 3])
        qks = sb("qks", [P, 2, DH])
        rot = sb("rot", [P, 4, DH])
        xw = sb("xw", [P, 3, P])
        xwo = sb("xwo", [DH, 2, P])
        xb = sb("xb", [P, 3])
        xbv = sb("xbv", [DH, 2])
        yw_in = sb("yw_in", [P, 8, P])
        yw = sb("yw", [P, 8, P])
        yb = sb("yb", [P, 7])

        base_x = sb("base_x", [P, TOK])
        z = sb("z", [P, TOK])
        ctx_t = sb("ctx_t", [P, TOK])
        shifted = sb("shifted", [P, NB, P])
        cen = sb("cen", [P, TOK])
        dev = sb("dev", [P, TOK])
        big = sb("big", [P, 8 * TOK])
        x_q, x_k, x_v = (big[:, i * TOK:(i + 1) * TOK] for i in range(3))
        xk_s = [big[:, 3 * TOK + i * HU * P:3 * TOK + (i + 1) * HU * P].rearrange("p (h t) -> p h t", h=HU) for i in range(2)]
        xv_s = [big[:, 4 * TOK + i * HU * DH:4 * TOK + (i + 1) * HU * DH].rearrange("p (h t) -> p h t", h=HU) for i in range(2)]
        gl = [big[:, i * BLK:(i + 1) * BLK] for i in range(2)]
        hid = [big[:, i * BLK:(i + 1) * BLK] for i in range(2, 5)]
        y_qk = big[:, 0:4 * TOK].rearrange("p (a n) -> p a n", a=4)
        y_v = big[:, 4 * TOK:6 * TOK].rearrange("p (b a n) -> p b a n", b=NB, a=2)
        y_ctx = big[:, 6 * TOK:8 * TOK].rearrange("p (a n) -> p a n", a=2)

        hs = [sb(f"hs{i}", [P, P]) for i in range(2)]
        hv = [sb(f"hv{i}", [P, P]) for i in range(2)]
        v_s = [sb(f"v_s{i}", [P, HU, DH]) for i in range(2)]
        sq = [sb(f"sq{i}", [P, HU, DH]) for i in range(2)]
        rc = [[sb(f"rc{i}{j}", [P, HU, DH]) for j in range(2)] for i in range(2)]
        rs = [[sb(f"rs{i}{j}", [P, HU, DH]) for j in range(2)] for i in range(2)]
        ss = sb("ss", [P, 2 * HU])
        ssc = sb("ssc", [P, 2 * HU])
        nt_y = [sb(f"nt_y{i}", [P, 2 * HU]) for i in range(3)]
        nt_a = sb("nt_a", [P, 2 * HU])
        nt_b = sb("nt_b", [P, 2 * HU])
        rnorm = [sb(f"rnorm{i}", [P, 2 * HU]) for i in range(2)]
        q_t = sb("q_t", [P, 4, P])
        k_blk = sb("k_blk", [P, 4, 2, P])
        xq_s = [sb(f"xq_s{i}", [P, P]) for i in range(2)]
        nmx = sb("nmx", [P, HU])
        rsum = sb("rsum", [P, HU])
        rinv = sb("rinv", [P, HU])
        xbq = sb("xbq", [P, 1])
        rstd = sb("rstd", [P, NB])
        lt_s = sb("lt_s", [P, NB])
        lt_y = [sb(f"lt_y{i}", [P, NB]) for i in range(3)]
        lt_a = sb("lt_a", [P, NB])
        lt_b = sb("lt_b", [P, NB])
        prob = [[sb(f"prob{g}", [P, 4, P])[:] for g in range(2)],
                [big[:, 6 * TOK + g * BLK:6 * TOK + (g + 1) * BLK].rearrange("p (h t) -> p h t", h=4) for g in range(2)]]
        prob_t = [sb(f"prob_t{g}", [P, 4, P]) for g in range(2)]
        o_tok = sb("o_tok", [P, HU * DH])
        o_t = sb("o_t", [P, 4, P])
        yq_s = sb("yq_s", [P, 2, 2, P])

        ld_c, ld_x, ld_xw, ld_yw = sem("ld_c"), sem("ld_x"), sem("ld_xw"), sem("ld_yw")
        ld_qkv, ld_rot, ld_wo, ld_ff = sem("ld_qkv"), sem("ld_rot"), sem("ld_wo"), sem("ld_ff")
        c_dve, c_act, c_pool = sem("c_dve"), sem("c_act"), sem("c_pool")
        in_ps, in_dve, in_act = sem("in_ps"), sem("in_dve"), sem("in_act")
        out_ps, out_dve, out_st = sem("out_ps"), sem("out_dve"), sem("out_st")
        LN = {n: sem("ln_" + n) for n in "mean cen sq var bc xn aff".split()}
        LNT = [sem(f"lnt{i}") for i in range(11)]
        FF = {n: sem("ff_" + n) for n in "lo hi ag gelu hid y z outer".split()}
        XP = {n: sem("xp_" + n) for n in "q k v qe ke ve bq".split()}
        YP = {n: sem("yp_" + n) for n in "w we qk qke v ve g gd gm sg s mx sh ex rs pt pte o rr on ot ote qs".split()}
        COMMON = "s0 s1 mx0 mx1 ex0 ex1 ri0 ri1 pn0 pn1 pt0 pt1 pe0 pe1 o ote y res".split()
        X0 = {n: sem("x0_" + n) for n in COMMON + "kp qp vp".split()}
        AT = {n: sem("at_" + n) for n in COMMON + "hs hv q k v sqq sqk ve rq rk ssq ssk aq ak mq mk qt kt qte kta ktb rot".split()}
        NT = [sem(f"nt{i}") for i in range(11)]

        NETS = [dict(idx=0, H=16, depth=6, units=32, base0=0, ff0=0, ln0=2, pre="L0_ffn_",
                     Wqkv="Wqkv", Wo="Wo", W1="W1", W2="W2"),
                dict(idx=1, H=8, depth=2, units=16, base0=192, ff0=6, ln0=10, pre="L1_ffn_",
                     Wqkv="wqkv", Wo="wo", W1="w1", W2="w2")]

        def batch_of(net_idx, st, lag):
            return st.half(lag)[0] if net_idx == 0 else st.unit(lag)

        def ln_pe(pe, m, src, ready):
            for k in range(NBLK):
                ready(pe, k)
                nc.tensor.matmul(bank[k][:], mean_w[:], src[:, k * BLK:(k + 1) * BLK],
                                 start=True, stop=True).then_inc(LN["mean"], 1)
            for k in range(NBLK):
                pe.wait_ge(LN["sq"], m * 4 + (k + 1))
                for b in range(4 * k, 4 * k + 4):
                    mm = nc.tensor.matmul(bank[4][:, 2 * b:2 * b + 2], dev[:, b * P:(b + 1) * P], mean_w[:, 0:2],
                                          start=True, stop=True)
            mm.then_inc(LN["var"], 1)
            pe.wait_ge(LNT[10], m + 1)
            for k in range(NBLK):
                for j in range(4):
                    b = 4 * k + j
                    mm = nc.tensor.transpose(bank4[4 + k][:, j, :], rstd[:, b:b + 1].to_broadcast([P, P]), ident[:])
                mm.then_inc(LN["bc"], 1)

        def ln_act(act, m):
            for k in range(NBLK):
                b = slice(k * BLK, (k + 1) * BLK)
                act.wait_ge(LN["cen"], m * 4 + (k + 1))
                nc.scalar.activation(dev[:, b], cen[:, b], ACT.Square).then_inc(LN["sq"], 1)

        def ln_dve(dve, m, src, dst, affine):
            for k in range(NBLK):
                b = slice(k * BLK, (k + 1) * BLK)
                dve.wait_ge(LN["mean"], m * 4 + (k + 1))
                nc.vector.tensor_tensor(cen[:, b], src[:, b], bank[k][:], ALU.subtract).then_inc(LN["cen"], 1)
            dve.wait_ge(LN["var"], m + 1)
            var = bank[4][:, 0:2 * NB].rearrange("p (b a) -> p b a", a=2)[:, :, 0]
            nc.vector.tensor_scalar(lt_s[:], var, EPS, None, ALU.add).then_inc(LNT[0], 1)
            dve.wait_ge(LNT[0], m + 1)
            nc.vector.tensor_scalar(lt_y[0][:].bitcast(I32), lt_s[:].bitcast(I32), -0.5, MAGIC, ALU.mult, ALU.add
                                    ).then_inc(LNT[1], 1)
            for n in range(3):
                y, dst_y = lt_y[n], lt_y[n + 1] if n < 2 else rstd
                dve.wait_ge(LNT[3 * n + 1], m + 1)
                nc.vector.scalar_tensor_tensor(out=lt_a[:], in0=y[:], scalar=-0.5, in1=y[:], op0=ALU.mult, op1=ALU.mult
                                               ).then_inc(LNT[3 * n + 2], 1)
                dve.wait_ge(LNT[3 * n + 2], m + 1)
                nc.vector.tensor_tensor(lt_b[:], lt_a[:], lt_s[:], ALU.mult).then_inc(LNT[3 * n + 3], 1)
                dve.wait_ge(LNT[3 * n + 3], m + 1)
                nc.vector.scalar_tensor_tensor(out=dst_y[:], in0=lt_b[:], scalar=1.5, in1=y[:], op0=ALU.add, op1=ALU.mult
                                               ).then_inc(LNT[3 * n + 4], 1)
            for k in range(NBLK):
                b = slice(k * BLK, (k + 1) * BLK)
                dve.wait_ge(LN["bc"], m * 4 + (k + 1))
                nc.vector.tensor_tensor(dst[:, b], cen[:, b], bank[4 + k][:], ALU.mult).then_inc(LN["xn"], 1)
                if affine:
                    dve.wait_ge(LN["xn"], m * 4 + (k + 1))
                    nc.vector.tensor_scalar(dst[:, b], dst[:, b], lnp[:, 0:1], lnp[:, 1:2],
                                            ALU.mult, ALU.add).then_inc(LN["aff"], 1)

        def pe_probs_t(pe, st, S, lc):
            if st.has(lc + 2):
                p = st.half(lc + 2)[1]
                st.wait(pe, S["pn0"], lc + 2)
                if S is AT and st.has(lc):
                    st.wait(pe, S["qte"], lc)
                else:
                    st.wait(pe, S["pe0"], lc + 3)
                for h in range(4):
                    mm = nc.tensor.transpose(bank4[5][:, h, :], prob[p][0][:, h, :], ident[:])
                mm.then_inc(S["pt0"], 1)
                st.wait(pe, S["pn1"], lc + 2)
                if S is AT and st.has(lc):
                    st.wait(pe, S["kta"], lc)
                    st.wait(pe, S["ktb"], lc)
                else:
                    st.wait(pe, S["pe1"], lc + 3)
                for h in range(4):
                    mm = nc.tensor.transpose(bank4[6][:, h, :], prob[p][1][:, h, :], ident[:])
                mm.then_inc(S["pt1"], 1)

        def pe_values(pe, st, S, lc):
            if st.has(lc + 2):
                p = st.half(lc + 2)[1]
                st.wait(pe, S["pe0"], lc + 2)
                if S is AT:
                    st.wait(pe, S["ve"], lc + 2)
                else:
                    st.wait(pe, S["vp"], lc + 2)
                st.wait(pe, S["res"], lc + 3)
                for h in range(HU):
                    if h == 4:
                        st.wait(pe, S["pe1"], lc + 2)
                    pt = prob_t[h // 4][:, h % 4, :]
                    if S is AT:
                        a = DH * (h % 2)
                        mm = nc.tensor.matmul(bank4[7][a:a + DH, h // 2, :], v_s[p][:, h, :], pt, start=True, stop=True)
                    else:
                        mm = nc.tensor.matmul(bank4[7][0:DH, 0, :], xv_s[p][:, h, :], pt,
                                              start=(h == 0), stop=(h == HU - 1))
                mm.then_inc(S["o"], 1)

        def pe_project(pe, st, S, lc, net=0):
            if st.has(lc + 2):
                st.wait(pe, S["ote"], lc + 2)
                p = st.half(lc + 2)[1]
                if S is AT:
                    for j in range(4):
                        mm = nc.tensor.matmul(bank4[7][:, 0, :], wo[:, (4 * p if net == 0 else 0) + j, :],
                                              o_t[:, j, :], start=(j == 0), stop=(j == 3))
                else:
                    mm = nc.tensor.matmul(bank4[7][:, 0, :], xwo[:, p, :], o_t[0:DH, 0, :], start=True, stop=True)
                mm.then_inc(S["y"], 1)

        def act_probs_t(act, st, S, lc):
            if st.has(lc + 2):
                for g in range(2):
                    st.wait(act, S["pt%d" % g], lc + 2)
                    st.wait(act, S["o"], lc + 3)
                    nc.scalar.activation(prob_t[g][:], bank4[5 + g], ACT.Copy).then_inc(S["pe%d" % g], 1)

        def act_outputs(act, st, S, lc):
            if st.has(lc + 2):
                st.wait(act, S["o"], lc + 2)
                st.wait(act, S["y"], lc + 3)
                if S is AT:
                    nc.scalar.activation(o_t[:], bank4[7], ACT.Copy).then_inc(S["ote"], 1)
                else:
                    p = st.half(lc + 2)[1]
                    nc.scalar.activation(o_t[0:DH, 0, :], bank4[7][0:DH, 0, :], ACT.Identity,
                                         bias=xbv[:, p:p + 1]).then_inc(S["ote"], 1)

        def act_exp(act, st, S, lc, g):
            if st.has(lc + 1):
                st.wait(act, S["mx%d" % g], lc + 1)
                p = st.half(lc + 1)[1]
                st.wait(act, S["pt%d" % g], lc + 3)
                st.wait(act, S["ri%d" % g], lc + 2)
                for h in range(4):
                    ins = nc.scalar.activation(prob[p][g][:, h, :], bank4[3 + g][:, h, :], ACT.Exp,
                                               bias=nmx[:, 4 * g + h:4 * g + h + 1],
                                               accum_out=rsum[:, 4 * g + h:4 * g + h + 1])
                ins.then_inc(S["ex%d" % g], 1)

        def dve_max(dve, st, S, lc, g):
            if st.has(lc):
                st.wait(dve, S["s%d" % g], lc)
                nc.vector.tensor_reduce(nmx[:, 4 * g:4 * g + 4], bank4[3 + g], AX.X, ALU.max, negate=True
                                        ).then_inc(S["mx%d" % g], 1)

        def dve_rinv(dve, st, S, lc, g):
            if st.has(lc + 1):
                st.wait(dve, S["ex%d" % g], lc + 1)
                st.wait(dve, S["pn%d" % g], lc + 2)
                nc.vector.reciprocal(rinv[:, 4 * g:4 * g + 4], rsum[:, 4 * g:4 * g + 4]).then_inc(S["ri%d" % g], 1)

        def pool_divide(pool, st, S, lc, g):
            if st.has(lc + 1):
                st.wait(pool, S["ri%d" % g], lc + 1)
                p = st.half(lc + 1)[1]
                nc.gpsimd.tensor_tensor(prob[p][g], prob[p][g],
                                        rinv[:, 4 * g:4 * g + 4].unsqueeze(2).to_broadcast([P, 4, P]),
                                        ALU.mult).then_inc(S["pn%d" % g], 1)

        def dve_residual(dve, st, S, lc, lag, net=0):
            if st.has(lag):
                st.wait(dve, S["y"], lag)
                st.wait(dve, S["res"], lag + 1)
                half = st.half(lag)
                b = batch_of(net, st, lag)
                if S is AT:
                    x = z[:].rearrange("p (b t) -> p b t", b=NB)[:, b, :]
                    nc.vector.tensor_tensor(x, bank4[7][:, 0, :], x, ALU.add).then_inc(S["res"], 1)
                else:
                    x = base_x[:].rearrange("p (b t) -> p b t", b=NB)[:, half[0], :]
                    if half[1] == 0:
                        nc.vector.scalar_tensor_tensor(out=x, in0=bank4[7][:, 0, :], scalar=xb[:, 2:3], in1=x,
                                                       op0=ALU.add, op1=ALU.add).then_inc(S["res"], 1)
                    else:
                        nc.vector.tensor_tensor(x, bank4[7][:, 0, :], x, ALU.add).then_inc(S["res"], 1)

        block = ctx.enter_context(nc.Block())

        @block.sync
        def _(sp):
            sp.dma_start(cen[:].rearrange("p (b d) -> p b d", b=NB), A["x"].rearrange("b t d -> t b d")).then_inc(ld_x, 16)
            sp.dma_start(dev[:].rearrange("p (b d) -> p b d", b=NB), A["ctx_1024"].rearrange("b t d -> t b d")).then_inc(ld_x, 16)
            sp.dma_start(ident[:], c_ident).then_inc(ld_c, 16)
            for n in range(2):
                sp.dma_start(rot_c[n][:], c_rot[n].rearrange("p (a d) -> p a d", a=4)).then_inc(ld_c, 16)
            sp.dma_start(mask_f[:], c_mask.rearrange("p (a d) -> p a d", a=2)).then_inc(ld_c, 16)
            sp.dma_start(head_m[:], c_head).then_inc(ld_c, 16)
            sp.dma_start(v_mask[:], c_vmask.rearrange("p (h d) -> p h d", h=HU)).then_inc(ld_c, 16)
            col = lambda a: a.rearrange("(p o) -> p o", o=1)
            for i, n in enumerate(("Wq", "Wk", "Wv")):
                sp.dma_start(xw[:, i, :], A["L0_xattn_" + n]).then_inc(ld_xw, 16)
            sp.dma_start(xwo[:], A["L0_xattn_Wo"].rearrange("(a p) n -> p a n", a=2)).then_inc(ld_xw, 16)
            for i, n in enumerate(("bq", "bk", "bo")):
                sp.dma_start(xb[:, i:i + 1], col(A["L0_xattn_" + n])).then_inc(ld_xw, 16)
            for i in range(2):
                sp.dma_start(xbv[:, i:i + 1], col(A["L0_xattn_bv"][i * DH:(i + 1) * DH])).then_inc(ld_xw, 16)

            def load_layer(net, layer, first):
                pre, units = net["pre"], net["units"]
                inner = net["H"] * DH
                n_units = None if first and net["idx"] == 0 else net["base0"] + (0 if first else layer * units)
                n_ff = None if n_units is None else (net["ff0"] + (0 if first else layer)) * 4
                n_rot = None if n_units is None else net["ff0"] + (0 if first else layer)
                if n_units is not None:
                    sp.wait_ge(AT["v"], n_units)
                sp.dma_start(wqkv[:, 0:3 * inner], A[pre + net["Wqkv"]][layer]).then_inc(ld_qkv, 16)
                if n_rot is not None:
                    sp.wait_ge(AT["rot"], n_rot)
                for i, n in enumerate(("q_scale", "k_scale")):
                    sp.dma_start(qks[:, i, :], A[pre + n][layer].rearrange("(o d) -> o d", o=1).to_broadcast([P, DH])
                                 ).then_inc(ld_rot, 16)
                if n_units is not None:
                    sp.wait_ge(AT["y"], n_units)
                sp.dma_start(wo[:, 0:inner // P, :], A[pre + net["Wo"]][layer].rearrange("(j p) n -> p j n", p=P)
                             ).then_inc(ld_wo, 16)
                if n_ff is not None:
                    sp.wait_ge(FF["z"], n_ff)
                ff = [(w1[:], A[pre + net["W1"]][layer])]
                w2_, b1_ = A[pre + net["W2"]][layer], A[pre + "b1"][layer]
                ff.append((w2[:, 0:2, :], w2_[0:256, :].rearrange("(j p) n -> p j n", p=P)))
                ff.append((w2[0:CH[2][1], 2, :], w2_[256:HID, :]))
                for part in range(2):
                    for c, (o, w) in enumerate(CH):
                        ff.append((b1[0:w, 3 * part + c:3 * part + c + 1], col(b1_[part * HID + o:part * HID + o + w])))
                for i, n in enumerate(("ln_g", "ln_b", "b2")):
                    ff.append((lnp[:, i:i + 1], col(A[pre + n][layer])))
                assert len(ff) == 12
                for dst, src in ff:
                    sp.dma_start(dst, src).then_inc(ld_ff, 16)

            net = NETS[0]
            load_layer(net, 0, True)
            names = ["Wq_c", "Wk_s", "Wq_s", "Wk_c", "Wv_s", "Wv_c"]
            for i, n in enumerate(names):
                sp.dma_start(yw_in[:, i, :], A["L1_xattn_" + n]).then_inc(ld_yw, 16)
                sp.dma_start(yb[:, i:i + 1], col(A["L1_xattn_b" + n[1:]])).then_inc(ld_yw, 16)
            sp.dma_start(yw_in[:, 6:8, :], A["L1_xattn_Wg"].rearrange("o (a i) -> o a i", a=2)).then_inc(ld_yw, 16)
            sp.dma_start(yb[:, 6:7], col(A["L1_xattn_bg"])).then_inc(ld_yw, 16)
            with sp.Fori(1, net["depth"]) as layer:
                load_layer(net, layer, False)
            net = NETS[1]
            load_layer(net, 0, True)
            with sp.Fori(1, net["depth"]) as layer:
                load_layer(net, layer, False)
            sp.wait_ge(out_dve, NBLK)
            sp.dma_start(out.rearrange("b t d -> t b d"), cen[:].rearrange("p (b d) -> p b d", b=NB)).then_inc(out_st, 16)
            sp.wait_ge(out_st, 16)

        @block.tensor
        def _(pe):
            pe.wait_ge(ld_x, 32)
            pe.wait_ge(ld_c, 96)
            for src, o in ((cen, 0), (dev, 4)):
                for k in range(NBLK):
                    for j in range(4):
                        b = 4 * k + j
                        mm = nc.tensor.transpose(bank4[o + k][:, j, :], src[:, b * P:(b + 1) * P], ident[:])
                    mm.then_inc(in_ps, 1)

            pe.wait_ge(c_pool, 1)
            pe.wait_ge(in_act, NBLK)
            ln_pe(pe, 0, base_x, lambda e, k: e.wait_ge(in_dve, NBLK))
            pe.wait_ge(ld_xw, 9 * 16)
            for k in range(NBLK):
                pe.wait_ge(LN["xn"], k + 1)
                nc.tensor.matmul(bank[k][:], xw[:, 0, :], z[:, k * BLK:(k + 1) * BLK], start=True, stop=True
                                 ).then_inc(XP["q"], 1)
            for k in range(NBLK):
                nc.tensor.matmul(bank[4 + k][:], xw[:, 1, :], ctx_t[:, k * BLK:(k + 1) * BLK], start=True, stop=True
                                 ).then_inc(XP["k"], 1)
            for k in range(NBLK):
                pe.wait_ge(XP["qe"], k + 1)
                for j in range(4):
                    b = 4 * k + j
                    mm = nc.tensor.matmul(bank4[k][:, j, :], ctx_t[:, b * P:(b + 1) * P], xw[:, 2, :],
                                          start=True, stop=True)
                mm.then_inc(XP["v"], 1)

            def x0_step(st):
                if st.c == 1 and st.r is None:
                    pe.wait_ge(XP["ve"], NBLK)
                    pe.wait_ge(XP["ke"], NBLK)
                pe_probs_t(pe, st, X0, 1)
                pe_values(pe, st, X0, 1)
                if st.has(1):
                    p = st.half(1)[1]
                    st.wait(pe, X0["kp"], 1)
                    st.wait(pe, X0["qp"], 1)
                    for g in range(2):
                        st.wait(pe, X0["ex%d" % g], 2)
                        nc.tensor.matmul(bank[3 + g][:], xq_s[p][:], xk_s[p][:, 4 * g:4 * g + 4, :],
                                         start=True, stop=True).then_inc(X0["s%d" % g], 1)
                pe_project(pe, st, X0, 1)

            run_steps(pe, 32, 0, 3, x0_step)

            def transformer(net):
                ni, units, inner = net["idx"], net["units"], net["H"] * DH

                def steps(base, layer):
                    def step(st):
                        if st.has(2):
                            p = st.half(2)[1]
                            st.wait(pe, AT["mq"], 2)
                            st.wait(pe, AT["pe0"], 5)
                            for j in range(4):
                                mm = nc.tensor.transpose(
                                    bank4[5][:, j, :], rc[0][p][:].rearrange("p h d -> p (h d)")[:, j * P:(j + 1) * P], ident[:])
                            mm.then_inc(AT["qt"], 1)
                            st.wait(pe, AT["mk"], 2)
                            st.wait(pe, AT["pe1"], 5)
                            for j in range(4):
                                mm = nc.tensor.transpose(
                                    bank4[6][:, j, :], rc[1][p][:].rearrange("p h d -> p (h d)")[:, j * P:(j + 1) * P], ident[:])
                            mm.then_inc(AT["kt"], 1)
                        if st.has(0):
                            p = st.parity
                            if st.c == 0 and st.r is None:
                                pe.wait_ge(ld_qkv, (layer + (net["ff0"] + 1)) * 16)
                            st.wait(pe, AT["hs"], 0)
                            o = 512 * p if ni == 0 else 0
                            st.wait(pe, AT["sqq"], 1)
                            nc.tensor.matmul(bank[0][:], hs[p][:], wqkv[:, o:o + 512], start=True, stop=True).then_inc(AT["q"], 1)
                            st.wait(pe, AT["sqk"], 1)
                            nc.tensor.matmul(bank[1][:], hs[p][:], wqkv[:, inner + o:inner + o + 512], start=True, stop=True).then_inc(AT["k"], 1)
                        pe_probs_t(pe, st, AT, 2)
                        if st.has(3):
                            p = st.half(3)[1]
                            o = 2 * inner + (512 * p if ni == 0 else 0)
                            st.wait(pe, AT["hv"], 3)
                            st.wait(pe, AT["ve"], 4)
                            nc.tensor.matmul(bank[2][:], hv[p][:], wqkv[:, o:o + 512], start=True, stop=True).then_inc(AT["v"], 1)
                        pe_values(pe, st, AT, 2)
                        if st.has(2):
                            st.wait(pe, AT["qte"], 2)
                            st.wait(pe, AT["kta"], 2)
                            st.wait(pe, AT["ktb"], 2)
                            for g in range(2):
                                st.wait(pe, AT["ex%d" % g], 3)
                                for j in range(2):
                                    pair = bank[3 + g][:, 256 * j:256 * j + 256]
                                    nc.tensor.matmul(pair, ident_b[:], mask_b[:, ni, 2 * j:2 * j + 2], start=True, stop=False)
                                    mm = nc.tensor.matmul(pair, q_t[:, 2 * g + j, :], k_blk[:, 2 * g + j], start=False, stop=True)
                                mm.then_inc(AT["s%d" % g], 1)
                        if st.c == 4 and st.r is None:
                            pe.wait_ge(ld_wo, (layer + (net["ff0"] + 1)) * 16)
                        pe_project(pe, st, AT, 2, ni)
                    run_steps(pe, units, base, 4, step)

                def feed_forward(layer):
                    f = layer + net["ff0"]
                    ln_pe(pe, layer + net["ln0"], shifted[:].rearrange("p b t -> p (b t)"),
                          lambda e, k: (e.wait_ge(FF["lo"], f * 4 + (k + 1)), e.wait_ge(FF["hi"], f * 4 + (k + 1))))
                    pe.wait_ge(ld_ff, (f + 1) * 192)

                    def down(i):
                        k, c = divmod(i, 3)
                        w = CH[c][1]
                        pe.wait_ge(FF["hid"], f * 12 + (i + 1))
                        mm = nc.tensor.matmul(bank[4 + k][:], w2[0:w, c, :], hid[i % 3][0:w, :], start=(c == 0), stop=(c == 2))
                        if c == 2:
                            mm.then_inc(FF["y"], 1)

                    for i in range(3 * NBLK):
                        k, c = divmod(i, 3)
                        o, w = CH[c]
                        if c == 0:
                            pe.wait_ge(LN["aff"], f * 4 + (k + 1))
                        if i >= 2:
                            pe.wait_ge(FF["hid"], f * 12 + (i - 1))
                        x = cen[:, k * BLK:(k + 1) * BLK]
                        nc.tensor.matmul(bank[2 + i % 2][0:w, :], w1[:, HID + o:HID + o + w], x, start=True, stop=True)
                        nc.tensor.matmul(bank[i % 2][0:w, :], w1[:, o:o + w], x, start=True, stop=True).then_inc(FF["ag"], 1)
                        if i >= 2:
                            down(i - 2)
                    down(3 * NBLK - 2)
                    down(3 * NBLK - 1)

                ln_pe(pe, net["ln0"] - 1, base_x, src_ready[ni])
                with pe.Fori(0, net["depth"]) as layer:
                    steps(layer * units + net["base0"], layer)
                    feed_forward(layer)

            src_ready = [lambda e, k: e.wait_ge(X0["res"], 32), lambda e, k: e.wait_ge(YP["gm"], 3 * NBLK)]
            transformer(NETS[0])

            ln_pe(pe, 8, base_x, lambda e, k: e.wait_ge(FF["outer"], NBLK))
            pe.wait_ge(ld_yw, 14 * 16)
            for g in range(2):
                if g == 0:
                    pe.wait_ge(LN["xn"], 4 * 9)
                for i in range(4 * g, 4 * g + 4):
                    mm = nc.tensor.transpose(bank4[g][:, i % 4, :], yw_in[:, i, :], ident[:])
                mm.then_inc(YP["w"], 1)
            n = 0
            for a in range(4):
                src = z if a in (0, 3) else ctx_t
                for k in range(NBLK):
                    if n == 0:
                        pe.wait_ge(YP["we"], 2)
                    if n >= 6:
                        pe.wait_ge(YP["qke"], n - 5)
                    nc.tensor.matmul(bank[2 + n % 6][:], yw[:, a, :], src[:, k * BLK:(k + 1) * BLK], start=True, stop=True
                                     ).then_inc(YP["qk"], 1)
                    n += 1
            for b2 in range(NB // 2):
                if b2 >= 2:
                    pe.wait_ge(YP["ve"], b2 - 1)
                for j in range(2):
                    b = 2 * b2 + j
                    for a, src in enumerate((ctx_t, z)):
                        mm = nc.tensor.matmul(bank4[b2 % 2][:, 2 * j + a, :], src[:, b * P:(b + 1) * P], yw[:, 4 + a, :],
                                              start=True, stop=True)
                mm.then_inc(YP["v"], 1)
            pe.wait_ge(YP["qke"], 16)
            pe.wait_ge(YP["ve"], 8)
            with pe.Fori(0, NB // 2) as it:
                cnt = it + 1
                pe.wait_ge(YP["qs"], cnt)
                for j in range(2):
                    for a in range(2):
                        ks = y_qk[:, 2 * a + 1, :].rearrange("p (b t) -> p b t", b=NB)[:, it * 2 + j, :]
                        mm = nc.tensor.matmul(bank4[3][:, 2 * j + a, :], yq_s[:, j, a, :], ks, start=True, stop=True)
                mm.then_inc(YP["s"], 1)
                pe.wait_ge(YP["ex"], cnt)
                for i in range(4):
                    mm = nc.tensor.transpose(bank4[4][:, i, :], prob[0][0][:, i, :], ident[:])
                mm.then_inc(YP["pt"], 1)
                pe.wait_ge(YP["pte"], cnt)
                for j in range(2):
                    for a in range(2):
                        mm = nc.tensor.matmul(bank4[5][:, 2 * j + a, :], prob_t[0][:, 2 * j + a, :],
                                              y_v[:, it * 2 + j, a, :], start=True, stop=True)
                mm.then_inc(YP["o"], 1)
                pe.wait_ge(YP["on"], cnt)
                for i in range(4):
                    mm = nc.tensor.transpose(bank4[6][:, i, :], o_tok[:, i * P:(i + 1) * P], ident[:])
                mm.then_inc(YP["ot"], 1)
            pe.wait_ge(YP["ote"], 16)
            for k in range(NBLK):
                for a in range(2):
                    mm = nc.tensor.matmul(bank[k][:], yw[:, 6 + a, :], y_ctx[:, a, k * BLK:(k + 1) * BLK],
                                          start=(a == 0), stop=(a == 1))
                mm.then_inc(YP["g"], 1)

            transformer(NETS[1])

            pe.wait_ge(FF["outer"], 2 * NBLK)
            for k in range(NBLK):
                for j in range(4):
                    b = 4 * k + j
                    mm = nc.tensor.transpose(bank4[k][:, j, :], base_x[:, b * P:(b + 1) * P], ident[:])
                mm.then_inc(out_ps, 1)

        @block.scalar
        def _(act):
            act.wait_ge(ld_c, 96)
            nc.scalar.activation(ident_b[:], ident[:], ACT.Copy).then_inc(c_act, 1)
            for n in range(2):
                nc.scalar.activation(mask_b[:, n], mask_f[:, n, :].unsqueeze(1).to_broadcast([P, 4, P]), ACT.Copy
                                     ).then_inc(c_act, 1)
            for k in range(NBLK):
                act.wait_ge(in_ps, NBLK + k + 1)
                nc.scalar.activation(ctx_t[:, k * BLK:(k + 1) * BLK], bank[4 + k][:], ACT.Copy).then_inc(in_act, 1)
            ln_act(act, 0)
            act.wait_ge(ld_xw, 9 * 16)
            act.wait_ge(XP["bq"], 1)
            for k in range(NBLK):
                act.wait_ge(XP["q"], k + 1)
                nc.scalar.activation(x_q[:, k * BLK:(k + 1) * BLK], bank[k][:], ACT.Identity, bias=xbq[:, 0:1],
                                     scale=float(1 / np.sqrt(XD))).then_inc(XP["qe"], 1)
            for k in range(NBLK):
                act.wait_ge(XP["v"], k + 1)
                nc.scalar.activation(x_v[:, k * BLK:(k + 1) * BLK], bank[k][:], ACT.Copy).then_inc(XP["ve"], 1)

            def x0_step(st):
                act_probs_t(act, st, X0, 1)
                act_exp(act, st, X0, 1, 0)
                act_outputs(act, st, X0, 1)
                act_exp(act, st, X0, 1, 1)

            run_steps(act, 32, 0, 3, x0_step)

            def transformer(net):
                ni, units = net["idx"], net["units"]

                def step(st):
                    act_exp(act, st, AT, 2, 0)
                    if st.has(2):
                        st.wait(act, AT["qt"], 2)
                        st.wait(act, AT["s1"], 3)
                        nc.scalar.activation(q_t[:], bank4[5], ACT.Copy).then_inc(AT["qte"], 1)
                        st.wait(act, AT["kt"], 2)
                        nc.scalar.activation(k_blk[0:DH, :, 0, :], bank4[6][0:DH], ACT.Copy).then_inc(AT["kta"], 1)
                        nc.scalar.activation(k_blk[DH:P, :, 1, :], bank4[6][DH:P], ACT.Copy).then_inc(AT["ktb"], 1)
                    act_probs_t(act, st, AT, 2)
                    if st.has(0):
                        st.wait(act, AT["rq"], 0)
                        st.wait(act, AT["ssq"], 1)
                        nc.scalar.activation(sq[0][:].rearrange("p h d -> p (h d)"), bank[0][:], ACT.Square).then_inc(AT["sqq"], 1)
                        st.wait(act, AT["rk"], 0)
                        st.wait(act, AT["ssk"], 1)
                        nc.scalar.activation(sq[1][:].rearrange("p h d -> p (h d)"), bank[1][:], ACT.Square).then_inc(AT["sqk"], 1)
                    act_exp(act, st, AT, 2, 1)
                    act_outputs(act, st, AT, 2)
                    if st.has(3):
                        st.wait(act, AT["v"], 3)
                        st.wait(act, AT["o"], 5)
                        nc.scalar.activation(v_s[st.half(3)[1]][:].rearrange("p h d -> p (h d)"), bank[2][:],
                                             ACT.Copy).then_inc(AT["ve"], 1)

                ln_act(act, net["ln0"] - 1)
                with act.Fori(0, net["depth"]) as layer:
                    run_steps(act, units, layer * units + net["base0"], 4, step)
                    f = layer + net["ff0"]
                    act.wait_ge(AT["res"], (layer + 1) * units + net["base0"])
                    zb = z[:].rearrange("p (b t) -> p b t", b=NB)
                    for k in range(NBLK):
                        nc.scalar.activation(shifted[DH:P, 4 * k:4 * k + 4, 1:P], zb[DH:P, 4 * k:4 * k + 4, 0:P - 1],
                                             ACT.Copy).then_inc(FF["hi"], 1)
                    ln_act(act, layer + net["ln0"])
                    act.wait_ge(ld_ff, (f + 1) * 192)
                    for i in range(3 * NBLK):
                        w = CH[i % 3][1]
                        act.wait_ge(FF["ag"], f * 12 + (i + 1))
                        if i >= 2:
                            act.wait_ge(FF["hid"], f * 12 + (i - 1))
                        nc.scalar.activation(gl[i % 2][0:w, :], bank[2 + i % 2][0:w, :], ACT.Gelu,
                                             bias=b1[0:w, 3 + i % 3:4 + i % 3]).then_inc(FF["gelu"], 1)

            transformer(NETS[0])

            ln_act(act, 8)
            act.wait_ge(ld_yw, 14 * 16)
            for g in range(2):
                act.wait_ge(YP["w"], g + 1)
                nc.scalar.activation(yw[:, 4 * g:4 * g + 4, :], bank4[g], ACT.Copy).then_inc(YP["we"], 1)
            for n in range(16):
                act.wait_ge(YP["qk"], n + 1)
                nc.scalar.activation(y_qk[:, n // 4, (n % 4) * BLK:(n % 4 + 1) * BLK], bank[2 + n % 6][:], ACT.Identity,
                                     bias=yb[:, n // 4:n // 4 + 1]).then_inc(YP["qke"], 1)
            for b2 in range(NB // 2):
                act.wait_ge(YP["v"], b2 + 1)
                nc.scalar.activation(y_v[:, 2 * b2:2 * b2 + 2].rearrange("p b a n -> p (b a) n"), bank4[b2 % 2], ACT.Copy
                                     ).then_inc(YP["ve"], 1)
            with act.Fori(0, NB // 2) as it:
                cnt = it + 1
                act.wait_ge(YP["sh"], cnt)
                nc.scalar.activation(prob[0][0], prob[0][0], ACT.Exp, scale=float(1 / np.sqrt(P))).then_inc(YP["ex"], 1)
                act.wait_ge(YP["pt"], cnt)
                nc.scalar.activation(prob_t[0][:], bank4[4], ACT.Copy).then_inc(YP["pte"], 1)
                act.wait_ge(YP["ot"], cnt)
                src = bank4[6].rearrange("p (j a) n -> p j a n", j=2)
                for a in range(2):
                    dst = y_ctx[:, a, :].rearrange("p (i n) -> p i n", i=NB // 2)[:, it, :].rearrange("p (j n) -> p j n", j=2)
                    nc.scalar.activation(dst, src[:, :, a, :], ACT.Identity, bias=yb[:, 4 + a:5 + a]).then_inc(YP["ote"], 1)
            for k in range(NBLK):
                act.wait_ge(YP["g"], k + 1)
                nc.scalar.activation(dev[:, k * BLK:(k + 1) * BLK], bank[k][:], ACT.Sigmoid, bias=yb[:, 6:7]
                                     ).then_inc(YP["sg"], 1)
            transformer(NETS[1])

        @block.gpsimd
        def _(pool):
            nc.gpsimd.memset(mean_w[:], 1.0 / P).then_inc(c_pool, 1)
            for i in range(2):
                nc.gpsimd.memset(hs[i][:], 0.0)
                nc.gpsimd.memset(hv[i][:], 0.0)
            nc.gpsimd.memset(k_blk[:], 0.0)
            nc.gpsimd.memset(shifted[:], 0.0)
            pool.wait_ge(ld_c, 96)
            pool.wait_ge(XP["qe"], NBLK)
            pool.wait_ge(XP["ve"], NBLK)

            def x0_step(st):
                if st.has(0):
                    st.wait(pool, X0["s1"], 2)
                if st.has(2):
                    st.wait(pool, X0["o"], 4)
                for g in range(2):
                    pool_divide(pool, st, X0, 1, g)
                if st.has(0):
                    b, p = st.half(0)
                    nc.gpsimd.tensor_copy(xq_s[p][:], x_q.rearrange("p (b t) -> p b t", b=NB)[:, b, :]
                                          ).then_inc(X0["qp"], 1)
                if st.has(2):
                    b, p = st.half(2)
                    nc.gpsimd.tensor_tensor(
                        xv_s[p], x_v.rearrange("p (b t) -> p b t", b=NB)[:, b, DH * p:DH * p + DH].unsqueeze(1)
                        .to_broadcast([P, HU, DH]), v_mask[:], ALU.mult).then_inc(X0["vp"], 1)

            run_steps(pool, 32, 0, 3, x0_step)

            def transformer(net):
                ni, units = net["idx"], net["units"]
                def step(st):
                    if st.has(1):
                        p = st.half(1)[1]
                        st.wait(pool, NT[10], 1)
                        for i, (a, m) in enumerate((("aq", "mq"), ("ak", "mk"))):
                            st.wait(pool, AT[a], 1)
                            nc.gpsimd.tensor_tensor(rc[i][p][:], rc[i][p][:],
                                                    rnorm[p][:, HU * i:HU * i + HU].unsqueeze(2).to_broadcast([P, HU, DH]),
                                                    ALU.mult).then_inc(AT[m], 1)
                    pool_divide(pool, st, AT, 2, 0)
                    if st.has(0):
                        p = st.parity
                        for i, (r_, a) in enumerate((("rq", "aq"), ("rk", "ak"))):
                            st.wait(pool, AT[r_], 0)
                            nc.gpsimd.tensor_tensor(rc[i][p][:], rc[i][p][:], rs[i][p][:], ALU.add).then_inc(AT[a], 1)
                    pool_divide(pool, st, AT, 2, 1)

                with pool.Fori(0, net["depth"]) as layer:
                    run_steps(pool, units, layer * units + net["base0"], 4, step)

            transformer(NETS[0])
            pool.wait_ge(YP["qke"], 16)
            with pool.Fori(0, NB // 2) as it:
                for a in range(2):
                    q = y_qk[:, 2 * a, :].rearrange("p (i n) -> p i n", i=NB // 2)[:, it, :].rearrange("p (j n) -> p j n", j=2)
                    cp = nc.gpsimd.tensor_copy(yq_s[:, :, a, :], q)
                cp.then_inc(YP["qs"], 1)
                pool.wait_ge(YP["s"], it + 1)
            transformer(NETS[1])

        @block.vector
        def _(dve):
            for k in range(NBLK):
                dve.wait_ge(in_ps, k + 1)
                nc.vector.tensor_copy(base_x[:, k * BLK:(k + 1) * BLK], bank[k][:]).then_inc(in_dve, 1)
            dve.wait_ge(in_dve, NBLK)
            dve.wait_ge(in_ps, 2 * NBLK)
            ln_dve(dve, 0, base_x, z, False)
            dve.wait_ge(ld_xw, 9 * 16)
            nc.vector.tensor_scalar(xbq[:], xb[:, 0:1], float(1 / np.sqrt(XD)), None, ALU.mult).then_inc(XP["bq"], 1)
            dve.wait_ge(ld_c, 96)
            for k in range(NBLK):
                dve.wait_ge(XP["k"], k + 1)
                nc.vector.tensor_scalar(x_k[:, k * BLK:(k + 1) * BLK], bank[4 + k][:], xb[:, 1:2], None, ALU.add
                                        ).then_inc(XP["ke"], 1)

            dve.wait_ge(XP["ke"], NBLK)

            def x0_step(st):
                if st.has(0):
                    b, p = st.half(0)
                    st.wait(dve, X0["s1"], 2)
                    nc.vector.tensor_tensor(
                        xk_s[p], x_k.rearrange("p (b t) -> p b t", b=NB)[:, b, :].unsqueeze(1).to_broadcast([P, HU, P]),
                        head_m[:, HU * p:HU * p + HU].unsqueeze(2).to_broadcast([P, HU, P]), ALU.mult
                    ).then_inc(X0["kp"], 1)
                for g in range(2):
                    dve_rinv(dve, st, X0, 1, g)
                for g in range(2):
                    dve_max(dve, st, X0, 1, g)
                dve_residual(dve, st, X0, 1, 3)

            run_steps(dve, 32, 0, 3, x0_step)

            def newton(st, i):
                if not st.has(0):
                    return
                if i > 0:
                    st.wait(dve, NT[i - 1], 0)
                if i == 0:
                    st.wait(dve, AT["ssq"], 0)
                    st.wait(dve, AT["ssk"], 0)
                    ins = nc.vector.tensor_scalar(ssc[:], ss[:], 1e-24, None, ALU.max)
                elif i == 1:
                    ins = nc.vector.tensor_scalar(nt_y[0][:].bitcast(I32), ssc[:].bitcast(I32), -0.5, MAGIC, ALU.mult, ALU.add)
                else:
                    n, part = divmod(i - 2, 3)
                    y = nt_y[n]
                    dst = nt_y[n + 1] if n < 2 else rnorm[st.parity]
                    if part == 0:
                        ins = nc.vector.scalar_tensor_tensor(out=nt_a[:], in0=y[:], scalar=-0.5, in1=y[:],
                                                             op0=ALU.mult, op1=ALU.mult)
                    elif part == 1:
                        ins = nc.vector.tensor_tensor(nt_b[:], nt_a[:], ssc[:], ALU.mult)
                    else:
                        if n == 2:
                            st.wait(dve, AT["mk"], 2)
                        ins = nc.vector.scalar_tensor_tensor(out=dst[:], in0=nt_b[:], scalar=1.5, in1=y[:],
                                                             op0=ALU.add, op1=ALU.mult)
                ins.then_inc(NT[i], 1)

            def rotate(st, i):
                if not st.has(0):
                    return
                p = st.parity
                st.wait(dve, AT["q" if i == 0 else "k"], 0)
                st.wait(dve, AT["qt" if i == 0 else "kt"], 2)
                src = bank[i][:].rearrange("p (h d) -> p h d", h=HU)
                nc.vector.tensor_tensor(rc[i][p][:], src, rot[:, 2 * i, :].unsqueeze(1).to_broadcast([P, HU, DH]), ALU.mult)
                hd = DH // 2
                for a in range(2):
                    dst = rs[i][p][:, :, a * hd:(a + 1) * hd]
                    ins = nc.vector.tensor_tensor(dst, src[:, :, (1 - a) * hd:(2 - a) * hd],
                                                  rot[:, 2 * i + 1, a * hd:(a + 1) * hd].unsqueeze(1).to_broadcast([P, HU, hd]),
                                                  ALU.mult)
                ins.then_inc(AT["rq" if i == 0 else "rk"], 1)

            def sum_squares(st, i):
                if st.has(0):
                    st.wait(dve, AT["sqq" if i == 0 else "sqk"], 0)
                    nc.vector.tensor_reduce(ss[:, HU * i:HU * i + HU], sq[i][:], AX.X, ALU.add
                                            ).then_inc(AT["ssq" if i == 0 else "ssk"], 1)

            def transformer(net):
                ni, units = net["idx"], net["units"]

                zb = z[:].rearrange("p (b t) -> p b t", b=NB)

                def shift(st, lag, dst, sem_, free, free_lag):
                    if not st.has(lag):
                        return
                    b = batch_of(ni, st, lag)
                    p = (st.c - lag) % 2
                    st.wait(dve, free, free_lag)
                    nc.vector.tensor_scalar(dst[p][0:DH, :], zb[0:DH, b, :], 1.0, None, ALU.mult)
                    nc.vector.tensor_scalar(dst[p][DH:P, 1:P], zb[DH:P, b, 0:P - 1], 1.0, None, ALU.mult
                                            ).then_inc(sem_, 1)

                def step(st):
                    if st.c == 0 and st.r is None:
                        shift(st, 0, hs, AT["hs"], AT["k"], 2)
                    dve_rinv(dve, st, AT, 2, 0)
                    rotate(st, 0)
                    rotate(st, 1)
                    sum_squares(st, 0)
                    sum_squares(st, 1)
                    newton(st, 0)
                    newton(st, 1)
                    dve_max(dve, st, AT, 2, 0)
                    newton(st, 2)
                    dve_rinv(dve, st, AT, 2, 1)
                    newton(st, 3)
                    shift(st, -1, hs, AT["hs"], AT["k"], 1)
                    newton(st, 4)
                    dve_max(dve, st, AT, 2, 1)
                    newton(st, 5)
                    newton(st, 6)
                    newton(st, 7)
                    shift(st, 2, hv, AT["hv"], AT["v"], 4)
                    newton(st, 8)
                    newton(st, 9)
                    newton(st, 10)
                    dve_residual(dve, st, AT, 2, 4, ni)

                m0 = net["ln0"] - 1
                ln_dve(dve, m0, base_x, z, False)
                dve.wait_ge(LN["xn"], net["ln0"] * 4)
                with dve.Fori(0, net["depth"]) as layer:
                    f = layer + net["ff0"]
                    base = layer * units + net["base0"]
                    dve.wait_ge(ld_rot, (f + 1) * 32)
                    for i in range(2):
                        nc.vector.tensor_tensor(rot[:, 2 * i, :], rot_c[ni][:, 2 * i, :], qks[:, i, :], ALU.mult)
                        hd = DH // 2
                        for a in range(2):
                            ins = nc.vector.tensor_tensor(rot[:, 2 * i + 1, a * hd:(a + 1) * hd],
                                                          rot_c[ni][:, 2 * i + 1, a * hd:(a + 1) * hd],
                                                          qks[:, i, (1 - a) * hd:(2 - a) * hd], ALU.mult)
                    ins.then_inc(AT["rot"], 1)
                    dve.wait_ge(AT["rot"], f + 1)
                    run_steps(dve, units, base, 4, step)
                    dve.wait_ge(AT["res"], base + units)
                    zb = z[:].rearrange("p (b t) -> p b t", b=NB)
                    for k in range(NBLK):
                        nc.vector.tensor_copy(shifted[0:DH, 4 * k:4 * k + 4, :], zb[0:DH, 4 * k:4 * k + 4, :]
                                              ).then_inc(FF["lo"], 1)
                    dve.wait_ge(FF["lo"], f * 4 + 4)
                    dve.wait_ge(FF["hi"], f * 4 + 4)
                    dve.wait_ge(ld_ff, (f + 1) * 192)
                    ln_dve(dve, layer + net["ln0"], shifted[:].rearrange("p b t -> p (b t)"), cen, True)

                    def close(k):
                        b = slice(k * BLK, (k + 1) * BLK)
                        dve.wait_ge(FF["y"], f * 4 + (k + 1))
                        nc.vector.scalar_tensor_tensor(out=z[:, b], in0=bank[4 + k][:], scalar=lnp[:, 2:3], in1=z[:, b],
                                                       op0=ALU.add, op1=ALU.add).then_inc(FF["z"], 1)

                    for i in range(3 * NBLK):
                        w = CH[i % 3][1]
                        dve.wait_ge(FF["gelu"], f * 12 + (i + 1))
                        nc.vector.scalar_tensor_tensor(out=hid[i % 3][0:w, :], in0=bank[i % 2][0:w, :],
                                                       scalar=b1[0:w, i % 3:i % 3 + 1], in1=gl[i % 2][0:w, :],
                                                       op0=ALU.add, op1=ALU.mult).then_inc(FF["hid"], 1)
                        if i % 3 == 1 and i > 3:
                            close(i // 3 - 1)
                    close(NBLK - 1)
                    dve.wait_ge(FF["z"], f * 4 + 4)
                for k in range(NBLK):
                    b = slice(k * BLK, (k + 1) * BLK)
                    nc.vector.tensor_tensor(base_x[:, b], base_x[:, b], z[:, b], ALU.add).then_inc(FF["outer"], 1)

            dve.wait_ge(X0["res"], 32)
            transformer(NETS[0])
            dve.wait_ge(FF["outer"], NBLK)
            ln_dve(dve, 8, base_x, z, False)
            with dve.Fori(0, NB // 2) as it:
                cnt = it + 1
                dve.wait_ge(YP["s"], cnt)
                nc.vector.tensor_reduce(nmx[:, 0:4], bank4[3], AX.X, ALU.max).then_inc(YP["mx"], 1)
                dve.wait_ge(YP["mx"], cnt)
                nc.vector.tensor_tensor(prob[0][0], bank4[3], nmx[:, 0:4].unsqueeze(2).to_broadcast([P, 4, P]),
                                        ALU.subtract).then_inc(YP["sh"], 1)
                dve.wait_ge(YP["ex"], cnt)
                nc.vector.tensor_reduce(rsum[:, 0:4], prob[0][0], AX.X, ALU.add).then_inc(YP["rs"], 1)
                dve.wait_ge(YP["rs"], cnt)
                nc.vector.reciprocal(rinv[:, 0:4], rsum[:, 0:4]).then_inc(YP["rr"], 1)
                dve.wait_ge(YP["rr"], cnt)
                dve.wait_ge(YP["o"], cnt)
                nc.vector.tensor_tensor(o_tok[:].rearrange("p (i n) -> p i n", i=4), bank4[5],
                                        rinv[:, 0:4].unsqueeze(2).to_broadcast([P, 4, P]), ALU.mult).then_inc(YP["on"], 1)
            dve.wait_ge(YP["ote"], 16)
            for k in range(NBLK):
                b = slice(k * BLK, (k + 1) * BLK)
                nc.vector.tensor_tensor(cen[:, b], y_ctx[:, 0, b], y_ctx[:, 1, b], ALU.subtract).then_inc(YP["gd"], 1)
            for k in range(NBLK):
                b = slice(k * BLK, (k + 1) * BLK)
                dve.wait_ge(YP["gd"], k + 1)
                nc.vector.tensor_tensor(base_x[:, b], base_x[:, b], y_ctx[:, 1, b], ALU.add).then_inc(YP["gm"], 1)
            for k in range(NBLK):
                b = slice(k * BLK, (k + 1) * BLK)
                dve.wait_ge(YP["sg"], k + 1)
                nc.vector.tensor_tensor(cen[:, b], cen[:, b], dev[:, b], ALU.mult).then_inc(YP["gm"], 1)
            for k in range(NBLK):
                b = slice(k * BLK, (k + 1) * BLK)
                dve.wait_ge(YP["gm"], NBLK + k + 1)
                nc.vector.tensor_tensor(base_x[:, b], base_x[:, b], cen[:, b], ALU.add).then_inc(YP["gm"], 1)
            dve.wait_ge(YP["gm"], 3 * NBLK)
            transformer(NETS[1])
            for k in range(NBLK):
                dve.wait_ge(out_ps, k + 1)
                nc.vector.tensor_copy(cen[:, k * BLK:(k + 1) * BLK], bank[k][:]).then_inc(out_dve, 1)


_INS = ["x", "ctx_1024"] + ["L0_xattn_" + n for n in "Wq bq Wk bk Wv bv Wo bo".split()] \
    + ["L0_ffn_" + n for n in "Wqkv q_scale k_scale Wo ln_g ln_b W1 b1 W2 b2".split()] \
    + ["L1_xattn_" + n for n in "Wq_c bq_c Wk_s bk_s Wv_s bv_s Wq_s bq_s Wk_c bk_c Wv_c bv_c Wg bg".split()] \
    + ["L1_ffn_" + n for n in "wqkv q_scale k_scale wo ln_g ln_b w1 b1 w2 b2".split()]


def kernel(**inputs):
    import concourse.bacc as _bacc
    from concourse.bass_utils import run_bass_kernel_spmd as _run

    nc = _bacc.Bacc("TRN2", target_bir_lowering=False, num_devices=1)
    arrays, aps = {}, {}
    for name in _INS:
        a = np.ascontiguousarray(inputs[name])
        arrays[f"in_{name}_dram"] = a
        aps[name] = nc.dram_tensor(f"in_{name}_dram", a.shape, mybir.dt.from_np(a.dtype), kind="ExternalInput").ap()
    out = nc.dram_tensor("out_0_dram", (NB, P, P), F32, kind="ExternalOutput").ap()
    build(nc, aps, out)
    r = _run(nc, [arrays], core_ids=[0])
    return r.results[0]["out_0_dram"]
```

```python
from contextlib import ExitStack

import numpy as np

import concourse.bass as bass
from concourse import mybir

ALU = mybir.AluOpType
ACT = mybir.ActivationFunctionType
F32 = mybir.dt.float32
I32 = mybir.dt.int32
BF16 = mybir.dt.bfloat16
AX = mybir.AxisListType

P = 128
NB = 16
TOK = NB * P
BLK = 512
NBLK = TOK // BLK
HU = 8
DH = 64
XH, XD = 16, 8
HID = int(P * 4 * 2 / 3)
CH = [(0, 128), (128, 128), (256, HID - 256)]
EPS = 1e-5
QK_SCALE = 8.0
MAGIC = float(0x5F3759DF)
MASKED = -1e30
RSQ = 11
UNROLL = 4
PEEL = 6


def rotary_constants(window):
    half = np.arange(0, DH, 2, dtype=np.float32)
    inv_freq = (1.0 / 10000.0 ** (half / DH)).astype(np.float32)
    t = np.arange(P, dtype=np.float32)
    freqs = t[:, None] * inv_freq[None, :]
    base = (half + np.float32(0.4 * DH)) / np.float32(1.4 * DH)
    power = (t - P // 2) / np.float32(window // 2)
    scale = base[None, :] ** power[:, None]
    two = lambda a: np.concatenate([a, a], -1)
    cos, sin, scale = two(np.cos(freqs)), np.sin(freqs), two(scale)
    sin = np.concatenate([-sin, sin], -1)
    return [a.astype(np.float32) for a in (QK_SCALE * cos * scale, QK_SCALE * sin * scale, cos / scale, sin / scale)]


def mask_constant(window):
    i, j = np.arange(P)[:, None], np.arange(P)[None, :]
    return np.where((i < j) | (i > j + window) | (j < (i // window - 1) * window), np.float32(MASKED), np.float32(0))


class Step:

    def __init__(self, units, base, c, r=None):
        self.units, self.base, self.c, self.r = units, base, c, r

    @property
    def parity(self):
        return self.c % 2

    def has(self, lag):
        return self.r is not None or 0 <= self.c - lag < self.units

    def count(self, lag):
        n = self.c + 1 - lag
        if self.r is not None:
            n = self.r * UNROLL + n
        return self.base + n

    def unit(self, lag):
        return self.c - lag if self.r is None else self.r * UNROLL + (self.c - lag)

    def half(self, lag):
        n = self.c - lag
        return (n // 2 if self.r is None else self.r * (UNROLL // 2) + n // 2), n % 2

    def wait(self, eng, sem, lag):
        if self.has(lag):
            eng.wait_ge(sem, self.count(lag))


def run_steps(eng, units, base, last_lag, step, after=None):
    for c in range(PEEL):
        step(Step(units, base, c))
    with eng.Fori(0, (units - PEEL - 2) // UNROLL) as r:
        for c in range(PEEL, PEEL + UNROLL):
            step(Step(units, base, c, r))
    for c in range(units - 2, units + last_lag):
        step(Step(units, base, c))
        if after and c >= units - 1:
            after(c - units)


def build(nc, A, out):
    const = lambda name, a: nc.inline_tensor(np.ascontiguousarray(a), name=name).ap()
    c_ident = const("c_ident", np.eye(P, dtype=np.float32))
    c_rot = [const(f"c_rot{n}", np.concatenate(rotary_constants(w), 1)) for n, w in enumerate((32, 64))]
    c_mask = const("c_mask", np.concatenate([mask_constant(32), mask_constant(64)], 1))
    c_vmask = const("c_vmask", np.tile(np.repeat(np.eye(HU), XD, 1).reshape(1, -1), (P, 1)).astype(np.float32))
    c_head = const("c_head", (np.arange(P)[:, None] // XD == np.arange(XH)[None, :]).astype(np.float32))

    with ExitStack() as ctx:
        sb = lambda name, shape, dt=F32: ctx.enter_context(nc.sbuf_tensor(name, shape, dt))
        sem = lambda name: ctx.enter_context(nc.semaphore(name))
        bank = [ctx.enter_context(nc.psum_tensor(f"bank{i}", [P, BLK], F32)) for i in range(8)]
        bank4 = [b[:].rearrange("p (a n) -> p a n", a=4) for b in bank]

        ident = sb("ident", [P, P])
        ident_b = sb("ident_b", [P, P], BF16)
        mean_w = sb("mean_w", [P, P])
        rot_c = [sb(f"rot_c{n}", [P, 4, DH]) for n in range(2)]
        mask_f = sb("mask_f", [P, 2, P])
        mask_b = sb("mask_b", [P, 2, 4, P], BF16)
        head_m = sb("head_m", [P, XH])
        v_mask = sb("v_mask", [P, HU, HU * XD])
        wqkv = sb("wqkv", [P, 3 * 1024])
        wo = sb("wo", [P, 8, P])
        w1 = sb("w1", [P, 2 * HID])
        w2 = sb("w2", [P, 3, P])
        b1 = sb("b1", [P, 6])
        lnp = sb("lnp", [P, 3])
        qks = sb("qks", [P, 2, DH])
        rot = sb("rot", [P, 4, DH])
        xw = sb("xw", [P, 3, P])
        xwo = sb("xwo", [DH, 2, P])
        xb = sb("xb", [P, 3])
        xbv = sb("xbv", [DH, 2])
        yw_in = sb("yw_in", [P, 8, P])
        yw = sb("yw", [P, 8, P])
        yb = sb("yb", [P, 7])

        base_x = sb("base_x", [P, TOK])
        z = sb("z", [P, TOK])
        ctx_t = sb("ctx_t", [P, TOK])
        shifted = sb("shifted", [P, NB, P])
        cen = sb("cen", [P, TOK])
        shifted_f = shifted[:].rearrange("p b t -> p (b t)")
        dev = sb("dev", [P, TOK])
        big = sb("big", [P, 8 * TOK])
        x_q, x_k, x_v = (big[:, i * TOK:(i + 1) * TOK] for i in range(3))
        xk_s = [big[:, 3 * TOK + i * HU * P:3 * TOK + (i + 1) * HU * P].rearrange("p (h t) -> p h t", h=HU) for i in range(2)]
        xv_s = [big[:, 4 * TOK + i * HU * DH:4 * TOK + (i + 1) * HU * DH].rearrange("p (h t) -> p h t", h=HU) for i in range(2)]
        gl = [big[:, i * BLK:(i + 1) * BLK] for i in range(2)]
        hid = [big[:, i * BLK:(i + 1) * BLK] for i in range(2, 5)]
        y_qk = big[:, 0:4 * TOK].rearrange("p (a n) -> p a n", a=4)
        y_v = big[:, 4 * TOK:6 * TOK].rearrange("p (b a n) -> p b a n", b=NB, a=2)
        y_ctx = big[:, 6 * TOK:8 * TOK].rearrange("p (a n) -> p a n", a=2)

        hs = [sb(f"hs{i}", [P, P]) for i in range(2)]
        hv = [sb(f"hv{i}", [P, P]) for i in range(2)]
        v_s = [sb(f"v_s{i}", [P, HU, DH]) for i in range(2)]
        sq = [sb(f"sq{i}", [P, HU, DH]) for i in range(2)]
        rc = [[sb(f"rc{i}{j}", [P, HU, DH]) for j in range(2)] for i in range(2)]
        rs = [[sb(f"rs{i}{j}", [P, HU, DH]) for j in range(2)] for i in range(2)]
        ss = sb("ss", [P, 2 * HU])
        ssc = sb("ssc", [P, 2 * HU])
        nt_y = [sb(f"nt_y{i}", [P, 2 * HU]) for i in range(3)]
        nt_a = sb("nt_a", [P, 2 * HU])
        nt_b = sb("nt_b", [P, 2 * HU])
        rnorm = [sb(f"rnorm{i}", [P, 2 * HU]) for i in range(2)]
        q_t = sb("q_t", [P, 4, P])
        k_blk = sb("k_blk", [P, 4, 2, P])
        xq_s = [sb(f"xq_s{i}", [P, P]) for i in range(2)]
        nmx2 = [sb(f"nmx{i}", [P, HU]) for i in range(2)]
        nmx = nmx2[0]
        rsum = sb("rsum", [P, HU])
        rinv = sb("rinv", [P, HU])
        xbq = sb("xbq", [P, 1])
        rstd = sb("rstd", [P, NB])
        lt_s = sb("lt_s", [P, NB])
        lt_y = [sb(f"lt_y{i}", [P, NB]) for i in range(3)]
        lt_a = sb("lt_a", [P, NB])
        lt_b = sb("lt_b", [P, NB])
        prob = [[sb(f"prob{g}", [P, 4, P])[:] for g in range(2)],
                [big[:, 6 * TOK + g * BLK:6 * TOK + (g + 1) * BLK].rearrange("p (h t) -> p h t", h=4) for g in range(2)]]
        prob_t = [sb(f"prob_t{g}", [P, 4, P]) for g in range(2)]
        o_tok = sb("o_tok", [P, HU * DH])
        o_t = sb("o_t", [P, 4, P])
        yq_s = sb("yq_s", [P, 2, 2, P])

        ld_c, ld_x, ld_xw, ld_yw = sem("ld_c"), sem("ld_x"), sem("ld_xw"), sem("ld_yw")
        ld_qkv, ld_rot, ld_wo, ld_ff = sem("ld_qkv"), sem("ld_rot"), sem("ld_wo"), sem("ld_ff")
        c_act, c_pool = sem("c_act"), sem("c_pool")
        in_ps, in_dve, in_act = sem("in_ps"), sem("in_dve"), sem("in_act")
        out_ps, out_dve, out_st = sem("out_ps"), sem("out_dve"), sem("out_st")
        LN = {n: sem("ln_" + n) for n in "mean cen sq var varl bc xn aff".split()}
        ln_rsqrt = sem("ln_rsqrt")
        lnl_rsqrt = sem("lnl_rsqrt")
        FF = {n: sem("ff_" + n) for n in "lo hi sq ag gelu hid y z outer".split()}
        XP = {n: sem("xp_" + n) for n in "q k v qe ke ve bq".split()}
        YP = {n: sem("yp_" + n) for n in "w we qk qke v ve g gd gm sg s mx sh ex rs pt pte o rr on ot ote qs".split()}
        COMMON = "s0 s1 mx0 mx1 ex0 ex1 ri0 ri1 pn0 pn1 pt0 pt1 pe0 pe1 o ote y res".split()
        X0 = {n: sem("x0_" + n) for n in COMMON + "kp qp vp".split()}
        AT = {n: sem("at_" + n) for n in COMMON + "hs hv q k v sqq sqk ve rq rk ssq ssk aq ak mq mk qt kt qte kta ktb rot".split()}
        NT = [sem(f"nt{i}") for i in range(11)]

        NETS = [dict(idx=0, H=16, depth=6, units=32, base0=0, ff0=0, ln0=2, pre="L0_ffn_",
                     Wqkv="Wqkv", Wo="Wo", W1="W1", W2="W2"),
                dict(idx=1, H=8, depth=2, units=16, base0=192, ff0=6, ln0=10, pre="L1_ffn_",
                     Wqkv="wqkv", Wo="wo", W1="w1", W2="w2")]

        def batch_of(net_idx, st, lag):
            return st.half(lag)[0] if net_idx == 0 else st.unit(lag)

        def pe_mean(k, o, src):
            nc.tensor.matmul(bank[o][:], mean_w[:], src[:, k * BLK:(k + 1) * BLK], start=True, stop=True
                             ).then_inc(LN["mean"], 1)

        def pe_var(k, o):
            for b in range(4 * k, 4 * k + 4):
                mm = nc.tensor.matmul(bank[o][:, 2 * b:2 * b + 2], dev[:, b * P:(b + 1) * P], mean_w[:, 0:2],
                                      start=True, stop=True)
            return mm

        def pe_broadcast(k, o):
            for j in range(4):
                b = 4 * k + j
                mm = nc.tensor.transpose(bank4[o][:, j, :], rstd[:, b:b + 1].to_broadcast([P, P]), ident[:])
            mm.then_inc(LN["bc"], 1)

        def ln_pe(pe, m, src, ready):
            for k in range(NBLK):
                ready(pe, k)
                pe_mean(k, k, src)
            for k in range(NBLK):
                pe.wait_ge(LN["sq"], m * 4 + (k + 1))
                mm = pe_var(k, 4)
            mm.then_inc(LN["var"], 1)
            pe.wait_ge(ln_rsqrt, (m + 1) * RSQ)
            for k in range(NBLK):
                pe_broadcast(k, 4 + k)

        def act_square(act, m, k, steps=1):
            b = slice(k * BLK, (k + 1) * BLK)
            act.wait_ge(LN["cen"], m * 4 + (k + 1))
            nc.scalar.activation(dev[:, b], cen[:, b], ACT.Square).then_inc(LN["sq"], steps)

        def ln_act(act, m):
            for k in range(NBLK):
                act_square(act, m, k)

        def dve_centre(dve, m, k, o, src):
            b = slice(k * BLK, (k + 1) * BLK)
            dve.wait_ge(LN["mean"], m * 4 + (k + 1))
            nc.vector.tensor_tensor(cen[:, b], src[:, b], bank[o][:], ALU.subtract).then_inc(LN["cen"], 1)

        def rsqrt(dve, i, before, var_sem, T, o, b0, b1_):
            c = slice(b0, b1_)
            if i == 0:
                dve.wait_ge(var_sem, before + 1)
                var = bank[o][:, 2 * b0:2 * b1_].rearrange("p (b a) -> p b a", a=2)[:, :, 0]
                nc.vector.tensor_scalar(lt_s[:, c], var, EPS, None, ALU.add).then_inc(T, 1)
                return
            dve.wait_ge(T, before * RSQ + i)
            if i == 1:
                ins = nc.vector.tensor_scalar(lt_y[0][:, c].bitcast(I32), lt_s[:, c].bitcast(I32), -0.5, MAGIC,
                                              ALU.mult, ALU.add)
            else:
                n, part = divmod(i - 2, 3)
                y = lt_y[n][:, c]
                if part == 0:
                    ins = nc.vector.scalar_tensor_tensor(out=lt_a[:, c], in0=y, scalar=-0.5, in1=y, op0=ALU.mult, op1=ALU.mult)
                elif part == 1:
                    ins = nc.vector.tensor_tensor(lt_b[:, c], lt_a[:, c], lt_s[:, c], ALU.mult)
                else:
                    dst = lt_y[n + 1] if n < 2 else rstd
                    ins = nc.vector.scalar_tensor_tensor(out=dst[:, c], in0=lt_b[:, c], scalar=1.5, in1=y,
                                                         op0=ALU.add, op1=ALU.mult)
            ins.then_inc(T, 1)

        def dve_normalise(dve, m, k, o, dst, affine):
            b = slice(k * BLK, (k + 1) * BLK)
            dve.wait_ge(LN["bc"], m * 4 + (k + 1))
            nc.vector.tensor_tensor(dst[:, b], cen[:, b], bank[o][:], ALU.mult).then_inc(LN["xn"], 1)
            if affine:
                dve.wait_ge(LN["xn"], m * 4 + (k + 1))
                nc.vector.tensor_scalar(dst[:, b], dst[:, b], lnp[:, 0:1], lnp[:, 1:2],
                                        ALU.mult, ALU.add).then_inc(LN["aff"], 1)

        def ln_dve(dve, m, src, dst, affine):
            for k in range(NBLK):
                dve_centre(dve, m, k, k, src)
            for i in range(RSQ):
                rsqrt(dve, i, m, LN["var"], ln_rsqrt, 4, 0, NB)
            for k in range(NBLK):
                dve_normalise(dve, m, k, 4 + k, dst, affine)

        def score_bank(S, p, g):
            return g if S is X0 and p == 0 else 3 + g

        def pe_probs_t(pe, st, S, lc):
            if st.has(lc + 2):
                p = st.half(lc + 2)[1]
                st.wait(pe, S["pn0"], lc + 2)
                if S is AT and st.has(lc):
                    st.wait(pe, S["qte"], lc)
                else:
                    st.wait(pe, S["pe0"], lc + 3)
                for h in range(4):
                    mm = nc.tensor.transpose(bank4[5][:, h, :], prob[p][0][:, h, :], ident[:])
                mm.then_inc(S["pt0"], 1)
                st.wait(pe, S["pn1"], lc + 2)
                if S is AT and st.has(lc):
                    st.wait(pe, S["kta"], lc)
                    st.wait(pe, S["ktb"], lc)
                else:
                    st.wait(pe, S["pe1"], lc + 3)
                for h in range(4):
                    mm = nc.tensor.transpose(bank4[6][:, h, :], prob[p][1][:, h, :], ident[:])
                mm.then_inc(S["pt1"], 1)

        def pe_values(pe, st, S, lc):
            if st.has(lc + 2):
                p = st.half(lc + 2)[1]
                st.wait(pe, S["pe0"], lc + 2)
                if S is AT:
                    st.wait(pe, S["ve"], lc + 2)
                else:
                    st.wait(pe, S["vp"], lc + 2)
                st.wait(pe, S["res"], lc + 3)
                for h in range(HU):
                    if h == 4:
                        st.wait(pe, S["pe1"], lc + 2)
                    pt = prob_t[h // 4][:, h % 4, :]
                    if S is AT:
                        a = DH * (h % 2)
                        mm = nc.tensor.matmul(bank4[7][a:a + DH, h // 2, :], v_s[p][:, h, :], pt, start=True, stop=True)
                    else:
                        mm = nc.tensor.matmul(bank4[7][0:DH, 0, :], xv_s[p][:, h, :], pt,
                                              start=(h == 0), stop=(h == HU - 1))
                mm.then_inc(S["o"], 1)

        def pe_project(pe, st, S, lc, net=0):
            if st.has(lc + 2):
                st.wait(pe, S["ote"], lc + 2)
                p = st.half(lc + 2)[1]
                if S is AT:
                    for j in range(4):
                        mm = nc.tensor.matmul(bank4[7][:, 0, :], wo[:, (4 * p if net == 0 else 0) + j, :],
                                              o_t[:, j, :], start=(j == 0), stop=(j == 3))
                else:
                    mm = nc.tensor.matmul(bank4[7][:, 0, :], xwo[:, p, :], o_t[0:DH, 0, :], start=True, stop=True)
                mm.then_inc(S["y"], 1)

        def act_probs_t(act, st, S, lc):
            if st.has(lc + 2):
                for g in range(2):
                    st.wait(act, S["pt%d" % g], lc + 2)
                    st.wait(act, S["o"], lc + 3)
                    nc.scalar.activation(prob_t[g][:], bank4[5 + g], ACT.Copy).then_inc(S["pe%d" % g], 1)

        def act_outputs(act, st, S, lc):
            if st.has(lc + 2):
                st.wait(act, S["o"], lc + 2)
                st.wait(act, S["y"], lc + 3)
                if S is AT:
                    nc.scalar.activation(o_t[:], bank4[7], ACT.Copy).then_inc(S["ote"], 1)
                else:
                    p = st.half(lc + 2)[1]
                    nc.scalar.activation(o_t[0:DH, 0, :], bank4[7][0:DH, 0, :], ACT.Identity,
                                         bias=xbv[:, p:p + 1]).then_inc(S["ote"], 1)

        def act_exp(act, st, S, lc, g):
            if st.has(lc + 1):
                st.wait(act, S["mx%d" % g], lc + 1)
                p = st.half(lc + 1)[1]
                st.wait(act, S["pt%d" % g], lc + 3)
                st.wait(act, S["ri%d" % g], lc + 2)
                for h in range(4):
                    ins = nc.scalar.activation(prob[p][g][:, h, :], bank4[score_bank(S, p, g)][:, h, :], ACT.Exp,
                                               bias=nmx2[p][:, 4 * g + h:4 * g + h + 1],
                                               accum_out=rsum[:, 4 * g + h:4 * g + h + 1])
                ins.then_inc(S["ex%d" % g], 1)

        def dve_max(dve, st, S, lc, g):
            if st.has(lc):
                st.wait(dve, S["s%d" % g], lc)
                p = st.half(lc)[1]
                nc.vector.tensor_reduce(nmx2[p][:, 4 * g:4 * g + 4], bank4[score_bank(S, p, g)], AX.X, ALU.max, negate=True
                                        ).then_inc(S["mx%d" % g], 1)

        def dve_rinv(dve, st, S, lc, g):
            if st.has(lc + 1):
                st.wait(dve, S["ex%d" % g], lc + 1)
                st.wait(dve, S["pn%d" % g], lc + 2)
                nc.vector.reciprocal(rinv[:, 4 * g:4 * g + 4], rsum[:, 4 * g:4 * g + 4]).then_inc(S["ri%d" % g], 1)

        def pool_divide(pool, st, S, lc, g):
            if st.has(lc + 1):
                st.wait(pool, S["ri%d" % g], lc + 1)
                p = st.half(lc + 1)[1]
                nc.gpsimd.tensor_tensor(prob[p][g], prob[p][g],
                                        rinv[:, 4 * g:4 * g + 4].unsqueeze(2).to_broadcast([P, 4, P]),
                                        ALU.mult).then_inc(S["pn%d" % g], 1)

        def dve_residual(dve, st, S, lc, lag, net=0):
            if st.has(lag):
                st.wait(dve, S["y"], lag)
                st.wait(dve, S["res"], lag + 1)
                half = st.half(lag)
                b = batch_of(net, st, lag)
                if S is AT:
                    x = z[:].rearrange("p (b t) -> p b t", b=NB)[:, b, :]
                    nc.vector.tensor_tensor(x, bank4[7][:, 0, :], x, ALU.add).then_inc(S["res"], 1)
                else:
                    x = base_x[:].rearrange("p (b t) -> p b t", b=NB)[:, half[0], :]
                    if half[1] == 0:
                        nc.vector.scalar_tensor_tensor(out=x, in0=bank4[7][:, 0, :], scalar=xb[:, 2:3], in1=x,
                                                       op0=ALU.add, op1=ALU.add).then_inc(S["res"], 1)
                    else:
                        nc.vector.tensor_tensor(x, bank4[7][:, 0, :], x, ALU.add).then_inc(S["res"], 1)

        block = ctx.enter_context(nc.Block())

        @block.sync
        def _(sp):
            sp.dma_start(cen[:].rearrange("p (b d) -> p b d", b=NB), A["x"].rearrange("b t d -> t b d")).then_inc(ld_x, 16)
            sp.dma_start(dev[:].rearrange("p (b d) -> p b d", b=NB), A["ctx_1024"].rearrange("b t d -> t b d")).then_inc(ld_x, 16)
            sp.dma_start(ident[:], c_ident).then_inc(ld_c, 16)
            for n in range(2):
                sp.dma_start(rot_c[n][:], c_rot[n].rearrange("p (a d) -> p a d", a=4)).then_inc(ld_c, 16)
            sp.dma_start(mask_f[:], c_mask.rearrange("p (a d) -> p a d", a=2)).then_inc(ld_c, 16)
            sp.dma_start(head_m[:], c_head).then_inc(ld_c, 16)
            sp.dma_start(v_mask[:], c_vmask.rearrange("p (h d) -> p h d", h=HU)).then_inc(ld_c, 16)
            col = lambda a: a.rearrange("(p o) -> p o", o=1)
            for i, n in enumerate(("Wq", "Wk", "Wv")):
                sp.dma_start(xw[:, i, :], A["L0_xattn_" + n]).then_inc(ld_xw, 16)
            sp.dma_start(xwo[:], A["L0_xattn_Wo"].rearrange("(a p) n -> p a n", a=2)).then_inc(ld_xw, 16)
            for i, n in enumerate(("bq", "bk", "bo")):
                sp.dma_start(xb[:, i:i + 1], col(A["L0_xattn_" + n])).then_inc(ld_xw, 16)
            for i in range(2):
                sp.dma_start(xbv[:, i:i + 1], col(A["L0_xattn_bv"][i * DH:(i + 1) * DH])).then_inc(ld_xw, 16)

            def load_layer(net, layer, first):
                pre, units = net["pre"], net["units"]
                inner = net["H"] * DH
                n_units = None if first and net["idx"] == 0 else net["base0"] + (0 if first else layer * units)
                n_ff = None if n_units is None else (net["ff0"] + (0 if first else layer)) * 4
                n_rot = None if n_units is None else net["ff0"] + (0 if first else layer)
                if n_units is not None:
                    sp.wait_ge(AT["v"], n_units)
                sp.dma_start(wqkv[:, 0:3 * inner], A[pre + net["Wqkv"]][layer]).then_inc(ld_qkv, 16)
                if n_rot is not None:
                    sp.wait_ge(AT["rot"], n_rot)
                for i, n in enumerate(("q_scale", "k_scale")):
                    sp.dma_start(qks[:, i, :], A[pre + n][layer].rearrange("(o d) -> o d", o=1).to_broadcast([P, DH])
                                 ).then_inc(ld_rot, 16)
                if n_units is not None:
                    sp.wait_ge(AT["y"], n_units)
                sp.dma_start(wo[:, 0:inner // P, :], A[pre + net["Wo"]][layer].rearrange("(j p) n -> p j n", p=P)
                             ).then_inc(ld_wo, 16)
                if n_ff is not None:
                    sp.wait_ge(FF["z"], n_ff)
                ff = [(w1[:], A[pre + net["W1"]][layer])]
                w2_, b1_ = A[pre + net["W2"]][layer], A[pre + "b1"][layer]
                ff.append((w2[:, 0:2, :], w2_[0:256, :].rearrange("(j p) n -> p j n", p=P)))
                ff.append((w2[0:CH[2][1], 2, :], w2_[256:HID, :]))
                for part in range(2):
                    for c, (o, w) in enumerate(CH):
                        ff.append((b1[0:w, 3 * part + c:3 * part + c + 1], col(b1_[part * HID + o:part * HID + o + w])))
                for i, n in enumerate(("ln_g", "ln_b", "b2")):
                    ff.append((lnp[:, i:i + 1], col(A[pre + n][layer])))
                assert len(ff) == 12
                for dst, src in ff:
                    sp.dma_start(dst, src).then_inc(ld_ff, 16)

            net = NETS[0]
            load_layer(net, 0, True)
            names = ["Wq_c", "Wk_s", "Wq_s", "Wk_c", "Wv_s", "Wv_c"]
            for i, n in enumerate(names):
                sp.dma_start(yw_in[:, i, :], A["L1_xattn_" + n]).then_inc(ld_yw, 16)
                sp.dma_start(yb[:, i:i + 1], col(A["L1_xattn_b" + n[1:]])).then_inc(ld_yw, 16)
            sp.dma_start(yw_in[:, 6:8, :], A["L1_xattn_Wg"].rearrange("o (a i) -> o a i", a=2)).then_inc(ld_yw, 16)
            sp.dma_start(yb[:, 6:7], col(A["L1_xattn_bg"])).then_inc(ld_yw, 16)
            with sp.Fori(1, net["depth"]) as layer:
                load_layer(net, layer, False)
            net = NETS[1]
            load_layer(net, 0, True)
            with sp.Fori(1, net["depth"]) as layer:
                load_layer(net, layer, False)
            sp.wait_ge(out_dve, NBLK)
            sp.dma_start(out.rearrange("b t d -> t b d"), cen[:].rearrange("p (b d) -> p b d", b=NB)).then_inc(out_st, 16)
            sp.wait_ge(out_st, 16)

        @block.tensor
        def _(pe):
            pe.wait_ge(ld_x, 32)
            pe.wait_ge(ld_c, 96)
            for src, o in ((cen, 0), (dev, 4)):
                for k in range(NBLK):
                    for j in range(4):
                        b = 4 * k + j
                        mm = nc.tensor.transpose(bank4[o + k][:, j, :], src[:, b * P:(b + 1) * P], ident[:])
                    mm.then_inc(in_ps, 1)

            pe.wait_ge(c_pool, 1)
            pe.wait_ge(c_act, 3)
            pe.wait_ge(in_act, NBLK)
            ln_pe(pe, 0, base_x, lambda e, k: e.wait_ge(in_dve, NBLK))
            pe.wait_ge(ld_xw, 9 * 16)
            for k in range(NBLK):
                pe.wait_ge(LN["xn"], k + 1)
                nc.tensor.matmul(bank[k][:], xw[:, 0, :], z[:, k * BLK:(k + 1) * BLK], start=True, stop=True
                                 ).then_inc(XP["q"], 1)
            for k in range(NBLK):
                nc.tensor.matmul(bank[4 + k][:], xw[:, 1, :], ctx_t[:, k * BLK:(k + 1) * BLK], start=True, stop=True
                                 ).then_inc(XP["k"], 1)
            for k in range(NBLK):
                pe.wait_ge(XP["qe"], k + 1)
                for j in range(4):
                    b = 4 * k + j
                    mm = nc.tensor.matmul(bank4[k][:, j, :], ctx_t[:, b * P:(b + 1) * P], xw[:, 2, :],
                                          start=True, stop=True)
                mm.then_inc(XP["v"], 1)

            def x0_step(st):
                if st.c == 1 and st.r is None:
                    pe.wait_ge(XP["ve"], NBLK)
                    pe.wait_ge(XP["ke"], NBLK)
                pe_probs_t(pe, st, X0, 1)
                if st.has(1):
                    p = st.half(1)[1]
                    st.wait(pe, X0["kp"], 1)
                    st.wait(pe, X0["qp"], 1)
                    for g in range(2):
                        st.wait(pe, X0["ex%d" % g], 3)
                        nc.tensor.matmul(bank[score_bank(X0, p, g)][:], xq_s[p][:], xk_s[p][:, 4 * g:4 * g + 4, :],
                                         start=True, stop=True).then_inc(X0["s%d" % g], 1)
                pe_values(pe, st, X0, 1)
                pe_project(pe, st, X0, 1)

            run_steps(pe, 32, 0, 3, x0_step)

            def transformer(net):
                ni, units, inner = net["idx"], net["units"], net["H"] * DH

                def steps(base, layer):
                    def step(st):
                        if st.has(2):
                            p = st.half(2)[1]
                            st.wait(pe, AT["mq"], 2)
                            st.wait(pe, AT["pe0"], 5)
                            for j in range(4):
                                mm = nc.tensor.transpose(
                                    bank4[5][:, j, :], rc[0][p][:].rearrange("p h d -> p (h d)")[:, j * P:(j + 1) * P], ident[:])
                            mm.then_inc(AT["qt"], 1)
                            st.wait(pe, AT["mk"], 2)
                            st.wait(pe, AT["pe1"], 5)
                            for j in range(4):
                                mm = nc.tensor.transpose(
                                    bank4[6][:, j, :], rc[1][p][:].rearrange("p h d -> p (h d)")[:, j * P:(j + 1) * P], ident[:])
                            mm.then_inc(AT["kt"], 1)
                        if st.has(0):
                            p = st.parity
                            if st.c == 0 and st.r is None:
                                pe.wait_ge(ld_qkv, (layer + (net["ff0"] + 1)) * 16)
                            st.wait(pe, AT["hs"], 0)
                            o = 512 * p if ni == 0 else 0
                            st.wait(pe, AT["sqq"], 1)
                            nc.tensor.matmul(bank[0][:], hs[p][:], wqkv[:, o:o + 512], start=True, stop=True).then_inc(AT["q"], 1)
                            st.wait(pe, AT["sqk"], 1)
                            nc.tensor.matmul(bank[1][:], hs[p][:], wqkv[:, inner + o:inner + o + 512], start=True, stop=True).then_inc(AT["k"], 1)
                        pe_probs_t(pe, st, AT, 2)
                        if st.has(3):
                            p = st.half(3)[1]
                            o = 2 * inner + (512 * p if ni == 0 else 0)
                            st.wait(pe, AT["hv"], 3)
                            st.wait(pe, AT["ve"], 4)
                            nc.tensor.matmul(bank[2][:], hv[p][:], wqkv[:, o:o + 512], start=True, stop=True).then_inc(AT["v"], 1)
                        pe_values(pe, st, AT, 2)
                        if st.has(2):
                            st.wait(pe, AT["qte"], 2)
                            st.wait(pe, AT["kta"], 2)
                            st.wait(pe, AT["ktb"], 2)
                            for g in range(2):
                                st.wait(pe, AT["ex%d" % g], 3)
                                for j in range(2):
                                    pair = bank[3 + g][:, 256 * j:256 * j + 256]
                                    nc.tensor.matmul(pair, ident_b[:], mask_b[:, ni, 2 * j:2 * j + 2], start=True, stop=False)
                                    mm = nc.tensor.matmul(pair, q_t[:, 2 * g + j, :], k_blk[:, 2 * g + j], start=False, stop=True)
                                mm.then_inc(AT["s%d" % g], 1)
                        if st.c == 4 and st.r is None:
                            pe.wait_ge(ld_wo, (layer + (net["ff0"] + 1)) * 16)
                        pe_project(pe, st, AT, 2, ni)
                    f, m = layer + net["ff0"], layer + net["ln0"]

                    def after(n):
                        if n == 0:
                            for k in range(3):
                                pe.wait_ge(FF["lo"], f * 4 + (k + 1))
                                pe.wait_ge(FF["hi"], f * 4 + (k + 1))
                                if k == 2:
                                    pe.wait_ge(LN["cen"], m * 4 + 1)
                                pe_mean(k, k % 2, shifted_f)
                        if n == 1:
                            for k in range(3):
                                pe.wait_ge(FF["sq"], f * 3 + max(2, k + 1))
                                mm = pe_var(k, 1)
                            mm.then_inc(LN["var"], 1)
                        if n == 2:
                            pe.wait_ge(ln_rsqrt, (m + 1) * RSQ)
                            for k in range(3):
                                if k == 2:
                                    pe.wait_ge(LN["xn"], m * 4 + 1)
                                pe_broadcast(k, k % 2)

                    run_steps(pe, units, base, 4, step, after)

                def feed_forward(layer):
                    f, m = layer + net["ff0"], layer + net["ln0"]
                    pe.wait_ge(ld_ff, (f + 1) * 192)

                    def down(i):
                        k, c = divmod(i, 3)
                        w = CH[c][1]
                        pe.wait_ge(FF["hid"], f * 12 + (i + 1))
                        mm = nc.tensor.matmul(bank[4 + k][:], w2[0:w, c, :], hid[i % 3][0:w, :], start=(c == 0), stop=(c == 2))
                        if c == 2:
                            mm.then_inc(FF["y"], 1)

                    for i in range(3 * NBLK):
                        k, c = divmod(i, 3)
                        o, w = CH[c]
                        if c == 0:
                            pe.wait_ge(LN["aff"], f * 4 + max(3, k + 1))
                        if i >= 2:
                            pe.wait_ge(FF["hid"], f * 12 + (i - 1))
                        x = cen[:, k * BLK:(k + 1) * BLK]
                        nc.tensor.matmul(bank[2 + i % 2][0:w, :], w1[:, HID + o:HID + o + w], x, start=True, stop=True)
                        nc.tensor.matmul(bank[i % 2][0:w, :], w1[:, o:o + w], x, start=True, stop=True).then_inc(FF["ag"], 1)
                        if i >= 2:
                            down(i - 2)
                        if i == 0:
                            pe.wait_ge(FF["lo"], f * 4 + 4)
                            pe.wait_ge(FF["hi"], f * 4 + 4)
                            pe_mean(3, 7, shifted_f)
                        if i == 2:
                            pe.wait_ge(LN["sq"], m * 4 + 4)
                            pe_var(3, 7).then_inc(LN["varl"], 1)
                        if i == 6:
                            pe.wait_ge(lnl_rsqrt, (f + 1) * RSQ)
                            pe_broadcast(3, 7)
                    down(3 * NBLK - 2)
                    down(3 * NBLK - 1)

                ln_pe(pe, net["ln0"] - 1, base_x, src_ready[ni])
                with pe.Fori(0, net["depth"]) as layer:
                    steps(layer * units + net["base0"], layer)
                    feed_forward(layer)

            src_ready = [lambda e, k: e.wait_ge(X0["res"], 32), lambda e, k: e.wait_ge(YP["gm"], 3 * NBLK)]
            transformer(NETS[0])

            ln_pe(pe, 8, base_x, lambda e, k: e.wait_ge(FF["outer"], NBLK))
            pe.wait_ge(ld_yw, 14 * 16)
            for g in range(2):
                if g == 0:
                    pe.wait_ge(LN["xn"], 4 * 9)
                for i in range(4 * g, 4 * g + 4):
                    mm = nc.tensor.transpose(bank4[g][:, i % 4, :], yw_in[:, i, :], ident[:])
                mm.then_inc(YP["w"], 1)
            n = 0
            for a in range(4):
                src = z if a in (0, 3) else ctx_t
                for k in range(NBLK):
                    if n == 0:
                        pe.wait_ge(YP["we"], 2)
                    if n >= 6:
                        pe.wait_ge(YP["qke"], n - 5)
                    nc.tensor.matmul(bank[2 + n % 6][:], yw[:, a, :], src[:, k * BLK:(k + 1) * BLK], start=True, stop=True
                                     ).then_inc(YP["qk"], 1)
                    n += 1
            for b2 in range(NB // 2):
                if b2 >= 2:
                    pe.wait_ge(YP["ve"], b2 - 1)
                for j in range(2):
                    b = 2 * b2 + j
                    for a, src in enumerate((ctx_t, z)):
                        mm = nc.tensor.matmul(bank4[b2 % 2][:, 2 * j + a, :], src[:, b * P:(b + 1) * P], yw[:, 4 + a, :],
                                              start=True, stop=True)
                mm.then_inc(YP["v"], 1)
            pe.wait_ge(YP["qke"], 16)
            pe.wait_ge(YP["ve"], 8)

            def y_scores(it):
                pe.wait_ge(YP["qs"], it + 1)
                for j in range(2):
                    for a in range(2):
                        ks = y_qk[:, 2 * a + 1, :].rearrange("p (b t) -> p b t", b=NB)[:, it * 2 + j, :]
                        mm = nc.tensor.matmul(bank4[3][:, 2 * j + a, :], yq_s[:, j, a, :], ks, start=True, stop=True)
                mm.then_inc(YP["s"], 1)

            def y_rest(it, scores_next):
                cnt = it + 1
                pe.wait_ge(YP["ex"], cnt)
                for i in range(4):
                    mm = nc.tensor.transpose(bank4[4][:, i, :], prob[0][0][:, i, :], ident[:])
                mm.then_inc(YP["pt"], 1)
                if scores_next:
                    y_scores(it + 1)
                pe.wait_ge(YP["pte"], cnt)
                for j in range(2):
                    for a in range(2):
                        mm = nc.tensor.matmul(bank4[5][:, 2 * j + a, :], prob_t[0][:, 2 * j + a, :],
                                              y_v[:, it * 2 + j, a, :], start=True, stop=True)
                mm.then_inc(YP["o"], 1)
                pe.wait_ge(YP["on"], cnt)
                for i in range(4):
                    mm = nc.tensor.transpose(bank4[6][:, i, :], o_tok[:, i * P:(i + 1) * P], ident[:])
                mm.then_inc(YP["ot"], 1)

            y_scores(0)
            with pe.Fori(0, NB // 2 - 1) as it:
                y_rest(it, True)
            y_rest(NB // 2 - 1, False)
            pe.wait_ge(YP["ote"], 16)
            for k in range(NBLK):
                for a in range(2):
                    mm = nc.tensor.matmul(bank[k][:], yw[:, 6 + a, :], y_ctx[:, a, k * BLK:(k + 1) * BLK],
                                          start=(a == 0), stop=(a == 1))
                mm.then_inc(YP["g"], 1)

            transformer(NETS[1])

            pe.wait_ge(FF["outer"], 2 * NBLK)
            for k in range(NBLK):
                for j in range(4):
                    b = 4 * k + j
                    mm = nc.tensor.transpose(bank4[k][:, j, :], base_x[:, b * P:(b + 1) * P], ident[:])
                mm.then_inc(out_ps, 1)

        @block.scalar
        def _(act):
            act.wait_ge(ld_c, 96)
            nc.scalar.activation(ident_b[:], ident[:], ACT.Copy).then_inc(c_act, 1)
            for n in range(2):
                nc.scalar.activation(mask_b[:, n], mask_f[:, n, :].unsqueeze(1).to_broadcast([P, 4, P]), ACT.Copy
                                     ).then_inc(c_act, 1)
            for k in range(NBLK):
                act.wait_ge(in_ps, NBLK + k + 1)
                nc.scalar.activation(ctx_t[:, k * BLK:(k + 1) * BLK], bank[4 + k][:], ACT.Copy).then_inc(in_act, 1)
            ln_act(act, 0)
            act.wait_ge(ld_xw, 9 * 16)
            act.wait_ge(XP["bq"], 1)
            for k in range(NBLK):
                act.wait_ge(XP["q"], k + 1)
                nc.scalar.activation(x_q[:, k * BLK:(k + 1) * BLK], bank[k][:], ACT.Identity, bias=xbq[:, 0:1],
                                     scale=float(1 / np.sqrt(XD))).then_inc(XP["qe"], 1)
            for k in range(NBLK):
                act.wait_ge(XP["v"], k + 1)
                nc.scalar.activation(x_v[:, k * BLK:(k + 1) * BLK], bank[k][:], ACT.Copy).then_inc(XP["ve"], 1)

            def x0_step(st):
                act_exp(act, st, X0, 1, 0)
                act_probs_t(act, st, X0, 1)
                act_exp(act, st, X0, 1, 1)
                act_outputs(act, st, X0, 1)

            run_steps(act, 32, 0, 3, x0_step)

            def transformer(net):
                ni, units = net["idx"], net["units"]

                def step(st):
                    act_exp(act, st, AT, 2, 0)
                    if st.has(2):
                        st.wait(act, AT["qt"], 2)
                        st.wait(act, AT["s1"], 3)
                        nc.scalar.activation(q_t[:], bank4[5], ACT.Copy).then_inc(AT["qte"], 1)
                        st.wait(act, AT["kt"], 2)
                        nc.scalar.activation(k_blk[0:DH, :, 0, :], bank4[6][0:DH], ACT.Copy).then_inc(AT["kta"], 1)
                        nc.scalar.activation(k_blk[DH:P, :, 1, :], bank4[6][DH:P], ACT.Copy).then_inc(AT["ktb"], 1)
                    act_probs_t(act, st, AT, 2)
                    if st.has(0):
                        st.wait(act, AT["rq"], 0)
                        st.wait(act, AT["ssq"], 1)
                        nc.scalar.activation(sq[0][:].rearrange("p h d -> p (h d)"), bank[0][:], ACT.Square).then_inc(AT["sqq"], 1)
                        st.wait(act, AT["rk"], 0)
                        st.wait(act, AT["ssk"], 1)
                        nc.scalar.activation(sq[1][:].rearrange("p h d -> p (h d)"), bank[1][:], ACT.Square).then_inc(AT["sqk"], 1)
                    act_exp(act, st, AT, 2, 1)
                    act_outputs(act, st, AT, 2)
                    if st.has(3):
                        st.wait(act, AT["v"], 3)
                        st.wait(act, AT["o"], 5)
                        nc.scalar.activation(v_s[st.half(3)[1]][:].rearrange("p h d -> p (h d)"), bank[2][:],
                                             ACT.Copy).then_inc(AT["ve"], 1)

                ln_act(act, net["ln0"] - 1)
                with act.Fori(0, net["depth"]) as layer:
                    f, m = layer + net["ff0"], layer + net["ln0"]
                    base = layer * units + net["base0"]
                    zb = z[:].rearrange("p (b t) -> p b t", b=NB)

                    def shift_up(k):
                        nc.scalar.activation(shifted[DH:P, 4 * k:4 * k + 4, 1:P], zb[DH:P, 4 * k:4 * k + 4, 0:P - 1],
                                             ACT.Copy).then_inc(FF["hi"], 1)

                    def after(n):
                        if n == -1:
                            act.wait_ge(AT["res"], base + 3 * units // 4)
                            for k in range(3):
                                shift_up(k)

                    run_steps(act, units, base, 4, step, after)
                    act.wait_ge(AT["res"], base + units)
                    shift_up(3)
                    act.wait_ge(ld_ff, (f + 1) * 192)
                    for i in range(3 * NBLK):
                        w = CH[i % 3][1]
                        act.wait_ge(FF["ag"], f * 12 + (i + 1))
                        if i >= 2:
                            act.wait_ge(FF["hid"], f * 12 + (i - 1))
                        nc.scalar.activation(gl[i % 2][0:w, :], bank[2 + i % 2][0:w, :], ACT.Gelu,
                                             bias=b1[0:w, 3 + i % 3:4 + i % 3]).then_inc(FF["gelu"], 1)
                        if i == 0:
                            act_square(act, m, 3, 4)

            transformer(NETS[0])

            ln_act(act, 8)
            act.wait_ge(ld_yw, 14 * 16)
            for g in range(2):
                act.wait_ge(YP["w"], g + 1)
                nc.scalar.activation(yw[:, 4 * g:4 * g + 4, :], bank4[g], ACT.Copy).then_inc(YP["we"], 1)
            for n in range(16):
                act.wait_ge(YP["qk"], n + 1)
                nc.scalar.activation(y_qk[:, n // 4, (n % 4) * BLK:(n % 4 + 1) * BLK], bank[2 + n % 6][:], ACT.Identity,
                                     bias=yb[:, n // 4:n // 4 + 1]).then_inc(YP["qke"], 1)
            for b2 in range(NB // 2):
                act.wait_ge(YP["v"], b2 + 1)
                nc.scalar.activation(y_v[:, 2 * b2:2 * b2 + 2].rearrange("p b a n -> p (b a) n"), bank4[b2 % 2], ACT.Copy
                                     ).then_inc(YP["ve"], 1)
            with act.Fori(0, NB // 2) as it:
                cnt = it + 1
                act.wait_ge(YP["sh"], cnt)
                nc.scalar.activation(prob[0][0], prob[0][0], ACT.Exp, scale=float(1 / np.sqrt(P))).then_inc(YP["ex"], 1)
                act.wait_ge(YP["pt"], cnt)
                nc.scalar.activation(prob_t[0][:], bank4[4], ACT.Copy).then_inc(YP["pte"], 1)
                act.wait_ge(YP["ot"], cnt)
                src = bank4[6].rearrange("p (j a) n -> p j a n", j=2)
                for a in range(2):
                    dst = y_ctx[:, a, :].rearrange("p (i n) -> p i n", i=NB // 2)[:, it, :].rearrange("p (j n) -> p j n", j=2)
                    nc.scalar.activation(dst, src[:, :, a, :], ACT.Identity, bias=yb[:, 4 + a:5 + a]).then_inc(YP["ote"], 1)
            for k in range(NBLK):
                act.wait_ge(YP["g"], k + 1)
                nc.scalar.activation(dev[:, k * BLK:(k + 1) * BLK], bank[k][:], ACT.Sigmoid, bias=yb[:, 6:7]
                                     ).then_inc(YP["sg"], 1)
            transformer(NETS[1])

        @block.gpsimd
        def _(pool):
            nc.gpsimd.memset(mean_w[:], 1.0 / P).then_inc(c_pool, 1)
            for i in range(2):
                nc.gpsimd.memset(hs[i][:], 0.0)
                nc.gpsimd.memset(hv[i][:], 0.0)
            nc.gpsimd.memset(k_blk[:], 0.0)
            nc.gpsimd.memset(shifted[:], 0.0)
            pool.wait_ge(ld_c, 96)
            pool.wait_ge(XP["qe"], NBLK)
            pool.wait_ge(XP["ve"], NBLK)

            def x0_step(st):
                if st.has(0):
                    st.wait(pool, X0["s1"], 2)
                if st.has(2):
                    st.wait(pool, X0["o"], 4)
                pool_divide(pool, st, X0, 1, 0)
                if st.has(0):
                    b, p = st.half(0)
                    nc.gpsimd.tensor_copy(xq_s[p][:], x_q.rearrange("p (b t) -> p b t", b=NB)[:, b, :]
                                          ).then_inc(X0["qp"], 1)
                if st.has(2):
                    b, p = st.half(2)
                    nc.gpsimd.tensor_tensor(
                        xv_s[p], x_v.rearrange("p (b t) -> p b t", b=NB)[:, b, DH * p:DH * p + DH].unsqueeze(1)
                        .to_broadcast([P, HU, DH]), v_mask[:], ALU.mult).then_inc(X0["vp"], 1)
                pool_divide(pool, st, X0, 1, 1)

            run_steps(pool, 32, 0, 3, x0_step)

            def transformer(net):
                ni, units = net["idx"], net["units"]
                def step(st):
                    if st.has(1):
                        p = st.half(1)[1]
                        st.wait(pool, NT[10], 1)
                        for i, (a, m) in enumerate((("aq", "mq"), ("ak", "mk"))):
                            st.wait(pool, AT[a], 1)
                            nc.gpsimd.tensor_tensor(rc[i][p][:], rc[i][p][:],
                                                    rnorm[p][:, HU * i:HU * i + HU].unsqueeze(2).to_broadcast([P, HU, DH]),
                                                    ALU.mult).then_inc(AT[m], 1)
                    pool_divide(pool, st, AT, 2, 0)
                    if st.has(0):
                        p = st.parity
                        for i, (r_, a) in enumerate((("rq", "aq"), ("rk", "ak"))):
                            st.wait(pool, AT[r_], 0)
                            nc.gpsimd.tensor_tensor(rc[i][p][:], rc[i][p][:], rs[i][p][:], ALU.add).then_inc(AT[a], 1)
                    pool_divide(pool, st, AT, 2, 1)

                with pool.Fori(0, net["depth"]) as layer:
                    m = layer + net["ln0"]

                    def after(n):
                        if n == 0:
                            for k in range(3):
                                b = slice(k * BLK, (k + 1) * BLK)
                                pool.wait_ge(LN["cen"], m * 4 + (k + 1))
                                nc.gpsimd.tensor_tensor(dev[:, b], cen[:, b], cen[:, b], ALU.mult).then_inc(FF["sq"], 1)

                    run_steps(pool, units, layer * units + net["base0"], 4, step, after)

            transformer(NETS[0])
            pool.wait_ge(YP["qke"], 16)
            with pool.Fori(0, NB // 2) as it:
                for a in range(2):
                    q = y_qk[:, 2 * a, :].rearrange("p (i n) -> p i n", i=NB // 2)[:, it, :].rearrange("p (j n) -> p j n", j=2)
                    cp = nc.gpsimd.tensor_copy(yq_s[:, :, a, :], q)
                cp.then_inc(YP["qs"], 1)
                pool.wait_ge(YP["s"], it + 1)
            transformer(NETS[1])

        @block.vector
        def _(dve):
            for k in range(NBLK):
                dve.wait_ge(in_ps, k + 1)
                nc.vector.tensor_copy(base_x[:, k * BLK:(k + 1) * BLK], bank[k][:]).then_inc(in_dve, 1)
            dve.wait_ge(in_dve, NBLK)
            dve.wait_ge(in_ps, 2 * NBLK)
            ln_dve(dve, 0, base_x, z, False)
            dve.wait_ge(ld_xw, 9 * 16)
            nc.vector.tensor_scalar(xbq[:], xb[:, 0:1], float(1 / np.sqrt(XD)), None, ALU.mult).then_inc(XP["bq"], 1)
            dve.wait_ge(ld_c, 96)
            for k in range(NBLK):
                dve.wait_ge(XP["k"], k + 1)
                nc.vector.tensor_scalar(x_k[:, k * BLK:(k + 1) * BLK], bank[4 + k][:], xb[:, 1:2], None, ALU.add
                                        ).then_inc(XP["ke"], 1)

            dve.wait_ge(XP["ke"], NBLK)

            def x0_step(st):
                dve_rinv(dve, st, X0, 1, 0)
                for g in range(2):
                    dve_max(dve, st, X0, 1, g)
                if st.has(0):
                    b, p = st.half(0)
                    st.wait(dve, X0["s1"], 2)
                    nc.vector.tensor_tensor(
                        xk_s[p], x_k.rearrange("p (b t) -> p b t", b=NB)[:, b, :].unsqueeze(1).to_broadcast([P, HU, P]),
                        head_m[:, HU * p:HU * p + HU].unsqueeze(2).to_broadcast([P, HU, P]), ALU.mult
                    ).then_inc(X0["kp"], 1)
                dve_rinv(dve, st, X0, 1, 1)
                dve_residual(dve, st, X0, 1, 3)

            run_steps(dve, 32, 0, 3, x0_step)

            def newton(st, i):
                if not st.has(0):
                    return
                if i > 0:
                    st.wait(dve, NT[i - 1], 0)
                if i == 0:
                    st.wait(dve, AT["ssq"], 0)
                    st.wait(dve, AT["ssk"], 0)
                    ins = nc.vector.tensor_scalar(ssc[:], ss[:], 1e-24, None, ALU.max)
                elif i == 1:
                    ins = nc.vector.tensor_scalar(nt_y[0][:].bitcast(I32), ssc[:].bitcast(I32), -0.5, MAGIC, ALU.mult, ALU.add)
                else:
                    n, part = divmod(i - 2, 3)
                    y = nt_y[n]
                    dst = nt_y[n + 1] if n < 2 else rnorm[st.parity]
                    if part == 0:
                        ins = nc.vector.scalar_tensor_tensor(out=nt_a[:], in0=y[:], scalar=-0.5, in1=y[:],
                                                             op0=ALU.mult, op1=ALU.mult)
                    elif part == 1:
                        ins = nc.vector.tensor_tensor(nt_b[:], nt_a[:], ssc[:], ALU.mult)
                    else:
                        if n == 2:
                            st.wait(dve, AT["mk"], 2)
                        ins = nc.vector.scalar_tensor_tensor(out=dst[:], in0=nt_b[:], scalar=1.5, in1=y[:],
                                                             op0=ALU.add, op1=ALU.mult)
                ins.then_inc(NT[i], 1)

            def rotate(st, i):
                if not st.has(0):
                    return
                p = st.parity
                st.wait(dve, AT["q" if i == 0 else "k"], 0)
                st.wait(dve, AT["qt" if i == 0 else "kt"], 2)
                src = bank[i][:].rearrange("p (h d) -> p h d", h=HU)
                nc.vector.tensor_tensor(rc[i][p][:], src, rot[:, 2 * i, :].unsqueeze(1).to_broadcast([P, HU, DH]), ALU.mult)
                hd = DH // 2
                for a in range(2):
                    dst = rs[i][p][:, :, a * hd:(a + 1) * hd]
                    ins = nc.vector.tensor_tensor(dst, src[:, :, (1 - a) * hd:(2 - a) * hd],
                                                  rot[:, 2 * i + 1, a * hd:(a + 1) * hd].unsqueeze(1).to_broadcast([P, HU, hd]),
                                                  ALU.mult)
                ins.then_inc(AT["rq" if i == 0 else "rk"], 1)

            def sum_squares(st, i):
                if st.has(0):
                    st.wait(dve, AT["sqq" if i == 0 else "sqk"], 0)
                    nc.vector.tensor_reduce(ss[:, HU * i:HU * i + HU], sq[i][:], AX.X, ALU.add
                                            ).then_inc(AT["ssq" if i == 0 else "ssk"], 1)

            def transformer(net):
                ni, units = net["idx"], net["units"]

                zb = z[:].rearrange("p (b t) -> p b t", b=NB)

                def shift(st, lag, dst, sem_, free, free_lag):
                    if not st.has(lag):
                        return
                    b = batch_of(ni, st, lag)
                    p = (st.c - lag) % 2
                    st.wait(dve, free, free_lag)
                    nc.vector.tensor_scalar(dst[p][0:DH, :], zb[0:DH, b, :], 1.0, None, ALU.mult)
                    nc.vector.tensor_scalar(dst[p][DH:P, 1:P], zb[DH:P, b, 0:P - 1], 1.0, None, ALU.mult
                                            ).then_inc(sem_, 1)

                def step(st):
                    rotate(st, 0)
                    dve_rinv(dve, st, AT, 2, 0)
                    rotate(st, 1)
                    sum_squares(st, 0)
                    sum_squares(st, 1)
                    newton(st, 0)
                    newton(st, 1)
                    dve_max(dve, st, AT, 2, 0)
                    newton(st, 2)
                    dve_rinv(dve, st, AT, 2, 1)
                    newton(st, 3)
                    shift(st, -1, hs, AT["hs"], AT["k"], 1)
                    newton(st, 4)
                    dve_max(dve, st, AT, 2, 1)
                    newton(st, 5)
                    newton(st, 6)
                    newton(st, 7)
                    shift(st, 2, hv, AT["hv"], AT["v"], 4)
                    newton(st, 8)
                    newton(st, 9)
                    newton(st, 10)
                    dve_residual(dve, st, AT, 2, 4, ni)

                m0 = net["ln0"] - 1
                ln_dve(dve, m0, base_x, z, False)
                dve.wait_ge(LN["xn"], net["ln0"] * 4)
                with dve.Fori(0, net["depth"]) as layer:
                    f = layer + net["ff0"]
                    base = layer * units + net["base0"]
                    shift(Step(units, base, 0), 0, hs, AT["hs"], AT["k"], 2)
                    dve.wait_ge(ld_rot, (f + 1) * 32)
                    for i in range(2):
                        nc.vector.tensor_tensor(rot[:, 2 * i, :], rot_c[ni][:, 2 * i, :], qks[:, i, :], ALU.mult)
                        hd = DH // 2
                        for a in range(2):
                            ins = nc.vector.tensor_tensor(rot[:, 2 * i + 1, a * hd:(a + 1) * hd],
                                                          rot_c[ni][:, 2 * i + 1, a * hd:(a + 1) * hd],
                                                          qks[:, i, (1 - a) * hd:(2 - a) * hd], ALU.mult)
                    ins.then_inc(AT["rot"], 1)
                    dve.wait_ge(AT["rot"], f + 1)
                    m = layer + net["ln0"]

                    def shift_low(k):
                        nc.vector.tensor_copy(shifted[0:DH, 4 * k:4 * k + 4, :],
                                              z[:].rearrange("p (b t) -> p b t", b=NB)[0:DH, 4 * k:4 * k + 4, :]
                                              ).then_inc(FF["lo"], 1)

                    def after(n):
                        if n == -1:
                            dve.wait_ge(AT["res"], base + 3 * units // 4)
                            for k in range(3):
                                shift_low(k)
                        if n == 0:
                            for k in range(3):
                                dve.wait_ge(FF["lo"], f * 4 + (k + 1))
                                dve_centre(dve, m, k, k % 2, shifted_f)
                        if n == 1:
                            for i in range(RSQ):
                                rsqrt(dve, i, m, LN["var"], ln_rsqrt, 1, 0, 12)
                        if n == 2:
                            dve.wait_ge(ld_ff, (f + 1) * 192)
                            for k in range(3):
                                dve_normalise(dve, m, k, k % 2, cen, True)

                    run_steps(dve, units, base, 4, step, after)
                    dve.wait_ge(AT["res"], base + units)
                    shift_low(3)
                    dve.wait_ge(FF["lo"], f * 4 + 4)
                    dve_centre(dve, m, 3, 7, shifted_f)

                    def close(k):
                        b = slice(k * BLK, (k + 1) * BLK)
                        dve.wait_ge(FF["y"], f * 4 + (k + 1))
                        nc.vector.scalar_tensor_tensor(out=z[:, b], in0=bank[4 + k][:], scalar=lnp[:, 2:3], in1=z[:, b],
                                                       op0=ALU.add, op1=ALU.add).then_inc(FF["z"], 1)

                    for i in range(3 * NBLK):
                        w = CH[i % 3][1]
                        dve.wait_ge(FF["gelu"], f * 12 + (i + 1))
                        nc.vector.scalar_tensor_tensor(out=hid[i % 3][0:w, :], in0=bank[i % 2][0:w, :],
                                                       scalar=b1[0:w, i % 3:i % 3 + 1], in1=gl[i % 2][0:w, :],
                                                       op0=ALU.add, op1=ALU.mult).then_inc(FF["hid"], 1)
                        if 2 <= i <= 5:
                            for j in range(3 * i - 6, min(3 * i - 3, RSQ)):
                                rsqrt(dve, j, f, LN["varl"], lnl_rsqrt, 7, 12, 16)
                        if i == 6:
                            dve_normalise(dve, m, 3, 7, cen, True)
                        if i % 3 == 1 and i > 3:
                            close(i // 3 - 1)
                    close(NBLK - 1)
                    dve.wait_ge(FF["z"], f * 4 + 4)
                for k in range(NBLK):
                    b = slice(k * BLK, (k + 1) * BLK)
                    nc.vector.tensor_tensor(base_x[:, b], base_x[:, b], z[:, b], ALU.add).then_inc(FF["outer"], 1)

            dve.wait_ge(X0["res"], 32)
            transformer(NETS[0])
            dve.wait_ge(FF["outer"], NBLK)
            ln_dve(dve, 8, base_x, z, False)
            with dve.Fori(0, NB // 2) as it:
                cnt = it + 1
                dve.wait_ge(YP["s"], cnt)
                nc.vector.tensor_reduce(nmx[:, 0:4], bank4[3], AX.X, ALU.max).then_inc(YP["mx"], 1)
                dve.wait_ge(YP["mx"], cnt)
                nc.vector.tensor_tensor(prob[0][0], bank4[3], nmx[:, 0:4].unsqueeze(2).to_broadcast([P, 4, P]),
                                        ALU.subtract).then_inc(YP["sh"], 1)
                dve.wait_ge(YP["ex"], cnt)
                nc.vector.tensor_reduce(rsum[:, 0:4], prob[0][0], AX.X, ALU.add).then_inc(YP["rs"], 1)
                dve.wait_ge(YP["rs"], cnt)
                nc.vector.reciprocal(rinv[:, 0:4], rsum[:, 0:4]).then_inc(YP["rr"], 1)
                dve.wait_ge(YP["rr"], cnt)
                dve.wait_ge(YP["o"], cnt)
                nc.vector.tensor_tensor(o_tok[:].rearrange("p (i n) -> p i n", i=4), bank4[5],
                                        rinv[:, 0:4].unsqueeze(2).to_broadcast([P, 4, P]), ALU.mult).then_inc(YP["on"], 1)
            dve.wait_ge(YP["ote"], 16)
            for k in range(NBLK):
                b = slice(k * BLK, (k + 1) * BLK)
                nc.vector.tensor_tensor(cen[:, b], y_ctx[:, 0, b], y_ctx[:, 1, b], ALU.subtract).then_inc(YP["gd"], 1)
            for k in range(NBLK):
                b = slice(k * BLK, (k + 1) * BLK)
                dve.wait_ge(YP["gd"], k + 1)
                nc.vector.tensor_tensor(base_x[:, b], base_x[:, b], y_ctx[:, 1, b], ALU.add).then_inc(YP["gm"], 1)
            for k in range(NBLK):
                b = slice(k * BLK, (k + 1) * BLK)
                dve.wait_ge(YP["sg"], k + 1)
                nc.vector.tensor_tensor(cen[:, b], cen[:, b], dev[:, b], ALU.mult).then_inc(YP["gm"], 1)
            for k in range(NBLK):
                b = slice(k * BLK, (k + 1) * BLK)
                dve.wait_ge(YP["gm"], NBLK + k + 1)
                nc.vector.tensor_tensor(base_x[:, b], base_x[:, b], cen[:, b], ALU.add).then_inc(YP["gm"], 1)
            dve.wait_ge(YP["gm"], 3 * NBLK)
            transformer(NETS[1])
            for k in range(NBLK):
                dve.wait_ge(out_ps, k + 1)
                nc.vector.tensor_copy(cen[:, k * BLK:(k + 1) * BLK], bank[k][:]).then_inc(out_dve, 1)


_INS = ["x", "ctx_1024"] + ["L0_xattn_" + n for n in "Wq bq Wk bk Wv bv Wo bo".split()] \
    + ["L0_ffn_" + n for n in "Wqkv q_scale k_scale Wo ln_g ln_b W1 b1 W2 b2".split()] \
    + ["L1_xattn_" + n for n in "Wq_c bq_c Wk_s bk_s Wv_s bv_s Wq_s bq_s Wk_c bk_c Wv_c bv_c Wg bg".split()] \
    + ["L1_ffn_" + n for n in "wqkv q_scale k_scale wo ln_g ln_b w1 b1 w2 b2".split()]


def kernel(**inputs):
    import concourse.bacc as _bacc
    from concourse.bass_utils import run_bass_kernel_spmd as _run

    nc = _bacc.Bacc("TRN2", target_bir_lowering=False, num_devices=1)
    arrays, aps = {}, {}
    for name in _INS:
        a = np.ascontiguousarray(inputs[name])
        arrays[f"in_{name}_dram"] = a
        aps[name] = nc.dram_tensor(f"in_{name}_dram", a.shape, mybir.dt.from_np(a.dtype), kind="ExternalInput").ap()
    out = nc.dram_tensor("out_0_dram", (NB, P, P), F32, kind="ExternalOutput").ap()
    build(nc, aps, out)
    r = _run(nc, [arrays], core_ids=[0])
    return r.results[0]["out_0_dram"]
```
